# Optimizing a Trainium2 kernel written in Bass

```python
import numpy as np
import jax
import jax.numpy as jnp

def _softmax(x, axis=-1):
    return jax.nn.softmax(x, axis=axis)

def _gelu(x):
    return jax.nn.gelu(x, approximate=True)

def _silu(x):
    return jax.nn.silu(x)

def _sigmoid(x):
    return jax.nn.sigmoid(x)

def _layernorm(x, axis=-1, eps=1e-05):
    m = jnp.mean(x, axis=axis, keepdims=True)
    v = jnp.var(x, axis=axis, keepdims=True)
    return (x - m) / jnp.sqrt(v + eps)

def _scatter_add(tgt, idx, src, axis=0):
    return tgt.at[idx].add(src)

def _segment_sum(src, seg, n):
    return jax.ops.segment_sum(src, seg, n)
kernel_name = 'mk_seq_preln_d4_jaxref_r8_86aeb6'

def setup_inputs(seed: int=0):
    np.random.seed(seed)
    _w = jnp.asarray

    def _L0_attn_setup():
        import jax, jax.numpy as jnp
        import numpy as np
        import math
        DIM = 128
        NUM_HEADS = 16
        HEAD_DIM = DIM // NUM_HEADS
        B, S = (2, 256)
        key = jax.random.key(seed)
        ks = jax.random.split(key, 9)
        sc = 0.02
        return {'x': jax.random.normal(ks[0], (B, S, DIM), jnp.float32), 'Wq': jax.random.normal(ks[1], (DIM, DIM), jnp.float32) * sc, 'bq': jax.random.normal(ks[2], (DIM,), jnp.float32) * sc, 'Wk': jax.random.normal(ks[3], (DIM, DIM), jnp.float32) * sc, 'bk': jax.random.normal(ks[4], (DIM,), jnp.float32) * sc, 'Wv': jax.random.normal(ks[5], (DIM, DIM), jnp.float32) * sc, 'bv': jax.random.normal(ks[6], (DIM,), jnp.float32) * sc, 'Wo': jax.random.normal(ks[7], (DIM, DIM), jnp.float32) * sc, 'bo': jax.random.normal(ks[8], (DIM,), jnp.float32) * sc}
    _L0_attn_in = _L0_attn_setup()

    def _L0_ffn_setup():
        import jax, jax.numpy as jnp
        import numpy as np
        B, S, D = (2, 256, 128)
        E, F, K = (8, 256, 2)
        key = jax.random.key(seed)
        k0, k1, k2, k3, k4 = jax.random.split(key, 5)
        scale = 0.02
        x = jax.random.normal(k0, (B, S, D), dtype=jnp.float32)
        w1 = jax.random.normal(k1, (E * F, D), dtype=jnp.float32) * scale
        v1 = jax.random.normal(k2, (E * F, D), dtype=jnp.float32) * scale
        w2 = jax.random.normal(k3, (E * F, D), dtype=jnp.float32) * scale
        router_w = jax.random.normal(k4, (E, D), dtype=jnp.float32) * scale
        return {'x': x, 'w1': w1, 'v1': v1, 'w2': w2, 'router_w': router_w}
    _L0_ffn_in = _L0_ffn_setup()

    def _L1_attn_setup():
        import jax, jax.numpy as jnp
        import numpy as np
        B, N, C = (4, 512, 128)
        H = 16
        D = C // H
        EPS = 1e-06

        def _feature_map(x):
            return jax.nn.elu(x) + 1.0
        key = jax.random.key(seed)
        k1, k2, k3, k4 = jax.random.split(key, 4)
        x = jax.random.normal(k1, (B, N, C), dtype=jnp.float32)
        Wqkv = jax.random.normal(k2, (3 * C, C), dtype=jnp.float32) * 0.02
        Wproj = jax.random.normal(k3, (C, C), dtype=jnp.float32) * 0.02
        bproj = jax.random.normal(k4, (C,), dtype=jnp.float32) * 0.02
        return {'x': x, 'Wqkv': Wqkv, 'Wproj': Wproj, 'bproj': bproj}
    _L1_attn_in = _L1_attn_setup()

    def _L1_ffn_setup():
        import jax, jax.numpy as jnp
        import numpy as np
        DIM = 128
        DEPTH = 6
        HEADS = 16
        DIM_HEAD = 64
        WINDOW = 32
        INNER = HEADS * DIM_HEAD
        DIM_INNER = int(DIM * 4 * 2 / 3)
        QK_SCALE = 8.0

        def shift_tokens(t):
            a, s = jnp.split(t, 2, -1)
            s = jnp.pad(s, ((0, 0), (1, 0), (0, 0)))[:, :-1]
            return jnp.concatenate([a, s], -1)

        def l2norm(t):
            return t / jnp.maximum(jnp.linalg.norm(t, axis=-1, keepdims=True), 1e-12)

        def rotate_half(x):
            x1, x2 = jnp.split(x, 2, -1)
            return jnp.concatenate([-x2, x1], -1)

        def rotary_tables(n):
            half = jnp.arange(0, DIM_HEAD, 2, dtype=jnp.float32)
            inv_freq = 1.0 / 10000.0 ** (half / DIM_HEAD)
            t = jnp.arange(n, dtype=jnp.float32)
            freqs = t[:, None] * inv_freq[None, :]
            freqs = jnp.concatenate([freqs, freqs], -1)
            base_scale = (half + 0.4 * DIM_HEAD) / (1.4 * DIM_HEAD)
            power = (t - n // 2) / (WINDOW // 2)
            scale = base_scale[None, :] ** power[:, None]
            scale = jnp.concatenate([scale, scale], -1)
            return (freqs, scale)

        def local_attention(q, k, v):
            b, h, n, d = q.shape
            w = WINDOW
            nw = n // w
            bq = q.reshape(b, h, nw, w, d)
            bk = k.reshape(b, h, nw, w, d)
            bv = v.reshape(b, h, nw, w, d)

            def look(t):
                p = jnp.pad(t, ((0, 0), (0, 0), (1, 0), (0, 0), (0, 0)))
                return jnp.concatenate([p[:, :, :nw], p[:, :, 1:]], axis=3)
            bk2, bv2 = (look(bk), look(bv))
            seq = jnp.arange(n).reshape(nw, w)
            seq_p = jnp.pad(seq, ((1, 0), (0, 0)), constant_values=-1)
            jt = jnp.concatenate([seq_p[:nw], seq_p[1:]], axis=1)
            it = seq[:, :, None]
            jb = jt[:, None, :]
            mask = (it < jb) | (it > jb + w) | (jb == -1)
            sim = jnp.einsum('bhwie,bhwje->bhwij', bq, bk2) * QK_SCALE
            sim = jnp.where(mask, -jnp.finfo(sim.dtype).max, sim)
            attn = jax.nn.softmax(sim, -1)
            out = jnp.einsum('bhwij,bhwje->bhwie', attn, bv2)
            return out.reshape(b, h, n, d)

        def attn_layer(x, Wqkv, qs, ksc, Wo):
            b, n, _ = x.shape
            qkv = x @ Wqkv
            q, k, v = jnp.split(qkv, 3, -1)
            sh = lambda t: t.reshape(b, n, HEADS, DIM_HEAD).transpose(0, 2, 1, 3)
            q, k, v = (sh(q), sh(k), sh(v))
            q = l2norm(q) * qs
            k = l2norm(k) * ksc
            freqs, scale = rotary_tables(n)
            cos, sin = (jnp.cos(freqs), jnp.sin(freqs))
            q = q * cos * scale + rotate_half(q) * sin * scale
            inv = 1.0 / scale
            k = k * cos * inv + rotate_half(k) * sin * inv
            out = local_attention(q, k, v)
            out = out.transpose(0, 2, 1, 3).reshape(b, n, INNER)
            return out @ Wo

        def ffn_layer(x, g, bln, W1, b1, W2, b2):
            mu = x.mean(-1, keepdims=True)
            var = ((x - mu) ** 2).mean(-1, keepdims=True)
            xn = (x - mu) / jnp.sqrt(var + 1e-05) * g + bln
            hg = xn @ W1 + b1
            a, gate = jnp.split(hg, 2, -1)
            return a * jax.nn.gelu(gate, approximate=False) @ W2 + b2
        key = jax.random.key(seed)
        ks = jax.random.split(key, 8)
        B, N = (2, 256)
        init = lambda k, shape: jax.random.normal(k, shape, jnp.float32) * 0.02
        return {'x': jax.random.normal(ks[0], (B, N, DIM), jnp.float32), 'Wqkv': init(ks[1], (DEPTH, DIM, 3 * INNER)), 'q_scale': jnp.ones((DEPTH, DIM_HEAD), jnp.float32), 'k_scale': jnp.ones((DEPTH, DIM_HEAD), jnp.float32), 'Wo': init(ks[2], (DEPTH, INNER, DIM)), 'ln_g': jnp.ones((DEPTH, DIM), jnp.float32), 'ln_b': jnp.zeros((DEPTH, DIM), jnp.float32), 'W1': init(ks[3], (DEPTH, DIM, 2 * DIM_INNER)), 'b1': jnp.zeros((DEPTH, 2 * DIM_INNER), jnp.float32), 'W2': init(ks[4], (DEPTH, DIM_INNER, DIM)), 'b2': jnp.zeros((DEPTH, DIM), jnp.float32)}
    _L1_ffn_in = _L1_ffn_setup()

    def _L2_attn_setup():
        import jax, jax.numpy as jnp
        import numpy as np
        B, M, D = (4, 256, 128)

        def _rope_tables(m, d):
            i = jnp.arange(d // 2, dtype=jnp.float32)
            phi = jnp.power(10000.0, -2.0 * (i - 1.0) / d)
            pos = jnp.arange(m, dtype=jnp.float32)
            ang = pos[:, None] * phi[None, :]
            return (jnp.cos(ang), jnp.sin(ang))

        def _apply_rope(t, cos, sin):
            te = t[..., 0::2]
            to = t[..., 1::2]
            oe = te * cos + to * sin
            oo = -te * sin + to * cos
            return jnp.stack([oe, oo], axis=-1).reshape(t.shape)
        key = jax.random.key(seed)
        k1, k2, k3, k4 = jax.random.split(key, 4)
        x = jax.random.normal(k1, (B, M, D), dtype=jnp.float32)
        scale = 0.02
        wq = jax.random.normal(k2, (D, D), dtype=jnp.float32) * scale
        wk = jax.random.normal(k3, (D, D), dtype=jnp.float32) * scale
        wv = jax.random.normal(k4, (D, D), dtype=jnp.float32) * scale
        return {'x': x, 'wq': wq, 'wk': wk, 'wv': wv}
    _L2_attn_in = _L2_attn_setup()

    def _L2_ffn_setup():
        import jax, jax.numpy as jnp
        import numpy as np
        DIM = 128
        DEPTH = 6
        HEADS = 16
        DIM_HEAD = 64
        WINDOW = 32
        INNER = HEADS * DIM_HEAD
        DIM_INNER = int(DIM * 4 * 2 / 3)
        QK_SCALE = 8.0

        def shift_tokens(t):
            a, s = jnp.split(t, 2, -1)
            s = jnp.pad(s, ((0, 0), (1, 0), (0, 0)))[:, :-1]
            return jnp.concatenate([a, s], -1)

        def l2norm(t):
            return t / jnp.maximum(jnp.linalg.norm(t, axis=-1, keepdims=True), 1e-12)

        def rotate_half(x):
            x1, x2 = jnp.split(x, 2, -1)
            return jnp.concatenate([-x2, x1], -1)

        def rotary_tables(n):
            half = jnp.arange(0, DIM_HEAD, 2, dtype=jnp.float32)
            inv_freq = 1.0 / 10000.0 ** (half / DIM_HEAD)
            t = jnp.arange(n, dtype=jnp.float32)
            freqs = t[:, None] * inv_freq[None, :]
            freqs = jnp.concatenate([freqs, freqs], -1)
            base_scale = (half + 0.4 * DIM_HEAD) / (1.4 * DIM_HEAD)
            power = (t - n // 2) / (WINDOW // 2)
            scale = base_scale[None, :] ** power[:, None]
            scale = jnp.concatenate([scale, scale], -1)
            return (freqs, scale)

        def local_attention(q, k, v):
            b, h, n, d = q.shape
            w = WINDOW
            nw = n // w
            bq = q.reshape(b, h, nw, w, d)
            bk = k.reshape(b, h, nw, w, d)
            bv = v.reshape(b, h, nw, w, d)

            def look(t):
                p = jnp.pad(t, ((0, 0), (0, 0), (1, 0), (0, 0), (0, 0)))
                return jnp.concatenate([p[:, :, :nw], p[:, :, 1:]], axis=3)
            bk2, bv2 = (look(bk), look(bv))
            seq = jnp.arange(n).reshape(nw, w)
            seq_p = jnp.pad(seq, ((1, 0), (0, 0)), constant_values=-1)
            jt = jnp.concatenate([seq_p[:nw], seq_p[1:]], axis=1)
            it = seq[:, :, None]
            jb = jt[:, None, :]
            mask = (it < jb) | (it > jb + w) | (jb == -1)
            sim = jnp.einsum('bhwie,bhwje->bhwij', bq, bk2) * QK_SCALE
            sim = jnp.where(mask, -jnp.finfo(sim.dtype).max, sim)
            attn = jax.nn.softmax(sim, -1)
            out = jnp.einsum('bhwij,bhwje->bhwie', attn, bv2)
            return out.reshape(b, h, n, d)

        def attn_layer(x, Wqkv, qs, ksc, Wo):
            b, n, _ = x.shape
            qkv = x @ Wqkv
            q, k, v = jnp.split(qkv, 3, -1)
            sh = lambda t: t.reshape(b, n, HEADS, DIM_HEAD).transpose(0, 2, 1, 3)
            q, k, v = (sh(q), sh(k), sh(v))
            q = l2norm(q) * qs
            k = l2norm(k) * ksc
            freqs, scale = rotary_tables(n)
            cos, sin = (jnp.cos(freqs), jnp.sin(freqs))
            q = q * cos * scale + rotate_half(q) * sin * scale
            inv = 1.0 / scale
            k = k * cos * inv + rotate_half(k) * sin * inv
            out = local_attention(q, k, v)
            out = out.transpose(0, 2, 1, 3).reshape(b, n, INNER)
            return out @ Wo

        def ffn_layer(x, g, bln, W1, b1, W2, b2):
            mu = x.mean(-1, keepdims=True)
            var = ((x - mu) ** 2).mean(-1, keepdims=True)
            xn = (x - mu) / jnp.sqrt(var + 1e-05) * g + bln
            hg = xn @ W1 + b1
            a, gate = jnp.split(hg, 2, -1)
            return a * jax.nn.gelu(gate, approximate=False) @ W2 + b2
        key = jax.random.key(seed)
        ks = jax.random.split(key, 8)
        B, N = (2, 256)
        init = lambda k, shape: jax.random.normal(k, shape, jnp.float32) * 0.02
        return {'x': jax.random.normal(ks[0], (B, N, DIM), jnp.float32), 'Wqkv': init(ks[1], (DEPTH, DIM, 3 * INNER)), 'q_scale': jnp.ones((DEPTH, DIM_HEAD), jnp.float32), 'k_scale': jnp.ones((DEPTH, DIM_HEAD), jnp.float32), 'Wo': init(ks[2], (DEPTH, INNER, DIM)), 'ln_g': jnp.ones((DEPTH, DIM), jnp.float32), 'ln_b': jnp.zeros((DEPTH, DIM), jnp.float32), 'W1': init(ks[3], (DEPTH, DIM, 2 * DIM_INNER)), 'b1': jnp.zeros((DEPTH, 2 * DIM_INNER), jnp.float32), 'W2': init(ks[4], (DEPTH, DIM_INNER, DIM)), 'b2': jnp.zeros((DEPTH, DIM), jnp.float32)}
    _L2_ffn_in = _L2_ffn_setup()

    def _L3_attn_setup():
        import jax, jax.numpy as jnp
        import numpy as np
        B, T, D = (2, 256, 128)
        H = 16
        HD = D // H
        DL = 64
        NR = 64
        EPS = 1.1920929e-07

        def _rms_norm(x, w):
            ms = jnp.mean(jnp.square(x), axis=-1, keepdims=True)
            return x * jax.lax.rsqrt(ms + EPS) * w
        key = jax.random.key(seed)
        ks = jax.random.split(key, 10)
        s = 0.02
        return {'x': jax.random.normal(ks[0], (B, T, D), dtype=jnp.float32), 'W_DQ': jax.random.normal(ks[1], (DL, HD), dtype=jnp.float32) * s, 'W_UQ': jax.random.normal(ks[2], (HD, DL), dtype=jnp.float32) * s, 'W_DKV': jax.random.normal(ks[3], (2 * DL, HD), dtype=jnp.float32) * s, 'W_UKV': jax.random.normal(ks[4], (2 * HD, 2 * DL), dtype=jnp.float32) * s, 'W_QR': jax.random.normal(ks[5], (NR, HD), dtype=jnp.float32) * s, 'W_KR': jax.random.normal(ks[6], (NR, HD), dtype=jnp.float32) * s, 'W_O': jax.random.normal(ks[7], (HD, HD), dtype=jnp.float32) * s, 'q_norm_w': jnp.ones((HD,), dtype=jnp.float32), 'k_norm_w': jnp.ones((HD,), dtype=jnp.float32)}
    _L3_attn_in = _L3_attn_setup()

    def _L3_ffn_setup():
        import jax, jax.numpy as jnp
        import numpy as np
        B, S, H, NH, E, F = (4, 128, 128, 16, 8, 512)
        D = H // NH
        EPS = 1e-05

        def _layernorm(x, g, b):
            mu = jnp.mean(x, axis=-1, keepdims=True)
            var = jnp.var(x, axis=-1, keepdims=True)
            return (x - mu) * jax.lax.rsqrt(var + EPS) * g + b
        key = jax.random.key(seed)
        ks = jax.random.split(key, 16)
        s = 0.02
        return {'x': jax.random.normal(ks[0], (B, S, H), jnp.float32), 'ln1_g': jnp.ones((H,), jnp.float32), 'ln1_b': jnp.zeros((H,), jnp.float32), 'ln2_g': jnp.ones((H,), jnp.float32), 'ln2_b': jnp.zeros((H,), jnp.float32), 'wq': jax.random.normal(ks[1], (H, H), jnp.float32) * s, 'bq': jnp.zeros((H,), jnp.float32), 'wk': jax.random.normal(ks[2], (H, H), jnp.float32) * s, 'bk': jnp.zeros((H,), jnp.float32), 'wv': jax.random.normal(ks[3], (H, H), jnp.float32) * s, 'bv': jnp.zeros((H,), jnp.float32), 'wo': jax.random.normal(ks[4], (H, H), jnp.float32) * s, 'bo': jnp.zeros((H,), jnp.float32), 'gate_w': jax.random.normal(ks[5], (H, E), jnp.float32) * s, 'gate_b': jnp.zeros((E,), jnp.float32), 'w1': jax.random.normal(ks[6], (E, H, F), jnp.float32) * s, 'b1': jnp.zeros((E, F), jnp.float32), 'w2': jax.random.normal(ks[7], (E, F, H), jnp.float32) * s, 'b2': jnp.zeros((E, H), jnp.float32)}
    _L3_ffn_in = _L3_ffn_setup()
    _d = {'L0_attn_x': _L0_attn_in['x'], 'L0_attn_Wq': _L0_attn_in['Wq'], 'L0_attn_bq': _L0_attn_in['bq'], 'L0_attn_Wk': _L0_attn_in['Wk'], 'L0_attn_bk': _L0_attn_in['bk'], 'L0_attn_Wv': _L0_attn_in['Wv'], 'L0_attn_bv': _L0_attn_in['bv'], 'L0_attn_Wo': _L0_attn_in['Wo'], 'L0_attn_bo': _L0_attn_in['bo'], 'L0_ffn_w1': _L0_ffn_in['w1'], 'L0_ffn_v1': _L0_ffn_in['v1'], 'L0_ffn_w2': _L0_ffn_in['w2'], 'L0_ffn_router_w': _L0_ffn_in['router_w'], 'L1_attn_Wqkv': _L1_attn_in['Wqkv'], 'L1_attn_Wproj': _L1_attn_in['Wproj'], 'L1_attn_bproj': _L1_attn_in['bproj'], 'L1_ffn_Wqkv': _L1_ffn_in['Wqkv'], 'L1_ffn_q_scale': _L1_ffn_in['q_scale'], 'L1_ffn_k_scale': _L1_ffn_in['k_scale'], 'L1_ffn_Wo': _L1_ffn_in['Wo'], 'L1_ffn_ln_g': _L1_ffn_in['ln_g'], 'L1_ffn_ln_b': _L1_ffn_in['ln_b'], 'L1_ffn_W1': _L1_ffn_in['W1'], 'L1_ffn_b1': _L1_ffn_in['b1'], 'L1_ffn_W2': _L1_ffn_in['W2'], 'L1_ffn_b2': _L1_ffn_in['b2'], 'L2_attn_wq': _L2_attn_in['wq'], 'L2_attn_wk': _L2_attn_in['wk'], 'L2_attn_wv': _L2_attn_in['wv'], 'L2_ffn_Wqkv': _L2_ffn_in['Wqkv'], 'L2_ffn_q_scale': _L2_ffn_in['q_scale'], 'L2_ffn_k_scale': _L2_ffn_in['k_scale'], 'L2_ffn_Wo': _L2_ffn_in['Wo'], 'L2_ffn_ln_g': _L2_ffn_in['ln_g'], 'L2_ffn_ln_b': _L2_ffn_in['ln_b'], 'L2_ffn_W1': _L2_ffn_in['W1'], 'L2_ffn_b1': _L2_ffn_in['b1'], 'L2_ffn_W2': _L2_ffn_in['W2'], 'L2_ffn_b2': _L2_ffn_in['b2'], 'L3_attn_W_DQ': _L3_attn_in['W_DQ'], 'L3_attn_W_UQ': _L3_attn_in['W_UQ'], 'L3_attn_W_DKV': _L3_attn_in['W_DKV'], 'L3_attn_W_UKV': _L3_attn_in['W_UKV'], 'L3_attn_W_QR': _L3_attn_in['W_QR'], 'L3_attn_W_KR': _L3_attn_in['W_KR'], 'L3_attn_W_O': _L3_attn_in['W_O'], 'L3_attn_q_norm_w': _L3_attn_in['q_norm_w'], 'L3_attn_k_norm_w': _L3_attn_in['k_norm_w'], 'L3_ffn_ln1_g': _L3_ffn_in['ln1_g'], 'L3_ffn_ln1_b': _L3_ffn_in['ln1_b'], 'L3_ffn_ln2_g': _L3_ffn_in['ln2_g'], 'L3_ffn_ln2_b': _L3_ffn_in['ln2_b'], 'L3_ffn_wq': _L3_ffn_in['wq'], 'L3_ffn_bq': _L3_ffn_in['bq'], 'L3_ffn_wk': _L3_ffn_in['wk'], 'L3_ffn_bk': _L3_ffn_in['bk'], 'L3_ffn_wv': _L3_ffn_in['wv'], 'L3_ffn_bv': _L3_ffn_in['bv'], 'L3_ffn_wo': _L3_ffn_in['wo'], 'L3_ffn_bo': _L3_ffn_in['bo'], 'L3_ffn_gate_w': _L3_ffn_in['gate_w'], 'L3_ffn_gate_b': _L3_ffn_in['gate_b'], 'L3_ffn_w1': _L3_ffn_in['w1'], 'L3_ffn_b1': _L3_ffn_in['b1'], 'L3_ffn_w2': _L3_ffn_in['w2'], 'L3_ffn_b2': _L3_ffn_in['b2']}
    _x0 = _d['L0_attn_x']
    _d['L0_attn_x'] = jax.random.normal(jax.random.fold_in(jax.random.key(seed), 1), (8, 256, 128), dtype=_x0.dtype)
    del _x0
    return _d

def reference(L0_attn_x, L0_attn_Wq, L0_attn_bq, L0_attn_Wk, L0_attn_bk, L0_attn_Wv, L0_attn_bv, L0_attn_Wo, L0_attn_bo, L0_ffn_w1, L0_ffn_v1, L0_ffn_w2, L0_ffn_router_w, L1_attn_Wqkv, L1_attn_Wproj, L1_attn_bproj, L1_ffn_Wqkv, L1_ffn_q_scale, L1_ffn_k_scale, L1_ffn_Wo, L1_ffn_ln_g, L1_ffn_ln_b, L1_ffn_W1, L1_ffn_b1, L1_ffn_W2, L1_ffn_b2, L2_attn_wq, L2_attn_wk, L2_attn_wv, L2_ffn_Wqkv, L2_ffn_q_scale, L2_ffn_k_scale, L2_ffn_Wo, L2_ffn_ln_g, L2_ffn_ln_b, L2_ffn_W1, L2_ffn_b1, L2_ffn_W2, L2_ffn_b2, L3_attn_W_DQ, L3_attn_W_UQ, L3_attn_W_DKV, L3_attn_W_UKV, L3_attn_W_QR, L3_attn_W_KR, L3_attn_W_O, L3_attn_q_norm_w, L3_attn_k_norm_w, L3_ffn_ln1_g, L3_ffn_ln1_b, L3_ffn_ln2_g, L3_ffn_ln2_b, L3_ffn_wq, L3_ffn_bq, L3_ffn_wk, L3_ffn_bk, L3_ffn_wv, L3_ffn_bv, L3_ffn_wo, L3_ffn_bo, L3_ffn_gate_w, L3_ffn_gate_b, L3_ffn_w1, L3_ffn_b1, L3_ffn_w2, L3_ffn_b2):

    def _L0_attn_ref(x, Wq, bq, Wk, bk, Wv, bv, Wo, bo):
        import jax, jax.numpy as jnp
        import numpy as np
        import math
        DIM = 128
        NUM_HEADS = 16
        HEAD_DIM = DIM // NUM_HEADS
        B, S = (2, 256)
        b, s, d = x.shape
        h, hd = (NUM_HEADS, HEAD_DIM)

        def split_heads(t):
            return t.reshape(b, s, h, hd).transpose(0, 2, 1, 3)
        q = split_heads(x @ Wq + bq)
        k = split_heads(x @ Wk + bk)
        v = split_heads(x @ Wv + bv)
        scores = jnp.einsum('bhqd,bhkd->bhqk', q, k) / math.sqrt(hd)
        causal = jnp.tril(jnp.ones((s, s), dtype=bool))
        scores = jnp.where(causal[None, None], scores, jnp.asarray(-10000.0, scores.dtype))
        probs = jax.nn.softmax(scores, axis=-1)
        ctx = jnp.einsum('bhqk,bhkd->bhqd', probs, v)
        ctx = ctx.transpose(0, 2, 1, 3).reshape(b, s, d)
        return ctx @ Wo + bo

    def _L0_ffn_ref(x, w1, v1, w2, router_w):
        import jax, jax.numpy as jnp
        import numpy as np
        B, S, D = (2, 256, 128)
        E, F, K = (8, 256, 2)
        logits = jnp.einsum('bsd,ed->bse', x, router_w)
        weights = jax.nn.softmax(logits.astype(jnp.float32), axis=-1)
        top_weights, top_experts = jax.lax.top_k(weights, K)
        norm = jnp.sum(jnp.abs(top_weights), axis=-1, keepdims=True)
        top_weights = (top_weights / norm).astype(x.dtype)
        w1e = w1.reshape(E, F, D)
        v1e = v1.reshape(E, F, D)
        w2e = w2.reshape(E, F, D)
        out = jnp.zeros_like(x)
        for e in range(E):
            gate = jnp.sum(jnp.where(top_experts == e, top_weights, 0.0), axis=-1)
            h1 = jax.nn.silu(jnp.einsum('bsd,fd->bsf', x, w1e[e]))
            h = h1 * jnp.einsum('bsd,fd->bsf', x, v1e[e])
            y = jnp.einsum('bsf,fd->bsd', h, w2e[e])
            out = out + gate[..., None] * y
        return out

    def _L1_attn_ref(x, Wqkv, Wproj, bproj):
        import jax, jax.numpy as jnp
        import numpy as np
        B, N, C = (4, 512, 128)
        H = 16
        D = C // H
        EPS = 1e-06

        def _feature_map(x):
            return jax.nn.elu(x) + 1.0
        b, n, c = x.shape
        qkv = jnp.einsum('bnc,fc->bnf', x, Wqkv).reshape(b, n, 3, H, D)
        qkv = jnp.transpose(qkv, (2, 0, 3, 1, 4))
        q, k, v = (qkv[0], qkv[1], qkv[2])
        q = _feature_map(q)
        k = _feature_map(k)
        kv = jnp.einsum('bhnd,bhne->bhde', k, v)
        k_sum = k.sum(axis=2)
        z = 1.0 / (jnp.einsum('bhnd,bhd->bhn', q, k_sum)[..., None] + EPS)
        out = jnp.einsum('bhnd,bhde->bhne', q, kv) * z
        out = jnp.transpose(out, (0, 2, 1, 3)).reshape(b, n, c)
        out = jnp.einsum('bnc,oc->bno', out, Wproj) + bproj
        return out

    def _L1_ffn_ref(x, Wqkv, q_scale, k_scale, Wo, ln_g, ln_b, W1, b1, W2, b2):
        import jax, jax.numpy as jnp
        import numpy as np
        DIM = 128
        DEPTH = 6
        HEADS = 16
        DIM_HEAD = 64
        WINDOW = 32
        INNER = HEADS * DIM_HEAD
        DIM_INNER = int(DIM * 4 * 2 / 3)
        QK_SCALE = 8.0

        def shift_tokens(t):
            a, s = jnp.split(t, 2, -1)
            s = jnp.pad(s, ((0, 0), (1, 0), (0, 0)))[:, :-1]
            return jnp.concatenate([a, s], -1)

        def l2norm(t):
            return t / jnp.maximum(jnp.linalg.norm(t, axis=-1, keepdims=True), 1e-12)

        def rotate_half(x):
            x1, x2 = jnp.split(x, 2, -1)
            return jnp.concatenate([-x2, x1], -1)

        def rotary_tables(n):
            half = jnp.arange(0, DIM_HEAD, 2, dtype=jnp.float32)
            inv_freq = 1.0 / 10000.0 ** (half / DIM_HEAD)
            t = jnp.arange(n, dtype=jnp.float32)
            freqs = t[:, None] * inv_freq[None, :]
            freqs = jnp.concatenate([freqs, freqs], -1)
            base_scale = (half + 0.4 * DIM_HEAD) / (1.4 * DIM_HEAD)
            power = (t - n // 2) / (WINDOW // 2)
            scale = base_scale[None, :] ** power[:, None]
            scale = jnp.concatenate([scale, scale], -1)
            return (freqs, scale)

        def local_attention(q, k, v):
            b, h, n, d = q.shape
            w = WINDOW
            nw = n // w
            bq = q.reshape(b, h, nw, w, d)
            bk = k.reshape(b, h, nw, w, d)
            bv = v.reshape(b, h, nw, w, d)

            def look(t):
                p = jnp.pad(t, ((0, 0), (0, 0), (1, 0), (0, 0), (0, 0)))
                return jnp.concatenate([p[:, :, :nw], p[:, :, 1:]], axis=3)
            bk2, bv2 = (look(bk), look(bv))
            seq = jnp.arange(n).reshape(nw, w)
            seq_p = jnp.pad(seq, ((1, 0), (0, 0)), constant_values=-1)
            jt = jnp.concatenate([seq_p[:nw], seq_p[1:]], axis=1)
            it = seq[:, :, None]
            jb = jt[:, None, :]
            mask = (it < jb) | (it > jb + w) | (jb == -1)
            sim = jnp.einsum('bhwie,bhwje->bhwij', bq, bk2) * QK_SCALE
            sim = jnp.where(mask, -jnp.finfo(sim.dtype).max, sim)
            attn = jax.nn.softmax(sim, -1)
            out = jnp.einsum('bhwij,bhwje->bhwie', attn, bv2)
            return out.reshape(b, h, n, d)

        def attn_layer(x, Wqkv, qs, ksc, Wo):
            b, n, _ = x.shape
            qkv = x @ Wqkv
            q, k, v = jnp.split(qkv, 3, -1)
            sh = lambda t: t.reshape(b, n, HEADS, DIM_HEAD).transpose(0, 2, 1, 3)
            q, k, v = (sh(q), sh(k), sh(v))
            q = l2norm(q) * qs
            k = l2norm(k) * ksc
            freqs, scale = rotary_tables(n)
            cos, sin = (jnp.cos(freqs), jnp.sin(freqs))
            q = q * cos * scale + rotate_half(q) * sin * scale
            inv = 1.0 / scale
            k = k * cos * inv + rotate_half(k) * sin * inv
            out = local_attention(q, k, v)
            out = out.transpose(0, 2, 1, 3).reshape(b, n, INNER)
            return out @ Wo

        def ffn_layer(x, g, bln, W1, b1, W2, b2):
            mu = x.mean(-1, keepdims=True)
            var = ((x - mu) ** 2).mean(-1, keepdims=True)
            xn = (x - mu) / jnp.sqrt(var + 1e-05) * g + bln
            hg = xn @ W1 + b1
            a, gate = jnp.split(hg, 2, -1)
            return a * jax.nn.gelu(gate, approximate=False) @ W2 + b2
        for i in range(DEPTH):
            x = attn_layer(shift_tokens(x), Wqkv[i], q_scale[i], k_scale[i], Wo[i]) + x
            x = ffn_layer(shift_tokens(x), ln_g[i], ln_b[i], W1[i], b1[i], W2[i], b2[i]) + x
        return x

    def _L2_attn_ref(x, wq, wk, wv):
        import jax, jax.numpy as jnp
        import numpy as np
        B, M, D = (4, 256, 128)

        def _rope_tables(m, d):
            i = jnp.arange(d // 2, dtype=jnp.float32)
            phi = jnp.power(10000.0, -2.0 * (i - 1.0) / d)
            pos = jnp.arange(m, dtype=jnp.float32)
            ang = pos[:, None] * phi[None, :]
            return (jnp.cos(ang), jnp.sin(ang))

        def _apply_rope(t, cos, sin):
            te = t[..., 0::2]
            to = t[..., 1::2]
            oe = te * cos + to * sin
            oo = -te * sin + to * cos
            return jnp.stack([oe, oo], axis=-1).reshape(t.shape)
        b, m, d = x.shape
        q = x @ wq.T
        k = x @ wk.T
        v = x @ wv.T
        cos, sin = _rope_tables(m, d)
        qr = _apply_rope(q, cos, sin)
        kr = _apply_rope(k, cos, sin)
        scores = jnp.einsum('bqd,bkd->bqk', qr, kr) / jnp.sqrt(jnp.float32(d))
        causal = jnp.tril(jnp.ones((m, m), dtype=bool))
        scores = jnp.where(causal[None, :, :], scores, jnp.finfo(scores.dtype).min)
        attn = jax.nn.softmax(scores, axis=-1)
        return jnp.einsum('bqk,bkd->bqd', attn, v)

    def _L2_ffn_ref(x, Wqkv, q_scale, k_scale, Wo, ln_g, ln_b, W1, b1, W2, b2):
        import jax, jax.numpy as jnp
        import numpy as np
        DIM = 128
        DEPTH = 6
        HEADS = 16
        DIM_HEAD = 64
        WINDOW = 32
        INNER = HEADS * DIM_HEAD
        DIM_INNER = int(DIM * 4 * 2 / 3)
        QK_SCALE = 8.0

        def shift_tokens(t):
            a, s = jnp.split(t, 2, -1)
            s = jnp.pad(s, ((0, 0), (1, 0), (0, 0)))[:, :-1]
            return jnp.concatenate([a, s], -1)

        def l2norm(t):
            return t / jnp.maximum(jnp.linalg.norm(t, axis=-1, keepdims=True), 1e-12)

        def rotate_half(x):
            x1, x2 = jnp.split(x, 2, -1)
            return jnp.concatenate([-x2, x1], -1)

        def rotary_tables(n):
            half = jnp.arange(0, DIM_HEAD, 2, dtype=jnp.float32)
            inv_freq = 1.0 / 10000.0 ** (half / DIM_HEAD)
            t = jnp.arange(n, dtype=jnp.float32)
            freqs = t[:, None] * inv_freq[None, :]
            freqs = jnp.concatenate([freqs, freqs], -1)
            base_scale = (half + 0.4 * DIM_HEAD) / (1.4 * DIM_HEAD)
            power = (t - n // 2) / (WINDOW // 2)
            scale = base_scale[None, :] ** power[:, None]
            scale = jnp.concatenate([scale, scale], -1)
            return (freqs, scale)

        def local_attention(q, k, v):
            b, h, n, d = q.shape
            w = WINDOW
            nw = n // w
            bq = q.reshape(b, h, nw, w, d)
            bk = k.reshape(b, h, nw, w, d)
            bv = v.reshape(b, h, nw, w, d)

            def look(t):
                p = jnp.pad(t, ((0, 0), (0, 0), (1, 0), (0, 0), (0, 0)))
                return jnp.concatenate([p[:, :, :nw], p[:, :, 1:]], axis=3)
            bk2, bv2 = (look(bk), look(bv))
            seq = jnp.arange(n).reshape(nw, w)
            seq_p = jnp.pad(seq, ((1, 0), (0, 0)), constant_values=-1)
            jt = jnp.concatenate([seq_p[:nw], seq_p[1:]], axis=1)
            it = seq[:, :, None]
            jb = jt[:, None, :]
            mask = (it < jb) | (it > jb + w) | (jb == -1)
            sim = jnp.einsum('bhwie,bhwje->bhwij', bq, bk2) * QK_SCALE
            sim = jnp.where(mask, -jnp.finfo(sim.dtype).max, sim)
            attn = jax.nn.softmax(sim, -1)
            out = jnp.einsum('bhwij,bhwje->bhwie', attn, bv2)
            return out.reshape(b, h, n, d)

        def attn_layer(x, Wqkv, qs, ksc, Wo):
            b, n, _ = x.shape
            qkv = x @ Wqkv
            q, k, v = jnp.split(qkv, 3, -1)
            sh = lambda t: t.reshape(b, n, HEADS, DIM_HEAD).transpose(0, 2, 1, 3)
            q, k, v = (sh(q), sh(k), sh(v))
            q = l2norm(q) * qs
            k = l2norm(k) * ksc
            freqs, scale = rotary_tables(n)
            cos, sin = (jnp.cos(freqs), jnp.sin(freqs))
            q = q * cos * scale + rotate_half(q) * sin * scale
            inv = 1.0 / scale
            k = k * cos * inv + rotate_half(k) * sin * inv
            out = local_attention(q, k, v)
            out = out.transpose(0, 2, 1, 3).reshape(b, n, INNER)
            return out @ Wo

        def ffn_layer(x, g, bln, W1, b1, W2, b2):
            mu = x.mean(-1, keepdims=True)
            var = ((x - mu) ** 2).mean(-1, keepdims=True)
            xn = (x - mu) / jnp.sqrt(var + 1e-05) * g + bln
            hg = xn @ W1 + b1
            a, gate = jnp.split(hg, 2, -1)
            return a * jax.nn.gelu(gate, approximate=False) @ W2 + b2
        for i in range(DEPTH):
            x = attn_layer(shift_tokens(x), Wqkv[i], q_scale[i], k_scale[i], Wo[i]) + x
            x = ffn_layer(shift_tokens(x), ln_g[i], ln_b[i], W1[i], b1[i], W2[i], b2[i]) + x
        return x

    def _L3_attn_ref(x, W_DQ, W_UQ, W_DKV, W_UKV, W_QR, W_KR, W_O, q_norm_w, k_norm_w):
        import jax, jax.numpy as jnp
        import numpy as np
        B, T, D = (2, 256, 128)
        H = 16
        HD = D // H
        DL = 64
        NR = 64
        EPS = 1.1920929e-07

        def _rms_norm(x, w):
            ms = jnp.mean(jnp.square(x), axis=-1, keepdims=True)
            return x * jax.lax.rsqrt(ms + EPS) * w
        b, t, d = x.shape
        scale = HD ** (-0.5)
        xh = x.reshape(b, t, H, HD).transpose(0, 2, 1, 3)
        c_q = jnp.einsum('bhtd,ld->bhtl', xh, W_DQ)
        q_c = jnp.einsum('bhtl,dl->bhtd', c_q, W_UQ)
        q_c_norm = _rms_norm(q_c, q_norm_w)
        q_r = jnp.einsum('bhtd,rd->bhtr', q_c_norm, W_QR)
        q = jnp.concatenate([q_c_norm, q_r], axis=-1)
        c_kv = jnp.einsum('bhtd,ld->bhtl', xh, W_DKV)
        kv = jnp.einsum('bhtl,dl->bhtd', c_kv, W_UKV)
        k_c, v_c = (kv[..., :HD], kv[..., HD:])
        k_c_norm = _rms_norm(k_c, k_norm_w)
        k_r = jnp.einsum('bhtd,rd->bhtr', xh, W_KR)
        k = jnp.concatenate([k_c_norm, k_r], axis=-1)
        scores = jnp.einsum('bhqd,bhkd->bhqk', q, k) * scale
        causal = jnp.triu(jnp.full((t, t), -jnp.inf, dtype=scores.dtype), k=1)
        attn = jax.nn.softmax(scores + causal, axis=-1)
        ctx = jnp.einsum('bhqk,bhkd->bhqd', attn, v_c)
        out = jnp.einsum('bhtd,od->bhto', ctx, W_O)
        return out.transpose(0, 2, 1, 3).reshape(b, t, d)

    def _L3_ffn_ref(x, ln1_g, ln1_b, ln2_g, ln2_b, wq, bq, wk, bk, wv, bv, wo, bo, gate_w, gate_b, w1, b1, w2, b2):
        import jax, jax.numpy as jnp
        import numpy as np
        B, S, H, NH, E, F = (4, 128, 128, 16, 8, 512)
        D = H // NH
        EPS = 1e-05

        def _layernorm(x, g, b):
            mu = jnp.mean(x, axis=-1, keepdims=True)
            var = jnp.var(x, axis=-1, keepdims=True)
            return (x - mu) * jax.lax.rsqrt(var + EPS) * g + b
        b, s, h = x.shape
        hn = _layernorm(x, ln1_g, ln1_b)
        q = (hn @ wq + bq).reshape(b, s, NH, D).transpose(0, 2, 1, 3)
        k = (hn @ wk + bk).reshape(b, s, NH, D).transpose(0, 2, 1, 3)
        v = (hn @ wv + bv).reshape(b, s, NH, D).transpose(0, 2, 1, 3)
        scores = jnp.einsum('bhqd,bhkd->bhqk', q, k) / jnp.sqrt(jnp.float32(D))
        attn = jax.nn.softmax(scores, axis=-1)
        o = jnp.einsum('bhqk,bhkd->bhqd', attn, v)
        o = o.transpose(0, 2, 1, 3).reshape(b, s, h)
        x = x + (o @ wo + bo)
        hn2 = _layernorm(x, ln2_g, ln2_b).reshape(-1, h)
        logits = hn2 @ gate_w + gate_b
        idx = jnp.argmax(logits, axis=-1)
        mid = jax.nn.relu(jnp.einsum('th,ehf->etf', hn2, w1) + b1[:, None, :])
        y = jnp.einsum('etf,efh->eth', mid, w2) + b2[:, None, :]
        moe = y[idx, jnp.arange(hn2.shape[0])]
        return x + moe.reshape(b, s, h)
    x = L0_attn_x
    x = x + _L0_attn_ref(_layernorm(x, axis=-1), L0_attn_Wq, L0_attn_bq, L0_attn_Wk, L0_attn_bk, L0_attn_Wv, L0_attn_bv, L0_attn_Wo, L0_attn_bo)
    x = x + _L0_ffn_ref(_layernorm(x, axis=-1), L0_ffn_w1, L0_ffn_v1, L0_ffn_w2, L0_ffn_router_w)
    x = x + _L1_attn_ref(_layernorm(x, axis=-1), L1_attn_Wqkv, L1_attn_Wproj, L1_attn_bproj)
    x = x + _L1_ffn_ref(_layernorm(x, axis=-1), L1_ffn_Wqkv, L1_ffn_q_scale, L1_ffn_k_scale, L1_ffn_Wo, L1_ffn_ln_g, L1_ffn_ln_b, L1_ffn_W1, L1_ffn_b1, L1_ffn_W2, L1_ffn_b2)
    x = x + _L2_attn_ref(_layernorm(x, axis=-1), L2_attn_wq, L2_attn_wk, L2_attn_wv)
    x = x + _L2_ffn_ref(_layernorm(x, axis=-1), L2_ffn_Wqkv, L2_ffn_q_scale, L2_ffn_k_scale, L2_ffn_Wo, L2_ffn_ln_g, L2_ffn_ln_b, L2_ffn_W1, L2_ffn_b1, L2_ffn_W2, L2_ffn_b2)
    x = x + _L3_attn_ref(_layernorm(x, axis=-1), L3_attn_W_DQ, L3_attn_W_UQ, L3_attn_W_DKV, L3_attn_W_UKV, L3_attn_W_QR, L3_attn_W_KR, L3_attn_W_O, L3_attn_q_norm_w, L3_attn_k_norm_w)
    x = x + _L3_ffn_ref(_layernorm(x, axis=-1), L3_ffn_ln1_g, L3_ffn_ln1_b, L3_ffn_ln2_g, L3_ffn_ln2_b, L3_ffn_wq, L3_ffn_bq, L3_ffn_wk, L3_ffn_bk, L3_ffn_wv, L3_ffn_bv, L3_ffn_wo, L3_ffn_bo, L3_ffn_gate_w, L3_ffn_gate_b, L3_ffn_w1, L3_ffn_b1, L3_ffn_w2, L3_ffn_b2)
    return x

_drawn_inputs = setup_inputs


def setup_inputs(seed=0):
    import zlib

    import numpy as np

    out = dict(_drawn_inputs(seed))
    spreads = {'L1_ffn_q_scale': (1.0, 0.6),
     'L1_ffn_k_scale': (1.0, 0.6),
     'L1_ffn_ln_g': (1.0, 0.6),
     'L1_ffn_ln_b': (0.0, 0.8),
     'L1_ffn_b1': (0.0, 0.8),
     'L1_ffn_b2': (0.0, 0.1),
     'L2_ffn_q_scale': (1.0, 0.6),
     'L2_ffn_k_scale': (1.0, 0.6),
     'L2_ffn_ln_g': (1.0, 0.6),
     'L2_ffn_ln_b': (0.0, 0.8),
     'L2_ffn_b1': (0.0, 0.8),
     'L2_ffn_b2': (0.0, 0.1),
     'L3_attn_q_norm_w': (1.0, 0.6),
     'L3_attn_k_norm_w': (1.0, 0.6),
     'L3_ffn_ln1_g': (1.0, 0.6),
     'L3_ffn_ln1_b': (0.0, 0.8),
     'L3_ffn_ln2_g': (1.0, 0.6),
     'L3_ffn_ln2_b': (0.0, 2.0),
     'L3_ffn_bq': (0.0, 0.8),
     'L3_ffn_bk': (0.0, 2.0),
     'L3_ffn_bv': (0.0, 0.8),
     'L3_ffn_bo': (0.0, 2.0),
     'L3_ffn_gate_b': (0.0, 0.319),
     'L3_ffn_b1': (0.0, 2.0),
     'L3_ffn_b2': (0.0, 1.614)}
    factors = {'L0_attn_Wq': 8.0,
     'L0_attn_bq': 8.0,
     'L0_attn_Wk': 8.0,
     'L0_attn_bk': 200.0,
     'L0_attn_Wv': 6.464,
     'L0_attn_bv': 8.0,
     'L0_attn_Wo': 5.634,
     'L0_ffn_w1': 8.0,
     'L0_ffn_v1': 8.0,
     'L0_ffn_w2': 8.0,
     'L0_ffn_router_w': 8.0,
     'L1_attn_Wqkv': 8.0,
     'L1_attn_Wproj': 8.0,
     'L1_ffn_W1': 3.561,
     'L1_ffn_W2': 3.52,
     'L2_attn_wq': 8.0,
     'L2_attn_wk': 8.0,
     'L2_ffn_W1': 5.33,
     'L2_ffn_W2': 5.243,
     'L3_attn_W_DQ': 64.0,
     'L3_attn_W_UQ': 64.0,
     'L3_attn_W_DKV': 42.111,
     'L3_attn_W_UKV': 38.081,
     'L3_attn_W_QR': 64.0,
     'L3_attn_W_KR': 64.0,
     'L3_attn_W_O': 32.418,
     'L3_ffn_wq': 8.0,
     'L3_ffn_wk': 8.0,
     'L3_ffn_wv': 8.0,
     'L3_ffn_wo': 6.962,
     'L3_ffn_w1': 10.598,
     'L3_ffn_w2': 2.801,
     'L1_attn_bproj': 6.034}
    for name, (base, spread) in spreads.items():
        noise = np.random.default_rng([zlib.crc32(name.encode()), seed]).standard_normal(out[name].shape)
        drawn = base * np.exp(spread * noise) if base else spread * noise
        out[name] = jnp.asarray(drawn.astype(out[name].dtype))
    for name, factor in factors.items():
        out[name] = (out[name] * factor).astype(out[name].dtype)
    return out
```

```python
import concourse.bass as bass
from concourse import mybir
from contextlib import ExitStack

F32 = mybir.dt.float32
I32 = mybir.dt.int32
BF16 = mybir.dt.bfloat16
ALU = mybir.AluOpType
ACT = mybir.ActivationFunctionType
AX = mybir.AxisListType.X

P = 128
B, S, D = 8, 256, 128
HALVES = S // P
ROW = S * D // P
NH = 16
HD = D // NH
GROUPS = NH // 4
DEPTH = 6
DH = 64
INNER = NH * DH
WINDOW = 32
FF = 341
FF_CHUNKS = [(0, 128), (128, 128), (256, 85)]
EXPERTS = 8
MASKED = -1e30
MAGIC = float(0x5F3759DF)
LN_EPS = 1e-5
RMS_EPS = 1.1920929e-07


def row(b, n=ROW, at=0):
    return bass.ds(b * n + at, n if at == 0 else n)


def half(b, t):
    return bass.ds(b * ROW + t * D, D)


class Steps:

    def __init__(self, eng, sem, turn, per_turn):
        self.eng, self.sem, self.turn, self.per_turn, self.n = eng, sem, turn, per_turn, 0

    def after(self, instruction):
        self.n += 1
        instruction.then_inc(self.sem, 1)
        self.eng.wait_ge(self.sem, self.turn * self.per_turn + self.n)

    def end(self):
        assert self.n == self.per_turn, (self.n, self.per_turn)


class Shared:

    def __init__(self, sem):
        self.sem, self.kept, self.turns = sem, {}, {}

    def take(self, stage, names, turns):
        if stage not in self.kept:
            self.kept[stage], self.turns[stage] = [self.sem(stage + "_" + n) for n in names], 0
        before = self.turns[stage]
        self.turns[stage] += turns
        return self.kept[stage], before


class Chip:
    pass


def allocate(nc, ctx):
    c = Chip()

    def sb(name, shape, dt=F32):
        return ctx.enter_context(nc.sbuf_tensor(name, shape, dt))

    c.X = sb("X", [P, B * ROW])
    c.Y = sb("Y", [P, B * ROW])
    c.ident = sb("ident", [P, P])
    c.identb = sb("identb", [P, P], BF16)
    c.causal = sb("causal", [P, P], BF16)
    c.band0 = sb("band0", [P, P], BF16)
    c.band1 = sb("band1", [P, P + WINDOW], BF16)
    c.shift = sb("shift", [P, P])
    c.carry = sb("carry", [P, P])
    c.headmask = sb("headmask", [P, P])
    c.headcol = sb("headcol", [P, NH])
    c.iota8 = sb("iota8", [P, HALVES, EXPERTS])
    c.neg_half = sb("neg_half", [P, 64])
    c.stats = sb("stats", [P, HALVES, 6])
    c.mv = sb("mv", [P, HALVES, 2])
    c.vareps = sb("vareps", [P, 32])
    c.rstd = sb("rstd", [P, 32])
    c.xn = sb("xn", [P, HALVES, D])
    c.xT = sb("xT", [P, S])
    c.qT = sb("qT", [P, 8, S])
    c.kT = sb("kT", [P, 8, S])
    c.V = sb("V", [P, HALVES, NH, DH + 1])
    c.negmax = sb("negmax", [P, NH, HALVES])
    c.probs = sb("probs", [P, 2, 512])
    c.probsT = sb("probsT", [P, 2, 512])
    c.recip = sb("recip", [P, 2, 32])
    c.ctx = sb("ctx", [P, HALVES, INNER])
    c.ctxT = sb("ctxT", [P, 8, S])
    c.wA = sb("wA", [P, 3 * INNER])
    c.wB = sb("wB", [P, 8 * D])
    c.wC = sb("wC", [P, 2 * FF])
    c.wD = sb("wD", [P, 3 * D])
    c.rope = sb("rope", [P, 4, HALVES, 2 * DH])
    c.ropes = sb("ropes", [P, 4, HALVES, DH])
    c.scl = sb("scl", [P, 4, DH])
    c.cols = sb("cols", [P, 32])
    c.colsA = sb("colsA", [P, 8 * DEPTH])
    c.rows = sb("rows", [P, 4, D])
    c.big = sb("big", [P, 2 * EXPERTS * 512])
    c.sq = sb("sq", [P, 2, 512])
    c.turnA = sb("turnA", [P, 2, 512])
    c.turnB = sb("turnB", [P, 2, 512])
    c.qk = sb("qk", [P, HALVES, 2, INNER])
    c.ss = sb("ss", [P, HALVES, 32])
    c.rs = sb("rs", [P, 3, HALVES, 32])
    c.v1 = sb("v1", [P, HALVES, D + 4])
    c.kvblock = sb("kvblock", [P, D + NH])
    c.hT = sb("hT", [P, 3, S])
    c.onehotT = sb("onehotT", [EXPERTS, S])
    c.bottom = sb("bottom", [EXPERTS, D])
    c.ints = sb("ints", [P, 64], I32)
    c.newton = sb("newton", [P, 3, 64])
    c.small = sb("small", [P, 16, HALVES * EXPERTS])
    c.bank = [ctx.enter_context(nc.psum_tensor(f"bank{i}", [P, 512], F32)) for i in range(8)]
    return c




def setup(nc, sem, c, io):
    loaded, zeroed, built = sem("x_loaded"), sem("consts_zeroed"), sem("consts_built")
    with nc.Block() as block:

        @block.sync
        def _(sp):
            for b in range(B):
                sp.dma_start(c.X[:, b * ROW:(b + 1) * ROW].rearrange("p (t d) -> p t d", t=HALVES),
                             io["x"][b].rearrange("(t p) d -> p t d", p=P)).then_inc(loaded, 16)
            sp.dma_start(c.headmask[:, :], io["headmask"]).then_inc(loaded, 16)
            sp.dma_start(c.headcol[:, :], io["headcol"]).then_inc(loaded, 16)
            sp.wait_ge(loaded, 16 * (B + 2))

        @block.vector
        def _(v):
            for tile, value in ((c.ident, 0.0), (c.identb, 0.0), (c.causal, 0.0), (c.band0, 0.0), (c.band1, 0.0),
                                (c.shift, 0.0), (c.carry, 0.0), (c.neg_half, -0.5)):
                last = v.memset(tile[:, :], value)
            v.memset(c.V[:, :, :, :], 1.0)
            v.memset(c.xT[:, :], 0.0)
            v.memset(c.v1[:, :, :], 1.0)
            v.memset(c.hT[:, :, :], 1.0)
            last = v.memset(c.probsT[:, :, :], 0.0)
            last.then_inc(zeroed, 1)

        @block.gpsimd
        def _(pool):
            pool.wait_ge(zeroed, 1)

            def where(tile, n, keep, base, mult, step, fill):
                return pool.affine_select(out=tile, in_=tile, pattern=[[step, n]], compare_op=keep, fill=fill,
                                          base=base, channel_multiplier=mult)

            where(c.ident[:, :], P, ALU.not_equal, 0, 1, -1, 1.0)
            where(c.identb[:, :], P, ALU.not_equal, 0, 1, -1, 1.0)
            where(c.shift[:, :], P, ALU.not_equal, 1, 1, -1, 1.0)
            where(c.carry[:, :], P, ALU.not_equal, 1 - P, 1, -P, 1.0)
            where(c.causal[:, :], P, ALU.is_ge, 0, 1, -1, MASKED)
            first = where(c.band0[:, :], P, ALU.is_ge, 0, 1, -1, MASKED)
            other = where(c.band1[:, :], P + WINDOW, ALU.is_ge, WINDOW, 1, -1, MASKED)
            other.then_inc(built, 1)
            pool.wait_ge(built, 1)
            where(c.band0[:, :], P, ALU.is_ge, WINDOW, -1, 1, MASKED)
            where(c.band1[:, :], P + WINDOW, ALU.is_ge, 0, -1, 1, MASKED)
            pool.iota(c.small[:, 0, :].bitcast(I32), pattern=[[0, HALVES], [1, EXPERTS]], base=0,
                      channel_multiplier=0).then_inc(built, 1)
            pool.wait_ge(built, 2)
            pool.tensor_copy(c.iota8[:, :, :], c.small[:, 0, :].bitcast(I32).rearrange("p (t e) -> p t e", t=HALVES))



LN_STEPS = 2


class Norm:

    def __init__(self, c, src, gain=None, stage="norm", turns=B):
        self.c, self.src, self.gain = c, src, gain
        names = ("var_ready", "rstd_ready", "xn_ready", "xT_in_psum", "xT_ready")
        (self.var_ready, self.rstd_ready, self.xn_ready, self.xT_in_psum,
         self.xT_ready), self.before = c.shared.take(stage, names, turns)

    def source(self, b, t):
        if self.src is None:
            return self.c.xn[:, t, :]
        return self.src[:, half(b, t)]

    def vector(self, v, b, step, turn=None):
        c, turn = self.c, (b if turn is None else turn) + self.before
        for t in range(HALVES):
            last = v.bn_stats(c.stats[:, t, :], self.source(b, t))
        step.after(last)
        v.memset(c.vareps[:, 30:31], 0.0)
        for t in range(HALVES):
            last = v.bn_aggr(c.mv[:, t, :], c.stats[:, t, :])
        step.after(last)
        v.tensor_scalar(c.vareps[:, 0:HALVES], c.mv[:, :, 1], LN_EPS, None, ALU.add).then_inc(self.var_ready, 1)
        v.wait_ge(self.rstd_ready, turn + 1)
        for t in range(HALVES):
            last = v.tensor_scalar(c.xn[:, t, :], self.source(b, t), c.mv[:, t, 0:1], c.rstd[:, t:t + 1],
                                   ALU.subtract, ALU.mult)
        last.then_inc(self.xn_ready, 1)

    def pool(self, g, turn):
        c, turn = self.c, turn + self.before
        g.wait_ge(self.var_ready, turn + 1)
        g.tensor_tensor(c.rstd[:, 0:HALVES], c.vareps[:, 0:HALVES], c.neg_half[:, 0:HALVES],
                        ALU.pow).then_inc(self.rstd_ready, 1)

    def tensor(self, pe, turn):
        c, turn = self.c, turn + self.before
        pe.wait_ge(self.xn_ready, turn + 1)
        for t in range(HALVES):
            last = pe.transpose(c.bank[6][:, t * P:(t + 1) * P], c.xn[:, t, :], c.ident[:, :])
        last.then_inc(self.xT_in_psum, 1)
        pe.wait_ge(self.xT_ready, turn + 1)

    def scalar(self, a, turn):
        c, turn = self.c, turn + self.before
        a.wait_ge(self.xT_in_psum, turn + 1)
        if self.gain is None:
            last = a.activation(c.xT[:, :], c.bank[6][:, 0:S], ACT.Identity)
        else:
            last = a.activation(c.xT[:, :], c.bank[6][:, 0:S], ACT.Identity, scale=self.gain[0], bias=self.gain[1])
        last.then_inc(self.xT_ready, 1)




class Core:

    def __init__(self, c, heads, blocks, operands, values, width, per_ctx, stage, turns=B):
        self.c, self.heads, self.blocks = c, heads, blocks
        self.operands, self.values, self.width, self.per_ctx = operands, values, width, per_ctx
        names = ("qk_ready", "scores_ready", "negmax_ready", "probs_ready", "probsT_in_psum", "probsT_ready",
                 "ctx_in_psum", "recip_ready", "ctx_ready")
        (self.qk_ready, self.scores_ready, self.negmax_ready, self.probs_ready, self.probsT_in_psum,
         self.probsT_ready, self.ctx_in_psum, self.recip_ready,
         self.ctx_ready), self.before = c.shared.take(stage, names, turns)
        self.n_ctx = heads // per_ctx
        self.at, n = [], 0
        for t in range(HALVES):
            for (kt, k0, kn, mask) in blocks[t]:
                self.at.append((t, kt, k0, kn, n))
                n += kn
        self.used = n
        self.span = [sum(x[2] for x in blocks[t]) for t in range(HALVES)]

    def scores(self, pe, turn, h):
        c = self.c
        out = c.bank[h % 2]
        at = 0
        for t in range(HALVES):
            q, k = self.operands(h)
            first = self.blocks[t][0]
            k0 = first[0] * P + first[1]
            n = self.span[t]
            masks = [x for x in self.blocks[t] if x[3] is not None]
            last = pe.matmul(out[:, at:at + n], q[:, t * P:(t + 1) * P], k[:, k0:k0 + n], start=True,
                             stop=not masks, skip_group_check=True)
            if masks:
                mask, off = masks[0][3]
                last = pe.matmul(out[:, at + off:at + n], self.c.identb[:, :], mask, start=False, stop=True,
                                 skip_group_check=True)
            at += n
        last.then_inc(self.scores_ready, 1)

    def turn_probs(self, pe, turn, h):
        c = self.c
        pe.wait_ge(self.probs_ready, turn * self.heads + h + 1)
        for i, (t, kt, k0, kn, at) in enumerate(self.at):
            last = pe.transpose(c.bank[2 + h % 2][0:kn, i * P:(i + 1) * P], c.probs[:, h % 2, at:at + kn],
                                c.ident[:, :])
        last.then_inc(self.probsT_in_psum, 1)

    def weigh(self, pe, turn, h):
        c = self.c
        n, w = self.per_ctx, self.width
        group = h // n
        pe.wait_ge(self.probsT_ready, turn * self.heads + h + 1)
        if h % n == 0 and group >= 2:
            pe.wait_ge(self.ctx_ready, turn * self.n_ctx + group - 1)
        for t in range(HALVES):
            mine = [(i, x) for i, x in enumerate(self.at) if x[0] == t]
            o = (t * n + h % n) * w
            for j, (i, (_, kt, k0, kn, at)) in enumerate(mine):
                last = pe.matmul(c.bank[4 + group % 2][:, o:o + w], c.probsT[k0:k0 + kn, h % 2, i * P:(i + 1) * P],
                                 self.values(h, kt)[k0:k0 + kn, :], start=(j == 0), stop=(j == len(mine) - 1))
        if h % n == n - 1:
            last.then_inc(self.ctx_in_psum, 1)

    def tensor(self, pe, turn):
        turn = turn + self.before
        pe.wait_ge(self.qk_ready, turn + 1)
        self.scores(pe, turn, 0)
        if self.heads > 1:
            self.scores(pe, turn, 1)
        for h in range(self.heads):
            self.turn_probs(pe, turn, h)
            if h + 2 < self.heads:
                self.scores(pe, turn, h + 2)
            if h >= 1:
                self.weigh(pe, turn, h - 1)
        self.weigh(pe, turn, self.heads - 1)

    def vector(self, v, turn):
        c, H, turn = self.c, self.heads, turn + self.before
        for h in range(H + 1):
            if h < H:
                v.wait_ge(self.scores_ready, turn * H + h + 1)
                at = 0
                for t in range(HALVES):
                    last = v.tensor_reduce(c.negmax[:, h, t:t + 1], c.bank[h % 2][:, at:at + self.span[t]], AX,
                                           ALU.max, negate=True)
                    at += self.span[t]
                last.then_inc(self.negmax_ready, 1)
            if h >= 1:
                self.copy_probs(v, turn, h - 1)
                if h % self.per_ctx == 0:
                    self.normalise(v, turn, h // self.per_ctx - 1)

    def copy_probs(self, v, turn, h):
        c, H = self.c, self.heads
        v.wait_ge(self.probsT_in_psum, turn * H + h + 1)
        src, dst = c.bank[2 + h % 2], c.probsT[:, h % 2, :]
        if all(x[3] == P for x in self.at):
            n = len(self.at) * P
            last = v.tensor_copy(dst[:, 0:n], src[:, 0:n])
        else:
            for i, (t, kt, k0, kn, at) in enumerate(self.at):
                last = v.tensor_copy(dst[k0:k0 + kn, i * P:(i + 1) * P], src[0:kn, i * P:(i + 1) * P])
        last.then_inc(self.probsT_ready, 1)

    def normalise(self, v, turn, group):
        c, n, w = self.c, self.per_ctx, self.width
        v.wait_ge(self.ctx_in_psum, turn * self.n_ctx + group + 1)
        src = c.bank[4 + group % 2][:, 0:HALVES * n * w].rearrange("p (t h w) -> p t h w", t=HALVES, h=n)
        rec = c.recip[:, group % 2, 0:HALVES * n].rearrange("p (t h) -> p t h", t=HALVES)
        v.reciprocal(rec, src[:, :, :, w - 1]).then_inc(self.recip_ready, 1)
        v.wait_ge(self.recip_ready, turn * self.n_ctx + group + 1)
        for t in range(HALVES):
            dst = c.ctx[:, t, group * n * (w - 1):(group + 1) * n * (w - 1)].rearrange("p (h w) -> p h w", h=n)
            last = v.tensor_tensor(dst, src[:, t, :, 0:w - 1],
                                   rec[:, t, :].unsqueeze(2).broadcast_to((P, n, w - 1)), ALU.mult)
        last.then_inc(self.ctx_ready, 1)

    def scalar(self, a, turn):
        c, H, turn = self.c, self.heads, turn + self.before
        for h in range(H):
            a.wait_ge(self.negmax_ready, turn * H + h + 1)
            at = 0
            for t in range(HALVES):
                last = a.activation(c.probs[:, h % 2, at:at + self.span[t]], c.bank[h % 2][:, at:at + self.span[t]],
                                    ACT.Exp, bias=c.negmax[:, h, t:t + 1])
                at += self.span[t]
            last.then_inc(self.probs_ready, 1)


def causal_blocks(c):
    tri = c.causal[:, :]
    return [[(0, 0, P, (tri, 0))], [(0, 0, P, None), (1, 0, P, (tri, P))]]


def full_blocks():
    return [[(0, 0, P, None), (1, 0, P, None)]] * 2




def plain_attention(nc, sem, c, name, io, x, causal, affine):
    w = io[name]
    norm = Norm(c, x, (c.cols[:, 8:9], c.cols[:, 9:10]) if affine else None)
    core = Core(c, NH, causal_blocks(c) if causal else full_blocks(),
                lambda h: (c.qT[32 * (h % 4):32 * (h % 4) + 32, h // 4, :], c.kT[32 * (h % 4):32 * (h % 4) + 32, h // 4, :]),
                lambda h, kt: c.V[:, kt, h, DH - HD:DH + 1], HD + 1, NH, "heads")
    loaded, bias_scaled = sem(name + "_weights"), sem(name + "_bias_scaled")
    proj_in_psum, proj_copied, step_v = sem(name + "_proj_in_psum"), sem(name + "_proj_copied"), sem(name + "_steps")
    v_in_psum, v_ready = sem(name + "_v_in_psum"), sem(name + "_v_ready")
    ctxT_in_psum, ctxT_ready = sem(name + "_ctxT_in_psum"), sem(name + "_ctxT_ready")
    out_in_psum = sem(name + "_out_in_psum")
    wq, wk = c.wA[:, 0:512], c.wA[:, 512:1024]
    wv, wo = c.wB[:, 0:D], c.wB[:, D:2 * D]
    scale = float(HD) ** -0.5
    with nc.Block() as block:

        @block.sync
        def _(sp):
            n = 0
            for dst, src in ((wq, w["wq"]), (wk, w["wk"]), (wv, w["wv"]), (wo, w["wo"]), (c.cols[:, 0:10], w["cols"]),
                             (c.rows[:, 0, :], w["bv"].partition_broadcast(P)),
                             (c.rows[:, 1, :], w["bo"].partition_broadcast(P))):
                sp.dma_start(dst, src).then_inc(loaded, 16)
                n += 16
            sp.wait_ge(loaded, n)

        @block.tensor
        def _(pe):
            pe.wait_ge(loaded, 112)
            with pe.Fori(0, B) as b:
                norm.tensor(pe, b)
                for u, (weights, g0) in enumerate(((wq, 0), (wq, 2), (wk, 0), (wk, 2))):
                    for g in range(2):
                        last = pe.matmul(c.bank[u][:, g * S:(g + 1) * S], weights[:, (g0 + g) * P:(g0 + g + 1) * P],
                                         c.xT[:, :], start=True, stop=True)
                    last.then_inc(proj_in_psum, 1)
                for t in range(HALVES):
                    last = pe.matmul(c.bank[7][:, t * D:(t + 1) * D], c.xT[:, t * P:(t + 1) * P], wv, start=True,
                                     stop=True)
                last.then_inc(v_in_psum, 1)
                pe.wait_ge(v_ready, b + 1)
                core.tensor(pe, b)
                pe.wait_ge(core.ctx_ready, core.before + b + 1)
                for t in range(HALVES):
                    last = pe.transpose(c.bank[6][:, t * P:(t + 1) * P], c.ctx[:, t, 0:D], c.ident[:, :])
                last.then_inc(ctxT_in_psum, 1)
                pe.wait_ge(ctxT_ready, b + 1)
                for t in range(HALVES):
                    last = pe.matmul(c.bank[7][:, t * D:(t + 1) * D], c.ctxT[:, 0, t * P:(t + 1) * P], wo, start=True,
                                     stop=True)
                last.then_inc(out_in_psum, 1)

        @block.gpsimd
        def _(g):
            with g.Fori(0, B) as b:
                norm.pool(g, b)

        @block.scalar
        def _(a):
            a.wait_ge(loaded, 112)
            a.mul(c.cols[:, 16:20], c.cols[:, 0:4], scale).then_inc(bias_scaled, 1)
            a.wait_ge(bias_scaled, 1)
            a.activation(c.cols[:, 30:31], c.cols[:, 0:1], ACT.Exp)
            with a.Fori(0, B) as b:
                norm.scalar(a, b)
                for u in range(4):
                    a.wait_ge(proj_in_psum, b * 4 + u + 1)
                    for g in range(2):
                        src, gg = c.bank[u][:, g * S:(g + 1) * S], 2 * (u % 2) + g
                        if u < 2:
                            last = a.activation(c.qT[:, gg, :], src, ACT.Identity, scale=scale,
                                                bias=c.cols[:, 16 + gg:17 + gg])
                        else:
                            last = a.activation(c.kT[:, gg, :], src, ACT.Identity, bias=c.cols[:, 4 + gg:5 + gg])
                last.then_inc(core.qk_ready, 1)
                core.scalar(a, b)
                a.wait_ge(ctxT_in_psum, b + 1)
                a.activation(c.ctxT[:, 0, :], c.bank[6][:, 0:S], ACT.Identity).then_inc(ctxT_ready, 1)

        @block.vector
        def _(v):
            v.wait_ge(loaded, 112)
            with v.Fori(0, B) as b:
                step = Steps(v, step_v, b, 3)
                norm.vector(v, b, step)
                v.wait_ge(v_in_psum, b + 1)
                v.tensor_tensor(c.V[:, :, :, DH - HD:DH],
                                c.bank[7][:, 0:S].rearrange("p (t h d) -> p t h d", t=HALVES, h=NH),
                                c.rows[:, 0, :].rearrange("p (h d) -> p h d", h=NH).unsqueeze(1)
                                .broadcast_to((P, HALVES, NH, HD)), ALU.add).then_inc(v_ready, 1)
                core.vector(v, b)
                v.wait_ge(out_in_psum, b + 1)
                add_rows(v, step, x, b, c.bank[7][:, 0:S], c.rows[:, 1, :])
                step.end()


def add_rows(v, step, x, b, more, bias=None):
    first = v.tensor_tensor(x[:, row(b)], x[:, row(b)], more, ALU.add)
    if bias is None:
        return first
    step.after(first)
    halves = x[:, row(b)].rearrange("p (t d) -> p t d", t=HALVES)
    return v.tensor_tensor(halves, halves, bias.unsqueeze(1).broadcast_to((P, HALVES, D)), ALU.add)


NEWTON_STEPS = 11


def rsqrt(v, step, c, x, y):
    n = x.shape[-1]
    ints, a, b, y2 = c.ints[:, 0:n], c.newton[:, 0, 0:n], c.newton[:, 1, 0:n], c.newton[:, 2, 0:n]
    step.after(v.tensor_scalar(ints, x.bitcast(I32), 1, None, ALU.logical_shift_right))
    step.after(v.tensor_scalar(a.bitcast(I32), ints, -1.0, MAGIC, ALU.mult, ALU.add))
    for src, dst in ((a, b), (b, a), (a, y)):
        step.after(v.tensor_tensor(y2, src, src, ALU.mult))
        step.after(v.scalar_tensor_tensor(out=y2, in0=y2, scalar=-0.5, in1=x, op0=ALU.mult, op1=ALU.mult))
        step.after(v.scalar_tensor_tensor(out=dst, in0=y2, scalar=1.5, in1=src, op0=ALU.add, op1=ALU.mult))




def experts(nc, sem, c, name, io, x, gated):
    w = io[name]
    F = 256 if gated else 512
    chunks = F // P
    norm = Norm(c, x, None if gated else (c.cols[:, 0:1], c.cols[:, 1:2]))
    loaded, step_v = sem(name + "_weights"), sem(name + "_steps")
    logits_in_psum, gap_ready, share_ready = sem(name + "_logits_in_psum"), sem(name + "_gap_ready"), sem(name + "_share_ready")
    onehot_ready, onehotT_in_psum, onehotT_ready = sem(name + "_onehot_ready"), sem(name + "_onehotT_in_psum"), sem(name + "_onehotT_ready")
    up_in_psum, act_ready, hidden_ready = sem(name + "_up_in_psum"), sem(name + "_act_ready"), sem(name + "_hidden_ready")
    down_in_psum, acc_done, bias_in_psum = sem(name + "_down_in_psum"), sem(name + "_acc_done"), sem(name + "_bias_in_psum")
    up, side = c.big[:, 0:EXPERTS * F], c.big[:, EXPERTS * F:2 * EXPERTS * F]
    down0 = 2 * EXPERTS * F if gated else EXPERTS * F
    down = c.big[:, down0:down0 + EXPERTS * F]
    router = c.wB[:, 0:EXPERTS]
    hidden = c.qk[:, :, 0, 0:chunks * S]

    def te(i):
        return c.small[:, i, :].rearrange("p (t e) -> p t e", t=HALVES)

    logits, equal, cand, best1, rest, best2, weight, tmp = [te(i) for i in range(1, 9)]
    top = c.small[:, 10, 0:12].rearrange("p (k t) -> p k t", t=HALVES)

    def over(col):
        return col.unsqueeze(2).broadcast_to((P, HALVES, EXPERTS))

    with nc.Block() as block:

        @block.sync
        def _(sp):
            n = 0
            todo = [(up, w["up"]), (down, w["down"]), (router, w["router"])]
            if gated:
                todo.append((side, w["side"]))
            else:
                todo += [(c.cols[:, 0:2], w["ln"]), (c.colsA[:, 0:32], w["b1"]), (c.bottom[:, :], w["b2"]),
                         (c.rows[:, 0, 0:EXPERTS], w["gate_b"].partition_broadcast(P))]
            for dst, src in todo:
                sp.dma_start(dst, src).then_inc(loaded, 16)
                n += 16
            sp.wait_ge(loaded, n)

        all_loaded = 16 * (4 if gated else 7)

        @block.tensor
        def _(pe):
            pe.wait_ge(loaded, all_loaded)

            def go_up(b, e):
                for k in range(chunks):
                    out = c.bank[2 * (e % 2) + (0 if gated else k // 2)][:, (k % 2) * S:(k % 2) * S + S]
                    last = pe.matmul(out, up[:, e * F + k * P:e * F + (k + 1) * P], c.xT[:, :], start=True, stop=True)
                if gated:
                    for k in range(chunks):
                        last = pe.matmul(c.bank[2 * (e % 2) + 1][:, k * S:(k + 1) * S],
                                         side[:, e * F + k * P:e * F + (k + 1) * P], c.xT[:, :], start=True, stop=True)
                last.then_inc(up_in_psum, 1)

            def go_down(b, e):
                pe.wait_ge(hidden_ready, b * EXPERTS + e + 1)
                if e >= 2:
                    pe.wait_ge(acc_done, b * EXPERTS + e - 1)
                for t in range(HALVES):
                    for k in range(chunks):
                        last = pe.matmul(c.bank[4 + e % 2][:, t * D:(t + 1) * D],
                                         hidden[:, e % 2, k * S + t * P:k * S + (t + 1) * P],
                                         down[:, e * F + k * D:e * F + (k + 1) * D], start=(k == 0),
                                         stop=(k == chunks - 1))
                last.then_inc(down_in_psum, 1)

            with pe.Fori(0, B) as b:
                norm.tensor(pe, b)
                for t in range(HALVES):
                    last = pe.matmul(c.bank[7][:, t * EXPERTS:(t + 1) * EXPERTS], c.xT[:, t * P:(t + 1) * P], router,
                                     start=True, stop=True)
                last.then_inc(logits_in_psum, 1)
                go_up(b, 0)
                for e in range(EXPERTS):
                    if e + 1 < EXPERTS:
                        if not gated and e + 1 >= 2:
                            pass
                        go_up(b, e + 1)
                    if e == 0 and not gated:
                        pe.wait_ge(onehot_ready, b + 1)
                        for t in range(HALVES):
                            last = pe.transpose(c.bank[7][0:EXPERTS, t * P:(t + 1) * P], best1[:, t, :],
                                                c.ident[:, :])
                        last.then_inc(onehotT_in_psum, 1)
                        pe.wait_ge(onehotT_ready, b + 1)
                        for t in range(HALVES):
                            last = pe.matmul(c.bank[7][:, S + t * D:S + (t + 1) * D],
                                             c.onehotT[:, t * P:(t + 1) * P], c.bottom[:, :], start=True, stop=True)
                        last.then_inc(bias_in_psum, 1)
                    go_down(b, e)

        @block.gpsimd
        def _(g):
            with g.Fori(0, B) as b:
                norm.pool(g, b)

        @block.scalar
        def _(a):
            a.wait_ge(loaded, all_loaded)
            a.activation(c.cols[:, 30:31], c.neg_half[:, 0:1], ACT.Silu if gated else ACT.Relu)
            with a.Fori(0, B) as b:
                norm.scalar(a, b)
                if gated:
                    a.wait_ge(gap_ready, b + 1)
                    a.activation(top[:, 3, :], top[:, 2, :], ACT.Tanh, scale=0.5).then_inc(share_ready, 1)
                for e in range(EXPERTS):
                    a.wait_ge(up_in_psum, b * EXPERTS + e + 1)
                    if gated:
                        if e >= 2:
                            a.wait_ge(hidden_ready, b * EXPERTS + e - 1)
                        a.activation(c.sq[:, e % 2, :], c.bank[2 * (e % 2)][:, :], ACT.Silu).then_inc(act_ready, 1)
                    else:
                        if e >= 2:
                            a.wait_ge(down_in_psum, b * EXPERTS + e - 1)
                        for k in range(chunks):
                            last = a.activation(hidden[:, e % 2, k * S:(k + 1) * S],
                                                c.bank[2 * (e % 2) + k // 2][:, (k % 2) * S:(k % 2) * S + S],
                                                ACT.Relu, bias=c.colsA[:, e * chunks + k:e * chunks + k + 1])
                        last.then_inc(hidden_ready, 1)

        @block.vector
        def _(v):
            v.wait_ge(loaded, all_loaded)

            def hottest(step, src, top_k, dst):
                step.after(v.tensor_reduce(top_k, src, AX, ALU.max))
                step.after(v.tensor_tensor(equal, src, over(top_k), ALU.is_equal))
                step.after(v.scalar_tensor_tensor(out=cand, in0=equal, scalar=-float(EXPERTS), in1=c.iota8[:, :, :],
                                                  op0=ALU.mult, op1=ALU.add))
                step.after(v.tensor_reduce(top[:, 5, :], cand, AX, ALU.min))
                step.after(v.tensor_tensor(dst, cand, over(top[:, 5, :]), ALU.is_equal))

            with v.Fori(0, B) as b:
                step = Steps(v, step_v, b, STEPS_GATED if gated else STEPS_PLAIN)
                norm.vector(v, b, step)
                v.wait_ge(logits_in_psum, b + 1)
                psum = c.bank[7][:, 0:HALVES * EXPERTS].rearrange("p (t e) -> p t e", t=HALVES)
                if gated:
                    step.after(v.tensor_copy(logits, psum))
                    hottest(step, logits, top[:, 0, :], best1)
                    step.after(v.scalar_tensor_tensor(out=rest, in0=best1, scalar=MASKED, in1=logits, op0=ALU.mult,
                                                      op1=ALU.add))
                    hottest(step, rest, top[:, 1, :], best2)
                    v.tensor_tensor(top[:, 2, :], top[:, 0, :], top[:, 1, :], ALU.subtract).then_inc(gap_ready, 1)
                    v.wait_ge(share_ready, b + 1)
                    step.after(v.tensor_scalar(top[:, 4, :], top[:, 3, :], 0.5, 0.5, ALU.mult, ALU.add))
                    step.after(v.tensor_scalar(top[:, 5, :], top[:, 3, :], -0.5, 0.5, ALU.mult, ALU.add))
                    step.after(v.tensor_tensor(weight, best1, over(top[:, 4, :]), ALU.mult))
                    step.after(v.tensor_tensor(tmp, best2, over(top[:, 5, :]), ALU.mult))
                    step.after(v.tensor_tensor(weight, weight, tmp, ALU.add))
                    share = weight
                else:
                    step.after(v.tensor_tensor(logits, psum, c.rows[:, 0, 0:EXPERTS].unsqueeze(1)
                                               .broadcast_to((P, HALVES, EXPERTS)), ALU.add))
                    hottest(step, logits, top[:, 0, :], best1)
                    last = v.memset(top[:, 1, 0:1], 0.0)
                    last.then_inc(onehot_ready, 1)
                    v.wait_ge(onehotT_in_psum, b + 1)
                    v.tensor_copy(c.onehotT[:, :], c.bank[7][0:EXPERTS, 0:S]).then_inc(onehotT_ready, 1)
                    share = best1

                def gather(e):
                    v.wait_ge(down_in_psum, b * EXPERTS + e + 1)
                    src = c.bank[4 + e % 2]
                    for t in range(HALVES):
                        part, acc = src[:, t * D:(t + 1) * D], c.ctx[:, t, 0:D]
                        if e == 0:
                            last = v.tensor_scalar(acc, part, share[:, t, e:e + 1], None, ALU.mult)
                        else:
                            last = v.scalar_tensor_tensor(out=acc, in0=part, scalar=share[:, t, e:e + 1], in1=acc,
                                                          op0=ALU.mult, op1=ALU.add)
                    last.then_inc(acc_done, 1)
                    v.wait_ge(acc_done, b * EXPERTS + e + 1)

                for e in range(EXPERTS):
                    if gated:
                        v.wait_ge(act_ready, b * EXPERTS + e + 1)
                        if e >= 2:
                            v.wait_ge(down_in_psum, b * EXPERTS + e - 1)
                        v.tensor_tensor(hidden[:, e % 2, :], c.sq[:, e % 2, :], c.bank[2 * (e % 2) + 1][:, :],
                                        ALU.mult).then_inc(hidden_ready, 1)
                    if e >= 1:
                        gather(e - 1)
                gather(EXPERTS - 1)
                halves = x[:, row(b)].rearrange("p (t d) -> p t d", t=HALVES)
                step.after(v.tensor_tensor(halves, halves, c.ctx[:, :, 0:D], ALU.add))
                if not gated:
                    v.wait_ge(bias_in_psum, b + 1)
                    step.after(v.tensor_tensor(x[:, row(b)], x[:, row(b)], c.bank[7][:, S:2 * S], ALU.add))
                step.end()


STEPS_GATED = LN_STEPS + 1 + 5 + 1 + 5 + 5 + 1
STEPS_PLAIN = LN_STEPS + 1 + 5 + 2




def linear_attention(nc, sem, c, name, io, x):
    w = io[name]
    norm = Norm(c, x)
    loaded, step_v = sem(name + "_weights"), sem(name + "_steps")
    proj_in_psum, low_ready, exp_ready, feat_ready = [sem(name + "_" + s) for s in
                                                      ("proj_in_psum", "low_ready", "exp_ready", "feat_ready")]
    kv_in_psum, kv_ready, out_in_psum, ctx_ready = [sem(name + "_" + s) for s in
                                                    ("kv_in_psum", "kv_ready", "num_in_psum", "ctx_ready")]
    ctxT_in_psum, ctxT_ready, proj2_in_psum = [sem(name + "_" + s) for s in
                                               ("ctxT_in_psum", "ctxT_ready", "out_in_psum")]
    wq, wkv, wp = c.wA[:, 0:D], c.wA[:, D:3 * D], c.wA[:, 3 * D:4 * D]
    qf, kf = c.turnA[:, 0, 0:S], c.turnA[:, 1, 0:S]
    lowq, lowk = c.turnB[:, 0, 0:S], c.turnB[:, 1, 0:S]
    expq, expk = c.sq[:, 0, 0:S], c.sq[:, 1, 0:S]
    with nc.Block() as block:

        @block.sync
        def _(sp):
            for dst, src in ((wq, w["wq"]), (wkv, w["wkv"]), (wp, w["wp"]),
                             (c.rows[:, 0, :], w["bp"].partition_broadcast(P))):
                sp.dma_start(dst, src).then_inc(loaded, 16)
            sp.wait_ge(loaded, 64)

        @block.tensor
        def _(pe):
            pe.wait_ge(loaded, 64)
            with pe.Fori(0, B) as b:
                norm.tensor(pe, b)
                pe.matmul(c.bank[0][:, 0:S], wq, c.xT[:, :], start=True, stop=True)
                for t in range(HALVES):
                    last = pe.matmul(c.bank[1 + t][:, 0:2 * D], c.xT[:, t * P:(t + 1) * P], wkv, start=True, stop=True)
                last.then_inc(proj_in_psum, 1)
                pe.wait_ge(feat_ready, b + 1)
                for t in range(HALVES):
                    last = pe.matmul(c.bank[3][:, 0:D + 1], kf[:, t * D:(t + 1) * D], c.v1[:, t, 0:D + 1],
                                     start=(t == 0), stop=(t == 1))
                last.then_inc(kv_in_psum, 1)
                pe.wait_ge(kv_ready, b + 1)
                for t in range(HALVES):
                    last = pe.matmul(c.bank[4][:, t * (D + NH):(t + 1) * (D + NH)], qf[:, t * P:(t + 1) * P],
                                     c.kvblock[:, :], start=True, stop=True)
                last.then_inc(out_in_psum, 1)
                pe.wait_ge(ctx_ready, b + 1)
                for t in range(HALVES):
                    last = pe.transpose(c.bank[6][:, t * P:(t + 1) * P], c.ctx[:, t, 0:D], c.ident[:, :])
                last.then_inc(ctxT_in_psum, 1)
                pe.wait_ge(ctxT_ready, b + 1)
                for t in range(HALVES):
                    last = pe.matmul(c.bank[7][:, t * D:(t + 1) * D], c.ctxT[:, 0, t * P:(t + 1) * P], wp, start=True,
                                     stop=True)
                last.then_inc(proj2_in_psum, 1)

        @block.gpsimd
        def _(g):
            with g.Fori(0, B) as b:
                norm.pool(g, b)

        @block.scalar
        def _(a):
            a.activation(c.cols[:, 30:31], c.neg_half[:, 0:1], ACT.Exp)
            with a.Fori(0, B) as b:
                norm.scalar(a, b)
                a.wait_ge(low_ready, b + 1)
                a.activation(expq, lowq, ACT.Exp)
                a.activation(expk, lowk, ACT.Exp).then_inc(exp_ready, 1)
                a.wait_ge(ctxT_in_psum, b + 1)
                a.activation(c.ctxT[:, 0, :], c.bank[6][:, 0:S], ACT.Identity).then_inc(ctxT_ready, 1)

        @block.vector
        def _(v):
            v.wait_ge(loaded, 64)
            with v.Fori(0, B) as b:
                step = Steps(v, step_v, b, LN_STEPS + 3)
                norm.vector(v, b, step)
                v.wait_ge(proj_in_psum, b + 1)
                v.tensor_scalar(lowq, c.bank[0][:, 0:S], 0.0, None, ALU.min)
                for t in range(HALVES):
                    last = v.tensor_scalar(lowk[:, t * D:(t + 1) * D], c.bank[1 + t][:, 0:D], 0.0, None, ALU.min)
                last.then_inc(low_ready, 1)
                for t in range(HALVES):
                    v.tensor_copy(c.v1[:, t, 0:D], c.bank[1 + t][:, D:2 * D])
                v.wait_ge(exp_ready, b + 1)
                v.scalar_tensor_tensor(out=qf, in0=c.bank[0][:, 0:S], scalar=0.0, in1=expq, op0=ALU.max, op1=ALU.add)
                for t in range(HALVES):
                    last = v.scalar_tensor_tensor(out=kf[:, t * D:(t + 1) * D], in0=c.bank[1 + t][:, 0:D], scalar=0.0,
                                                  in1=expk[:, t * D:(t + 1) * D], op0=ALU.max, op1=ALU.add)
                last.then_inc(feat_ready, 1)
                v.wait_ge(kv_in_psum, b + 1)
                v.tensor_tensor(c.kvblock[:, 0:D], c.bank[3][:, 0:D], c.headmask[:, :], ALU.mult)
                v.tensor_scalar(c.kvblock[:, D:D + NH], c.headcol[:, :], c.bank[3][:, D:D + 1], None,
                                ALU.mult).then_inc(kv_ready, 1)
                v.wait_ge(out_in_psum, b + 1)
                num = c.bank[4][:, 0:HALVES * (D + NH)].rearrange("p (t n) -> p t n", t=HALVES)
                den = c.recip[:, 0, 0:HALVES * NH].rearrange("p (t h) -> p t h", t=HALVES)
                step.after(v.tensor_scalar(den, num[:, :, D:D + NH], 1e-6, None, ALU.add))
                step.after(v.reciprocal(den, den))
                for t in range(HALVES):
                    last = v.tensor_tensor(c.ctx[:, t, 0:D].rearrange("p (h d) -> p h d", h=NH),
                                           num[:, t, 0:D].rearrange("p (h d) -> p h d", h=NH),
                                           den[:, t, :].unsqueeze(2).broadcast_to((P, NH, HD)), ALU.mult)
                last.then_inc(ctx_ready, 1)
                v.wait_ge(proj2_in_psum, b + 1)
                add_rows(v, step, x, b, c.bank[7][:, 0:S], c.rows[:, 0, :])
                step.end()




def rotary_attention(nc, sem, c, name, io, x):
    w = io[name]
    norm = Norm(c, x)
    core = Core(c, 1, causal_blocks(c), lambda h: (c.qT[:, 0, :], c.kT[:, 0, :]),
                lambda h, kt: c.v1[:, kt, 0:D + 1], D + 1, 1, "wide_head")
    loaded, step_v = sem(name + "_weights"), sem(name + "_steps")
    proj_in_psum, v_copied, qk_rotated, qkT_in_psum = [sem(name + "_" + s) for s in
                                                       ("proj_in_psum", "v_copied", "qk_rotated", "qkT_in_psum")]
    wqkv = c.wA[:, 0:3 * D]
    with nc.Block() as block:

        @block.sync
        def _(sp):
            sp.dma_start(wqkv, w["wqkv"]).then_inc(loaded, 16)
            sp.dma_start(c.rope[:, 0:2, :, :], w["rope"]).then_inc(loaded, 16)
            sp.wait_ge(loaded, 32)

        @block.tensor
        def _(pe):
            pe.wait_ge(loaded, 32)
            with pe.Fori(0, B) as b:
                norm.tensor(pe, b)
                for t in range(HALVES):
                    last = pe.matmul(c.bank[t][:, 0:3 * D], c.xT[:, t * P:(t + 1) * P], wqkv, start=True, stop=True)
                last.then_inc(proj_in_psum, 1)
                pe.wait_ge(qk_rotated, b + 1)
                for which in range(2):
                    for t in range(HALVES):
                        last = pe.transpose(c.bank[7][:, which * S + t * P:which * S + (t + 1) * P],
                                            c.qk[:, t, 0, which * D:(which + 1) * D], c.ident[:, :])
                last.then_inc(qkT_in_psum, 1)
                core.tensor(pe, b)

        @block.gpsimd
        def _(g):
            with g.Fori(0, B) as b:
                norm.pool(g, b)

        @block.scalar
        def _(a):
            a.activation(c.cols[:, 30:31], c.neg_half[:, 0:1], ACT.Exp)
            with a.Fori(0, B) as b:
                norm.scalar(a, b)
                a.wait_ge(proj_in_psum, b + 1)
                for t in range(HALVES):
                    last = a.activation(c.v1[:, t, 0:D], c.bank[t][:, 2 * D:3 * D], ACT.Identity)
                last.then_inc(v_copied, 1)
                a.wait_ge(qkT_in_psum, b + 1)
                a.activation(c.qT[:, 0, :], c.bank[7][:, 0:S], ACT.Identity, scale=float(D) ** -0.5)
                a.activation(c.kT[:, 0, :], c.bank[7][:, S:2 * S], ACT.Identity).then_inc(core.qk_ready, 1)
                core.scalar(a, b)

        @block.vector
        def _(v):
            v.wait_ge(loaded, 32)
            with v.Fori(0, B) as b:
                step = Steps(v, step_v, b, LN_STEPS + 1)
                norm.vector(v, b, step)
                v.wait_ge(v_copied, b + 1)
                for t in range(HALVES):
                    src = c.bank[t][:, 0:2 * D].rearrange("p (n d) -> p n d", n=2)
                    last = rotate(v, src, c.turnA[:, t, 0:2 * D], c.turnB[:, t, 0:2 * D], 2, D,
                                  c.rope[:, 0, t, :], c.rope[:, 1, t, :])
                step.after(last)
                for t in range(HALVES):
                    last = v.tensor_tensor(c.qk[:, t, 0, 0:2 * D], c.turnA[:, t, 0:2 * D], c.turnB[:, t, 0:2 * D],
                                           ALU.add)
                last.then_inc(qk_rotated, 1)
                core.vector(v, b)
                v.wait_ge(core.ctx_ready, core.before + b + 1)
                halves = x[:, row(b)].rearrange("p (t d) -> p t d", t=HALVES)
                v.tensor_tensor(halves, halves, c.ctx[:, :, 0:D], ALU.add)
                step.end()


def rotate(v, src, straight, crossed, n, width, cos, sin):
    h = width // 2
    straight = straight.rearrange("p (n d) -> p n d", n=n)
    crossed = crossed.rearrange("p (n d) -> p n d", n=n)

    def each(t):
        return t.unsqueeze(1).broadcast_to((P, n, t.shape[-1]))

    v.tensor_tensor(straight, src, each(cos), ALU.mult)
    v.tensor_tensor(crossed[:, :, 0:h], src[:, :, h:width], each(sin[:, 0:h]), ALU.mult)
    return v.tensor_tensor(crossed[:, :, h:width], src[:, :, 0:h], each(sin[:, h:width]), ALU.mult)




def latent_attention(nc, sem, c, name, io, x):
    w = io[name]
    norm = Norm(c, x)
    core = Core(c, NH, causal_blocks(c),
                lambda h: (c.qT[32 * (h % 4):32 * (h % 4) + 32, h // 4, :], c.kT[32 * (h % 4):32 * (h % 4) + 32, h // 4, :]),
                lambda h, kt: c.V[:, kt, h, DH - HD:DH + 1], HD + 1, NH, "heads")
    loaded, step_v, pads_zero = sem(name + "_weights"), sem(name + "_steps"), sem(name + "_pads_zero")
    products_in_psum, value_ready, value_in_psum, blocks_ready = [sem(name + "_" + s) for s in (
        "products_in_psum", "value_ready", "value_in_psum", "blocks_ready")]
    proj_in_psum, squared, normed, qkT_in_psum = [sem(name + "_" + s) for s in
                                                  ("proj_in_psum", "squared", "qk_normed", "qkT_in_psum")]
    blocks = c.wB[:, 0:4 * D]
    tiles = c.wA[:, 0:10 * D].rearrange("p (n d) -> p n d", n=10)
    pads = c.qk[:, :, :, 0:512].rearrange("p t w (h e) -> p t w h e", h=NH)
    with nc.Block() as block:

        @block.sync
        def _(sp):
            for dst, src in ((tiles[:, :, :], w["tiles"]), (c.rows[:, 0, 0:2 * HD], w["norms"].partition_broadcast(P))):
                sp.dma_start(dst, src).then_inc(loaded, 16)
            sp.wait_ge(loaded, 32)

        @block.tensor
        def _(pe):
            pe.wait_ge(loaded, 32)
            pe.matmul(c.bank[0][:, 0:D], tiles[0:DH, 0, :], tiles[0:DH, 1, :], start=True, stop=True)
            pe.matmul(c.bank[0][:, D:2 * D], tiles[:, 2, :], tiles[:, 3, :], start=True, stop=True)
            pe.matmul(c.bank[0][:, 2 * D:3 * D], tiles[0:DH, 4, :], tiles[0:DH, 5, :], start=True, stop=True)
            pe.matmul(c.bank[0][:, 3 * D:4 * D], tiles[:, 6, :], tiles[:, 2, :], start=True,
                      stop=True).then_inc(products_in_psum, 1)
            pe.wait_ge(value_ready, 1)
            pe.matmul(c.bank[1][:, 0:D], tiles[:, 8, :], tiles[:, 7, :], start=True,
                      stop=True).then_inc(value_in_psum, 1)
            pe.wait_ge(blocks_ready, 1)
            with pe.Fori(0, B) as b:
                norm.tensor(pe, b)
                for t in range(HALVES):
                    last = pe.matmul(c.bank[t][:, :], c.xT[:, t * P:(t + 1) * P], blocks, start=True, stop=True)
                last.then_inc(proj_in_psum, 1)
                pe.wait_ge(normed, b + 1)
                for which in range(2):
                    for g in range(GROUPS):
                        for t in range(HALVES):
                            o = ((g % 2) * HALVES + t) * P
                            last = pe.transpose(c.bank[2 + 2 * which + g // 2][:, o:o + P],
                                                c.qk[:, t, which, g * P:(g + 1) * P], c.ident[:, :])
                last.then_inc(qkT_in_psum, 1)
                core.tensor(pe, b)

        @block.gpsimd
        def _(g):
            with g.Fori(0, B) as b:
                norm.pool(g, b)

        @block.scalar
        def _(a):
            a.activation(c.cols[:, 30:31], c.neg_half[:, 0:1], ACT.Exp)
            with a.Fori(0, B) as b:
                norm.scalar(a, b)
                a.wait_ge(proj_in_psum, b + 1)
                for t in range(HALVES):
                    last = a.activation(c.sq[:, t, 0:2 * D], c.bank[t][:, 0:2 * D], ACT.Square)
                last.then_inc(squared, 1)
                a.wait_ge(qkT_in_psum, b + 1)
                for g in range(2):
                    a.activation(c.qT[:, 2 * g:2 * g + 2, :].rearrange("p g s -> p (g s)"), c.bank[2 + g][:, :],
                                 ACT.Identity, scale=float(HD) ** -0.5)
                for g in range(2):
                    last = a.activation(c.kT[:, 2 * g:2 * g + 2, :].rearrange("p g s -> p (g s)"), c.bank[4 + g][:, :],
                                        ACT.Identity)
                last.then_inc(core.qk_ready, 1)
                core.scalar(a, b)

        @block.vector
        def _(v):
            v.wait_ge(loaded, 32)
            v.memset(c.qk[:, :, :, :], 0.0)
            v.wait_ge(products_in_psum, 1)
            v.tensor_tensor(tiles[:, 8, :], c.bank[0][:, 3 * D:4 * D], c.headmask[:, :],
                            ALU.mult).then_inc(value_ready, 1)
            v.tensor_tensor(blocks[:, 0:3 * D].rearrange("p (n d) -> p n d", n=3),
                            c.bank[0][:, 0:3 * D].rearrange("p (n d) -> p n d", n=3),
                            c.headmask[:, :].unsqueeze(1).broadcast_to((P, 3, D)), ALU.mult)
            v.wait_ge(value_in_psum, 1)
            v.tensor_tensor(blocks[:, 3 * D:4 * D], c.bank[1][:, 0:D], c.headmask[:, :],
                            ALU.mult).then_inc(blocks_ready, 1)
            with v.Fori(0, B) as b:
                step = Steps(v, step_v, b, LN_STEPS + 1 + 1 + NEWTON_STEPS + 2 + 1)
                norm.vector(v, b, step)
                v.wait_ge(squared, b + 1)
                for t in range(HALVES):
                    last = v.tensor_reduce(c.ss[:, t, :], c.sq[:, t, 0:2 * D].rearrange("p (h d) -> p h d", d=HD), AX,
                                           ALU.add)
                step.after(last)
                ss = c.ss[:, :, :].rearrange("p t h -> p (t h)")
                step.after(v.tensor_scalar(ss, ss, 1.0 / HD, RMS_EPS, ALU.mult, ALU.add))
                rsqrt(v, step, c, ss, c.rs[:, 0, :, :].rearrange("p t h -> p (t h)"))
                for t in range(HALVES):
                    last = v.tensor_tensor(c.turnA[:, t, 0:2 * D].rearrange("p (h d) -> p h d", d=HD),
                                           c.bank[t][:, 0:2 * D].rearrange("p (h d) -> p h d", d=HD),
                                           c.rs[:, 0, t, :].unsqueeze(2).broadcast_to((P, 2 * NH, HD)), ALU.mult)
                step.after(last)
                for t in range(HALVES):
                    for which in range(2):
                        src = c.turnA[:, t, which * D:(which + 1) * D].rearrange("p (h d) -> p h d", d=HD)
                        dst = pads[:, t, 0, :, 0:HD] if which == 0 else src
                        last = v.tensor_tensor(dst, src, c.rows[:, 0, which * HD:(which + 1) * HD].unsqueeze(1)
                                               .broadcast_to((P, NH, HD)), ALU.mult)
                step.after(last)
                for t in range(HALVES):
                    v.tensor_tensor(pads[:, t, 1, :, 0:HD],
                                    c.turnA[:, t, D:2 * D].rearrange("p (h d) -> p h d", d=HD),
                                    c.bank[t][:, 2 * D:3 * D].rearrange("p (h d) -> p h d", d=HD), ALU.add)
                    last = v.tensor_copy(c.V[:, t, :, DH - HD:DH],
                                         c.bank[t][:, 3 * D:4 * D].rearrange("p (h d) -> p h d", d=HD))
                last.then_inc(normed, 1)
                core.vector(v, b)
                v.wait_ge(core.ctx_ready, core.before + b + 1)
                halves = x[:, row(b)].rearrange("p (t d) -> p t d", t=HALVES)
                step.after(v.tensor_tensor(halves, halves, c.ctx[:, :, 0:D], ALU.add))
                step.end()




def norm_rows(nc, c):
    (var_ready, rstd_ready, step_v), before = c.shared.take("rows", ("var_ready", "rstd_ready", "steps"), B)
    with nc.Block() as block:

        @block.gpsimd
        def _(g):
            with g.Fori(0, B) as b:
                g.wait_ge(var_ready, before + b + 1)
                g.tensor_tensor(c.rstd[:, 0:HALVES], c.vareps[:, 0:HALVES], c.neg_half[:, 0:HALVES],
                                ALU.pow).then_inc(rstd_ready, 1)

        @block.vector
        def _(v):
            with v.Fori(0, B) as b:
                step = Steps(v, step_v, before + b, LN_STEPS)
                for t in range(HALVES):
                    last = v.bn_stats(c.stats[:, t, :], c.X[:, half(b, t)])
                step.after(last)
                v.memset(c.vareps[:, 30:31], 0.0)
                for t in range(HALVES):
                    last = v.bn_aggr(c.mv[:, t, :], c.stats[:, t, :])
                step.after(last)
                v.tensor_scalar(c.vareps[:, 0:HALVES], c.mv[:, :, 1], LN_EPS, None, ALU.add).then_inc(var_ready, 1)
                v.wait_ge(rstd_ready, before + b + 1)
                for t in range(HALVES):
                    v.tensor_scalar(c.Y[:, half(b, t)], c.X[:, half(b, t)], c.mv[:, t, 0:1], c.rstd[:, t:t + 1],
                                    ALU.subtract, ALU.mult)
                step.end()


def add_back(nc, c):
    with nc.Block() as block:

        @block.vector
        def _(v):
            v.tensor_tensor(c.X[:, :], c.X[:, :], c.Y[:, :], ALU.add)




QK_CHUNKS = 4
CHUNKS = 3 * INNER // 512


def windowed_transformers(nc, sem, c, name, io):
    w = io[name]
    band = [[(0, 0, P, (c.band0[:, :], 0))], [(0, P - WINDOW, WINDOW, (c.band1[:, :], 0)), (1, 0, P, None)]]
    core = Core(c, NH, band,
                lambda h: (c.qT[DH * (h % 2):DH * (h % 2) + DH, h // 2, :], c.kT[DH * (h % 2):DH * (h % 2) + DH, h // 2, :]),
                lambda h, kt: c.V[:, kt, h, :], DH + 1, 2, "window_heads", 0)
    names = ("attn_weights", "ff_weights", "attn_added", "ff_added", "steps", "row_copied", "rowT_in_psum",
             "xT_ready", "chunk_in_psum", "chunk_read", "chunk_rotated", "sum_ready", "rs_ready", "first_half_scaled",
             "second_half_scaled", "qkT_in_psum", "qkT_by_scalar", "qkT_by_vector", "ctxT_in_psum", "ctxT_by_scalar",
             "ctxT_by_vector", "out_in_psum", "shifted_in_psum", "shifted_ready", "kept_ready", "ff_in_psum",
             "gelu_ready", "hidden_ready", "ff_out_in_psum", "tables_ready")
    s = Chip()
    (s.attn_weights, s.ff_weights, s.attn_added, s.ff_added, s.steps, s.row_copied, s.rowT_in_psum, s.xT_ready,
     s.chunk_in_psum, s.chunk_read, s.chunk_rotated, s.sum_ready, s.rs_ready, s.first_half_scaled,
     s.second_half_scaled, s.qkT_in_psum, s.qkT_by_scalar, s.qkT_by_vector, s.ctxT_in_psum, s.ctxT_by_scalar,
     s.ctxT_by_vector, s.out_in_psum, s.shifted_in_psum, s.shifted_ready, s.kept_ready, s.ff_in_psum, s.gelu_ready,
     s.hidden_ready, s.ff_out_in_psum, s.tables_ready) = [sem(name + "_" + n) for n in names]
    ff_norm = Norm(c, None, (c.cols[:, 0:1], c.cols[:, 1:2]), "window_norm", 0)
    ff_steps = sem(name + "_ff_steps")
    wqkv, wo = c.wA[:, :], c.wB[:, :]
    w1, w2 = c.wC[:, :], c.wD[:, :]
    n_attn, n_ff = 16 * 3, 16 * 3
    chunk_bank = 6
    tables_loaded = sem(name + "_tables_loaded")

    def scale_half(eng, t):
        both = c.qk[:, t, :, :].rearrange("p w (h d) -> p (w h) d", d=DH)
        return eng.tensor_tensor(both, both, c.rs[:, 0, t, :].unsqueeze(2).broadcast_to((P, 2 * NH, DH)), ALU.mult)

    def copy_to(which, pp):
        return (c.qT, c.kT)[which][:, 2 * pp:2 * pp + 2, :].rearrange("p k s -> p (k s)")

    def run(number):
        layer0, layer1 = number * DEPTH, (number + 1) * DEPTH
        with nc.Block() as block:

            @block.sync
            def _(sp):
                sp.dma_start(c.rope[:, :, :, 0:DH], w["rope"]).then_inc(tables_loaded, 16)
                with sp.Fori(layer0, layer1) as d:
                    sp.wait_ge(s.attn_added, d * B + 1)
                    sp.dma_start(wqkv, w["wqkv"][bass.ds(d, 1)].rearrange("a p n -> (a p) n")).then_inc(s.attn_weights, 16)
                    sp.dma_start(wo, w["wo"][bass.ds(d, 1)].rearrange("a p n -> (a p) n")).then_inc(s.attn_weights, 16)
                    sp.dma_start(c.scl[:, :, :].rearrange("p a b -> p (a b)"),
                                 w["scales"][bass.ds(d, 1)].rearrange("a n -> (a n)").partition_broadcast(P)).then_inc(s.attn_weights, 16)
                    sp.wait_ge(s.ff_added, d * B + 1)
                    sp.dma_start(w1, w["w1"][bass.ds(d, 1)].rearrange("a p n -> (a p) n")).then_inc(s.ff_weights, 16)
                    sp.dma_start(w2, w["w2"][bass.ds(d, 1)].rearrange("a p n -> (a p) n")).then_inc(s.ff_weights, 16)
                    sp.dma_start(c.cols[:, 0:8], w["cols"][bass.ds(d, 1)].rearrange("a p n -> (a p) n")).then_inc(s.ff_weights, 16)
                sp.wait_ge(s.attn_weights, n_attn * layer1)
                sp.wait_ge(s.ff_weights, n_ff * layer1)

            @block.tensor
            def _(pe):
                with pe.Fori(layer0, layer1) as d:
                    with pe.Fori(0, B) as b:
                        turn = d * B + b
                        pe.wait_ge(s.attn_weights, d * n_attn + n_attn)
                        pe.wait_ge(s.row_copied, turn + 1)
                        for t in range(HALVES):
                            last = pe.transpose(c.bank[6][:, t * P:(t + 1) * P], c.xn[:, t, :], c.ident[:, :])
                        last.then_inc(s.rowT_in_psum, 1)
                        pe.wait_ge(s.xT_ready, turn + 1)
                        for n in range(HALVES * CHUNKS):
                            t, k = divmod(n, CHUNKS)
                            if n >= chunk_bank:
                                t0, k0 = divmod(n - chunk_bank, CHUNKS)
                                pe.wait_ge(s.chunk_read, turn * HALVES * CHUNKS + n - chunk_bank + 1)
                                if k0 < QK_CHUNKS:
                                    pe.wait_ge(s.chunk_rotated, turn * HALVES * QK_CHUNKS + t0 * QK_CHUNKS + k0 + 1)
                            pe.matmul(c.bank[n % chunk_bank][:, :], c.xT[:, t * P:(t + 1) * P],
                                      wqkv[:, k * 512:(k + 1) * 512], start=True, stop=True).then_inc(s.chunk_in_psum, 1)
                        pe.wait_ge(s.first_half_scaled, turn + 1)
                        pe.wait_ge(s.second_half_scaled, turn + 1)
                        pe.wait_ge(s.chunk_read, (turn + 1) * HALVES * CHUNKS)
                        for i in range(8):
                            which, pp = divmod(i, 4)
                            if i >= 6:
                                pe.wait_ge((s.qkT_by_scalar, s.qkT_by_vector)[i % 2], turn * 4 + (i - 6) // 2 + 1)
                            for j in range(2):
                                for t in range(HALVES):
                                    at = (2 * pp + j) * P
                                    last = pe.transpose(c.bank[i % 6][:, (2 * j + t) * P:(2 * j + t + 1) * P],
                                                        c.qk[:, t, which, at:at + P], c.ident[:, :])
                            last.then_inc(s.qkT_in_psum, 1)
                        pe.wait_ge(s.qkT_by_scalar, (turn + 1) * 4)
                        pe.wait_ge(s.qkT_by_vector, (turn + 1) * 4)
                        core.tensor(pe, turn)
                        pe.wait_ge(core.ctx_ready, (turn + 1) * core.n_ctx)
                        for i in range(4):
                            for j in range(2):
                                for t in range(HALVES):
                                    at = (2 * i + j) * P
                                    last = pe.transpose(c.bank[i][:, (2 * j + t) * P:(2 * j + t + 1) * P],
                                                        c.ctx[:, t, at:at + P], c.ident[:, :])
                            last.then_inc(s.ctxT_in_psum, 1)
                        pe.wait_ge(s.ctxT_by_scalar, (turn + 1) * 2)
                        pe.wait_ge(s.ctxT_by_vector, (turn + 1) * 2)
                        for t in range(HALVES):
                            for k in range(8):
                                last = pe.matmul(c.bank[7][:, t * D:(t + 1) * D], c.ctxT[:, k, t * P:(t + 1) * P],
                                                 wo[:, k * D:(k + 1) * D], start=(k == 0), stop=(k == 7))
                        last.then_inc(s.out_in_psum, 1)
                    with pe.Fori(0, B) as b:
                        turn = d * B + b
                        pe.wait_ge(s.ff_weights, d * n_ff + n_ff)
                        pe.wait_ge(s.attn_added, turn + 2)
                        hi = D // 2
                        for t in range(HALVES):
                            last = pe.matmul(c.bank[6][:, t * hi:(t + 1) * hi], c.shift[:, :],
                                             c.Y[:, bass.ds(b * ROW + t * D + hi, hi)], start=True, stop=(t == 0))
                            if t == 1:
                                last = pe.matmul(c.bank[6][:, t * hi:(t + 1) * hi], c.carry[:, :],
                                                 c.Y[:, bass.ds(b * ROW + hi, hi)], start=False, stop=True)
                        last.then_inc(s.shifted_in_psum, 1)
                        ff_norm.tensor(pe, turn)
                        for k, (at, n) in enumerate(FF_CHUNKS):
                            for side in range(2):
                                last = pe.matmul(c.bank[k][0:n, side * S:(side + 1) * S],
                                                 w1[:, side * FF + at:side * FF + at + n], c.xT[:, :], start=True, stop=True)
                            last.then_inc(s.ff_in_psum, 1)
                        pe.wait_ge(s.hidden_ready, (turn + 1) * 3)
                        for t in range(HALVES):
                            for k, (at, n) in enumerate(FF_CHUNKS):
                                m = n + (k == 2)
                                last = pe.matmul(c.bank[7][:, t * D:(t + 1) * D], c.hT[0:m, k, t * P:(t + 1) * P],
                                                 w2[0:m, k * D:(k + 1) * D], start=(k == 0), stop=(k == 2))
                        last.then_inc(s.ff_out_in_psum, 1)

            @block.gpsimd
            def _(g):
                with g.Fori(layer0, layer1) as d:
                    with g.Fori(0, B) as b:
                        turn = d * B + b
                        g.wait_ge(s.ff_added, d * B + 1)
                        g.wait_ge(s.attn_added, turn + 1)
                        g.tensor_copy(c.xn[:, :, :].rearrange("p t d -> p (t d)"), c.Y[:, row(b)]).then_inc(s.row_copied, 1)
                        for m in range(HALVES * QK_CHUNKS):
                            t, k = divmod(m, QK_CHUNKS)
                            g.wait_ge(s.chunk_rotated, turn * HALVES * QK_CHUNKS + m + 1)
                            g.tensor_tensor(c.qk[:, t, k // 2, (k % 2) * 512:(k % 2) * 512 + 512], c.turnA[:, m % 2, :],
                                            c.turnB[:, m % 2, :], ALU.add).then_inc(s.sum_ready, 1)
                        g.wait_ge(s.rs_ready, turn + 1)
                        g.wait_ge(s.sum_ready, (turn + 1) * HALVES * QK_CHUNKS)
                        scale_half(g, 0).then_inc(s.first_half_scaled, 1)
                    with g.Fori(0, B) as b:
                        turn = d * B + b
                        g.wait_ge(s.attn_added, turn + 2)
                        g.wait_ge(s.ff_added, turn + 1)
                        hi = D // 2
                        g.tensor_copy(c.xn[:, :, 0:hi],
                                      c.Y[:, row(b)].rearrange("p (t d) -> p t d", t=HALVES)[:, :, 0:hi]).then_inc(s.kept_ready, 1)
                        ff_norm.pool(g, turn)

            @block.scalar
            def _(a):
                hi = D // 2
                with a.Fori(layer0, layer1) as d:
                    a.activation(c.cols[:, 30:31], c.neg_half[:, 0:1], ACT.Exp)
                    with a.Fori(0, B) as b:
                        turn = d * B + b
                        a.wait_ge(s.rowT_in_psum, turn + 1)
                        a.activation(c.xT[0:hi, :], c.bank[6][0:hi, 0:S], ACT.Identity)
                        a.activation(c.xT[hi:D, 0:1], c.bank[6][hi:D, 0:1], ACT.Copy, scale=0.0)
                        a.activation(c.xT[hi:D, 1:S], c.bank[6][hi:D, 0:S - 1], ACT.Identity).then_inc(s.xT_ready, 1)
                        m = 0
                        for n in range(HALVES * CHUNKS):
                            t, k = divmod(n, CHUNKS)
                            a.wait_ge(s.chunk_in_psum, turn * HALVES * CHUNKS + n + 1)
                            if k < QK_CHUNKS:
                                if m >= 2:
                                    a.wait_ge(s.chunk_rotated, turn * HALVES * QK_CHUNKS + m - 1)
                                last = a.activation(c.sq[:, m % 2, :], c.bank[n % chunk_bank][:, :], ACT.Square)
                                m += 1
                            else:
                                h0 = 8 * (k - QK_CHUNKS)
                                last = a.activation(c.V[:, t, h0:h0 + 8, 0:DH],
                                                    c.bank[n % chunk_bank][:, :].rearrange("p (h d) -> p h d", h=8),
                                                    ACT.Identity)
                            last.then_inc(s.chunk_read, 1)
                        for i in range(0, 8, 2):
                            which, pp = divmod(i, 4)
                            a.wait_ge(s.qkT_in_psum, turn * 8 + i + 1)
                            a.activation(copy_to(which, pp), c.bank[i % 6][:, :], ACT.Identity).then_inc(s.qkT_by_scalar, 1)
                        core.scalar(a, turn)
                        for i in range(0, 4, 2):
                            a.wait_ge(s.ctxT_in_psum, turn * 4 + i + 1)
                            a.activation(c.ctxT[:, 2 * i:2 * i + 2, :].rearrange("p k s -> p (k s)"), c.bank[i][:, :],
                                         ACT.Identity).then_inc(s.ctxT_by_scalar, 1)
                    a.wait_ge(s.ff_weights, d * n_ff + n_ff)
                    a.activation(c.cols[:, 30:31], c.neg_half[:, 0:1], ACT.Gelu)
                    with a.Fori(0, B) as b:
                        turn = d * B + b
                        a.wait_ge(s.shifted_in_psum, turn + 1)
                        a.activation(c.xn[:, :, hi:D], c.bank[6][:, 0:D].rearrange("p (t d) -> p t d", t=HALVES),
                                     ACT.Identity).then_inc(s.shifted_ready, 1)
                        ff_norm.scalar(a, turn)
                        for k, (at, n) in enumerate(FF_CHUNKS):
                            a.wait_ge(s.ff_in_psum, turn * 3 + k + 1)
                            a.activation(c.probs[0:n, :, :].rearrange("p a b -> p (a b)")[:, k * S:(k + 1) * S],
                                         c.bank[k][0:n, S:2 * S], ACT.Gelu,
                                         bias=c.cols[0:n, 5 + k:6 + k]).then_inc(s.gelu_ready, 1)

            @block.vector
            def _(v):
                if number == 0:
                    v.sem_inc(s.attn_added, 1)
                    v.sem_inc(s.ff_added, 1)
                v.wait_ge(tables_loaded, 16 * (number + 1))
                v.memset(c.recip[:, 0, 31:32], 0.0)
                with v.Fori(layer0, layer1) as d:
                    v.wait_ge(s.attn_weights, d * n_attn + n_attn)
                    v.tensor_tensor(c.ropes[:, :, :, :], c.rope[:, :, :, 0:DH],
                                    c.scl[:, :, :].unsqueeze(2).broadcast_to((P, 4, HALVES, DH)),
                                    ALU.mult).then_inc(s.tables_ready, 1)
                    with v.Fori(0, B) as b:
                        turn = d * B + b
                        v.wait_ge(s.tables_ready, d + 1)
                        step = Steps(v, s.steps, turn, 1 + 1 + NEWTON_STEPS - 1)
                        m = 0
                        for n in range(HALVES * CHUNKS):
                            t, k = divmod(n, CHUNKS)
                            if k >= QK_CHUNKS:
                                continue
                            v.wait_ge(s.chunk_read, turn * HALVES * CHUNKS + n + 1)
                            last = v.tensor_reduce(c.ss[:, t, 8 * k:8 * k + 8], c.sq[:, m % 2, :].rearrange("p (h d) -> p h d", h=8),
                                                   AX, ALU.add)
                            if m >= 2:
                                v.wait_ge(s.sum_ready, turn * HALVES * QK_CHUNKS + m - 1)
                            tab = 2 * (k // 2)
                            rotate(v, c.bank[n % chunk_bank][:, :].rearrange("p (h d) -> p h d", h=8), c.turnA[:, m % 2, :],
                                   c.turnB[:, m % 2, :], 8, DH, c.ropes[:, tab, t, :],
                                   c.ropes[:, tab + 1, t, :]).then_inc(s.chunk_rotated, 1)
                            m += 1
                        v.wait_ge(s.chunk_rotated, (turn + 1) * HALVES * QK_CHUNKS)
                        ss = c.ss[:, :, :].rearrange("p t h -> p (t h)")
                        step.after(v.tensor_scalar(ss, ss, 1e-24, None, ALU.max))
                        rsqrt(v, step, c, ss, c.rs[:, 0, :, :].rearrange("p t h -> p (t h)"))
                        v.memset(c.recip[:, 0, 31:32], 0.0).then_inc(s.rs_ready, 1)
                        v.wait_ge(s.sum_ready, (turn + 1) * HALVES * QK_CHUNKS)
                        scale_half(v, 1).then_inc(s.second_half_scaled, 1)
                        for i in range(1, 8, 2):
                            which, pp = divmod(i, 4)
                            v.wait_ge(s.qkT_in_psum, turn * 8 + i + 1)
                            v.tensor_copy(copy_to(which, pp), c.bank[i % 6][:, :]).then_inc(s.qkT_by_vector, 1)
                            if i == 7:
                                v.memset(c.recip[:, 0, 31:32], 0.0).then_inc(core.qk_ready, 1)
                        core.vector(v, turn)
                        for i in range(1, 4, 2):
                            v.wait_ge(s.ctxT_in_psum, turn * 4 + i + 1)
                            v.tensor_copy(c.ctxT[:, 2 * i:2 * i + 2, :].rearrange("p k s -> p (k s)"),
                                          c.bank[i][:, :]).then_inc(s.ctxT_by_vector, 1)
                        v.wait_ge(s.out_in_psum, turn + 1)
                        v.tensor_tensor(c.Y[:, row(b)], c.Y[:, row(b)], c.bank[7][:, 0:S], ALU.add).then_inc(s.attn_added, 1)
                        step.end()
                    with v.Fori(0, B) as b:
                        turn = d * B + b
                        v.wait_ge(s.ff_weights, d * n_ff + n_ff)
                        step = Steps(v, ff_steps, turn, LN_STEPS)
                        v.wait_ge(s.shifted_ready, turn + 1)
                        v.wait_ge(s.kept_ready, turn + 1)
                        ff_norm.vector(v, b, step, turn)
                        for k, (at, n) in enumerate(FF_CHUNKS):
                            v.wait_ge(s.gelu_ready, turn * 3 + k + 1)
                            v.scalar_tensor_tensor(out=c.hT[0:n, k, :], in0=c.bank[k][0:n, 0:S],
                                                   scalar=c.cols[0:n, 2 + k:3 + k],
                                                   in1=c.probs[0:n, :, :].rearrange("p a b -> p (a b)")[:, k * S:(k + 1) * S],
                                                   op0=ALU.add, op1=ALU.mult).then_inc(s.hidden_ready, 1)
                        v.wait_ge(s.ff_out_in_psum, turn + 1)
                        v.tensor_tensor(c.Y[:, row(b)], c.Y[:, row(b)], c.bank[7][:, 0:S], ALU.add).then_inc(s.ff_added, 1)
                        step.end()

    return run


def store(nc, sem, c, io):
    stored = sem("stored")
    with nc.Block() as block:

        @block.sync
        def _(sp):
            for b in range(B):
                sp.dma_start(io["out"][b].rearrange("(t p) d -> p t d", p=P),
                             c.X[:, b * ROW:(b + 1) * ROW].rearrange("p (t d) -> p t d", t=HALVES)).then_inc(stored, 16)
            sp.wait_ge(stored, 16 * B)


STOP = 99


def program(nc, io):
    with ExitStack() as ctx:
        c = allocate(nc, ctx)

        def sem(name):
            return ctx.enter_context(nc.semaphore(name))

        c.shared = Shared(sem)
        setup(nc, sem, c, io)

        transformer = windowed_transformers(nc, sem, c, "wt", io)

        def layer_on_Y(body):
            norm_rows(nc, c)
            body()
            add_back(nc, c)

        def last_block():
            plain_attention(nc, sem, c, "a3", io, c.Y, False, True)
            experts(nc, sem, c, "e3", io, c.Y, False)

        parts = [
            lambda: plain_attention(nc, sem, c, "a0", io, c.X, True, False),
            lambda: experts(nc, sem, c, "e0", io, c.X, True),
            lambda: linear_attention(nc, sem, c, "l1", io, c.X),
            lambda: layer_on_Y(lambda: transformer(0)),
            lambda: rotary_attention(nc, sem, c, "r2", io, c.X),
            lambda: layer_on_Y(lambda: transformer(1)),
            lambda: latent_attention(nc, sem, c, "m3", io, c.X),
            lambda: layer_on_Y(last_block),
        ]
        for part in parts[:STOP]:
            part()
        store(nc, sem, c, io)




def _heads_apart(w, np):
    out = np.zeros((w.shape[0], NH, 32), w.dtype)
    out[:, :, 0:HD] = w.reshape(w.shape[0], NH, HD)
    return out.reshape(w.shape[0], NH * 32)


def kernel(**inputs):
    import numpy as np
    import concourse.bacc as bacc
    from concourse.bass_utils import run_bass_kernel_spmd

    a = {k: np.ascontiguousarray(v) for k, v in inputs.items()}
    nc = bacc.Bacc("TRN2", target_bir_lowering=False, num_devices=1)
    arrays = {}

    def give(name, array):
        array = np.ascontiguousarray(array)
        name = "in_" + name
        arrays[name] = array
        return nc.dram_tensor(name, array.shape, mybir.dt.from_np(array.dtype), kind="ExternalInput").ap()

    def plain(name, wq, wk, wv, wo, bq, bk, bv, bo, g=None, bln=None):
        cols = np.zeros((P, 10), np.float32)
        cols[:, 0:4] = _heads_apart(bq[None], np).reshape(4, P).T
        cols[:, 4:8] = _heads_apart(bk[None], np).reshape(4, P).T
        if g is not None:
            cols[:, 8], cols[:, 9] = g, bln
        return {"wq": give(name + "_wq", _heads_apart(wq, np)), "wk": give(name + "_wk", _heads_apart(wk, np)),
                "wv": give(name + "_wv", wv), "wo": give(name + "_wo", wo), "cols": give(name + "_cols", cols),
                "bv": give(name + "_bv", bv), "bo": give(name + "_bo", bo)}

    def chunks(w, n, m):
        return w.reshape(n, P, m).transpose(1, 0, 2).reshape(P, n * m)

    def halves(t):
        return t.reshape(HALVES, P, -1).transpose(1, 0, 2)

    f32 = np.float32
    hd = np.arange(0, DH, 2, dtype=f32)
    inv_freq = (f32(1.0) / np.power(f32(10000.0), hd / f32(DH))).astype(f32)
    tok = np.arange(S, dtype=f32)
    fr = tok[:, None] * inv_freq[None, :]
    cos, sin = np.cos(fr).astype(f32), np.sin(fr).astype(f32)
    base = ((hd + f32(0.4 * DH)) / f32(1.4 * DH)).astype(f32)
    power = ((tok - S // 2) / (WINDOW // 2)).astype(f32)
    sc = np.power(base[None, :], power[:, None]).astype(f32)
    inv = (f32(1.0) / sc).astype(f32)
    tabs = []
    for m in (sc * f32(8.0), inv):
        tabs.append(np.concatenate([cos * m, cos * m], 1))
        tabs.append(np.concatenate([-(sin * m), sin * m], 1))
    window_rope = np.stack([halves(t) for t in tabs], 1).astype(f32)
    i = np.arange(D // 2, dtype=f32)
    ang = tok[:, None] * np.power(f32(10000.0), (f32(-2.0) * (i - f32(1.0)) / f32(D))).astype(f32)[None, :]
    c2, s2 = np.cos(ang).astype(f32), np.sin(ang).astype(f32)
    wide_rope = np.stack([halves(np.concatenate([c2, c2], 1)), halves(np.concatenate([s2, -s2], 1))], 1).astype(f32)

    def windowed(p):
        def swap(x):
            return np.concatenate([x[:, DH // 2:], x[:, :DH // 2]], 1)

        qs, ks = a[p + "q_scale"], a[p + "k_scale"]
        w1, w2, b1 = a[p + "W1"], a[p + "W2"], a[p + "b1"]
        w2p = np.zeros((DEPTH, P, 3, D), f32)
        cols = np.zeros((DEPTH, P, 8), f32)
        cols[:, :, 0], cols[:, :, 1] = a[p + "ln_g"], a[p + "ln_b"]
        for k, (at, n) in enumerate(FF_CHUNKS):
            w2p[:, 0:n, k] = w2[:, at:at + n]
            cols[:, 0:n, 2 + k] = b1[:, at:at + n]
            cols[:, 0:n, 5 + k] = b1[:, FF + at:FF + at + n]
        w2p[:, FF_CHUNKS[2][1], 2] = a[p + "b2"]
        return (a[p + "Wqkv"], a[p + "Wo"].reshape(DEPTH, 8, P, D).transpose(0, 2, 1, 3).reshape(DEPTH, P, 8 * D),
                np.concatenate([qs, swap(qs), ks, swap(ks)], 1), w1, w2p.reshape(DEPTH, P, 3 * D), cols)

    stacks = [np.concatenate(both) for both in zip(windowed("L1_ffn_"), windowed("L2_ffn_"))]
    window_io = {k: give("wt_" + k, v) for k, v in zip(("wqkv", "wo", "scales", "w1", "w2", "cols"), stacks)}
    window_io["rope"] = give("window_rope", window_rope)
    evens_first = np.concatenate([np.arange(0, D, 2), np.arange(1, D, 2)])
    wqkv1 = a["L1_attn_Wqkv"]
    tiles = np.zeros((P, 10, D), f32)
    m3 = {k: a["L3_attn_" + k] for k in ("W_DQ", "W_UQ", "W_DKV", "W_UKV", "W_QR", "W_KR", "W_O")}
    for n, t in enumerate((m3["W_DQ"], m3["W_UQ"].T, m3["W_DKV"], m3["W_UKV"][0:HD].T, m3["W_KR"], m3["W_QR"],
                           m3["W_UKV"][HD:2 * HD].T)):
        tiles[0:t.shape[0], n] = np.tile(t, (1, NH))
    tiles[:, 7] = np.tile(m3["W_O"].T, (NH, NH))
    eye = np.arange(D) // HD
    io = {
        "x": give("x", a["L0_attn_x"]),
        "headmask": give("headmask", (eye[:, None] == eye[None, :]).astype(np.float32)),
        "headcol": give("headcol", (eye[:, None] == np.arange(NH)[None, :]).astype(np.float32)),
        "a0": plain("a0", *[a["L0_attn_" + k] for k in ("Wq", "Wk", "Wv", "Wo", "bq", "bk", "bv", "bo")]),
    }
    io["e0"] = {"up": give("e0_up", a["L0_ffn_w1"].T), "side": give("e0_side", a["L0_ffn_v1"].T),
                "down": give("e0_down", chunks(a["L0_ffn_w2"], EXPERTS * 2, D)),
                "router": give("e0_router", a["L0_ffn_router_w"].T)}
    io["l1"] = {"wq": give("l1_wq", wqkv1[0:D].T), "wkv": give("l1_wkv", wqkv1[D:3 * D].T),
                "wp": give("l1_wp", a["L1_attn_Wproj"].T), "bp": give("l1_bp", a["L1_attn_bproj"])}
    io["wt"] = window_io
    io["r2"] = {"wqkv": give("r2_wqkv", np.concatenate([a["L2_attn_wq"].T[:, evens_first],
                                                        a["L2_attn_wk"].T[:, evens_first], a["L2_attn_wv"].T], 1)),
                "rope": give("r2_rope", wide_rope)}
    io["m3"] = {"tiles": give("m3_tiles", tiles),
                "norms": give("m3_norms", np.concatenate([a["L3_attn_q_norm_w"], a["L3_attn_k_norm_w"]]))}
    f = "L3_ffn_"
    io["a3"] = plain("a3", *[a[f + k] for k in ("wq", "wk", "wv", "wo", "bq", "bk", "bv", "bo", "ln1_g", "ln1_b")])
    io["e3"] = {"up": give("e3_up", a[f + "w1"].transpose(1, 0, 2).reshape(D, EXPERTS * 512)),
                "down": give("e3_down", chunks(a[f + "w2"].reshape(EXPERTS * 512, D), EXPERTS * 4, D)),
                "router": give("e3_router", a[f + "gate_w"]), "gate_b": give("e3_gate_b", a[f + "gate_b"]),
                "b1": give("e3_b1", a[f + "b1"].reshape(EXPERTS * 4, P).T), "b2": give("e3_b2", a[f + "b2"]),
                "ln": give("e3_ln", np.stack([a[f + "ln2_g"], a[f + "ln2_b"]], 1))}
    io["out"] = nc.dram_tensor("out", (B, S, D), F32, kind="ExternalOutput").ap()
    program(nc, io)
    result = run_bass_kernel_spmd(nc, [arrays], core_ids=[0])
    return result.results[0]["out"].reshape(B, S, D)
```

```python
import concourse.bass as bass
from concourse import mybir
from contextlib import ExitStack

F32 = mybir.dt.float32
I32 = mybir.dt.int32
BF16 = mybir.dt.bfloat16
ALU = mybir.AluOpType
ACT = mybir.ActivationFunctionType
AX = mybir.AxisListType.X

P = 128
B, S, D = 8, 256, 128
HALVES = S // P
ROW = S * D // P
NH = 16
HD = D // NH
GROUPS = NH // 4
DEPTH = 6
DH = 64
INNER = NH * DH
WINDOW = 32
FF = 341
FF_CHUNKS = [(0, 128), (128, 128), (256, 85)]
EXPERTS = 8
MASKED = -1e30
MAGIC = float(0x5F3759DF)
LN_EPS = 1e-5
RMS_EPS = 1.1920929e-07


def row(b, n=ROW, at=0):
    return bass.ds(b * n + at, n if at == 0 else n)


def half(b, t):
    return bass.ds(b * ROW + t * D, D)


class Steps:

    def __init__(self, eng, sem, turn, per_turn):
        self.eng, self.sem, self.turn, self.per_turn, self.n = eng, sem, turn, per_turn, 0

    def after(self, instruction):
        self.n += 1
        instruction.then_inc(self.sem, 1)
        self.eng.wait_ge(self.sem, self.turn * self.per_turn + self.n)

    def end(self):
        assert self.n == self.per_turn, (self.n, self.per_turn)


class Shared:

    def __init__(self, sem):
        self.sem, self.kept, self.turns = sem, {}, {}

    def take(self, stage, names, turns):
        if stage not in self.kept:
            self.kept[stage], self.turns[stage] = [self.sem(stage + "_" + n) for n in names], 0
        before = self.turns[stage]
        self.turns[stage] += turns
        return self.kept[stage], before


class Chip:
    pass


def allocate(nc, ctx):
    c = Chip()

    def sb(name, shape, dt=F32):
        return ctx.enter_context(nc.sbuf_tensor(name, shape, dt))

    c.X = sb("X", [P, B * ROW])
    c.Y = sb("Y", [P, B * ROW])
    c.ident = sb("ident", [P, P])
    c.identb = sb("identb", [P, P], BF16)
    c.causal = sb("causal", [P, P], BF16)
    c.band0 = sb("band0", [P, P], BF16)
    c.band1 = sb("band1", [P, P + WINDOW], BF16)
    c.shift = sb("shift", [P, P])
    c.carry = sb("carry", [P, P])
    c.headmask = sb("headmask", [P, P])
    c.headcol = sb("headcol", [P, NH])
    c.iota8 = sb("iota8", [P, HALVES, EXPERTS])
    c.neg_half = sb("neg_half", [P, 64])
    c.stats = sb("stats", [P, HALVES, 6])
    c.mv = sb("mv", [P, HALVES, 2])
    c.vareps = sb("vareps", [P, 32])
    c.rstd = sb("rstd", [P, 32])
    c.xn = sb("xn", [P, HALVES, D])
    c.xT = sb("xT", [P, S])
    c.qT = sb("qT", [P, 8, S])
    c.kT = sb("kT", [P, 8, S])
    c.V = sb("V", [P, HALVES, NH, DH + 1])
    c.negmax = sb("negmax", [P, NH, HALVES])
    c.probs = sb("probs", [P, 2, 512])
    c.probsT = sb("probsT", [P, 2, 512])
    c.recip = sb("recip", [P, 2, 32])
    c.ctx = sb("ctx", [P, HALVES, INNER])
    c.ctx2 = sb("ctx2", [P, HALVES, INNER])
    c.raw = sb("raw", [P, 4, 512])
    c.ctxT = sb("ctxT", [P, 8, S])
    c.wA = sb("wA", [P, 3 * INNER])
    c.wB = sb("wB", [P, 8 * D])
    c.wC = sb("wC", [P, 2 * FF])
    c.wD = sb("wD", [P, 3 * D])
    c.rope = sb("rope", [P, 4, HALVES, 2 * DH])
    c.ropes = sb("ropes", [P, 4, HALVES, DH])
    c.scl = sb("scl", [P, 4, DH])
    c.cols = sb("cols", [P, 32])
    c.colsA = sb("colsA", [P, 8 * DEPTH])
    c.rows = sb("rows", [P, 4, D])
    c.big = sb("big", [P, 2 * EXPERTS * 512])
    c.sq = sb("sq", [P, 2, 512])
    c.turnA = sb("turnA", [P, 2, 512])
    c.turnB = sb("turnB", [P, 2, 512])
    c.qk = sb("qk", [P, HALVES, 2, INNER])
    c.ss = sb("ss", [P, HALVES, 32])
    c.rs = sb("rs", [P, 3, HALVES, 32])
    c.v1 = sb("v1", [P, HALVES, D + 4])
    c.kvblock = sb("kvblock", [P, D + NH])
    c.hT = sb("hT", [P, 3, S])
    c.onehotT = sb("onehotT", [EXPERTS, S])
    c.bottom = sb("bottom", [EXPERTS, D])
    c.ints = sb("ints", [P, 64], I32)
    c.newton = sb("newton", [P, 3, 64])
    c.small = sb("small", [P, 16, HALVES * EXPERTS])
    c.bank = [ctx.enter_context(nc.psum_tensor(f"bank{i}", [P, 512], F32)) for i in range(8)]
    return c




def setup(nc, sem, c, io):
    loaded, zeroed, built = sem("x_loaded"), sem("consts_zeroed"), sem("consts_built")
    with nc.Block() as block:

        @block.sync
        def _(sp):
            for b in range(B):
                sp.dma_start(c.X[:, b * ROW:(b + 1) * ROW].rearrange("p (t d) -> p t d", t=HALVES),
                             io["x"][b].rearrange("(t p) d -> p t d", p=P)).then_inc(loaded, 16)
            sp.dma_start(c.headmask[:, :], io["headmask"]).then_inc(loaded, 16)
            sp.dma_start(c.headcol[:, :], io["headcol"]).then_inc(loaded, 16)
            sp.wait_ge(loaded, 16 * (B + 2))

        @block.vector
        def _(v):
            for tile, value in ((c.ident, 0.0), (c.identb, 0.0), (c.causal, 0.0), (c.band0, 0.0), (c.band1, 0.0),
                                (c.shift, 0.0), (c.carry, 0.0), (c.neg_half, -0.5)):
                last = v.memset(tile[:, :], value)
            v.memset(c.V[:, :, :, :], 1.0)
            v.memset(c.xT[:, :], 0.0)
            v.memset(c.v1[:, :, :], 1.0)
            v.memset(c.hT[:, :, :], 1.0)
            last = v.memset(c.probsT[:, :, :], 0.0)
            last.then_inc(zeroed, 1)

        @block.gpsimd
        def _(pool):
            pool.wait_ge(zeroed, 1)

            def where(tile, n, keep, base, mult, step, fill):
                return pool.affine_select(out=tile, in_=tile, pattern=[[step, n]], compare_op=keep, fill=fill,
                                          base=base, channel_multiplier=mult)

            where(c.ident[:, :], P, ALU.not_equal, 0, 1, -1, 1.0)
            where(c.identb[:, :], P, ALU.not_equal, 0, 1, -1, 1.0)
            where(c.shift[:, :], P, ALU.not_equal, 1, 1, -1, 1.0)
            where(c.carry[:, :], P, ALU.not_equal, 1 - P, 1, -P, 1.0)
            where(c.causal[:, :], P, ALU.is_ge, 0, 1, -1, MASKED)
            first = where(c.band0[:, :], P, ALU.is_ge, 0, 1, -1, MASKED)
            other = where(c.band1[:, :], P + WINDOW, ALU.is_ge, WINDOW, 1, -1, MASKED)
            other.then_inc(built, 1)
            pool.wait_ge(built, 1)
            where(c.band0[:, :], P, ALU.is_ge, WINDOW, -1, 1, MASKED)
            where(c.band1[:, :], P + WINDOW, ALU.is_ge, 0, -1, 1, MASKED)
            pool.iota(c.small[:, 0, :].bitcast(I32), pattern=[[0, HALVES], [1, EXPERTS]], base=0,
                      channel_multiplier=0).then_inc(built, 1)
            pool.wait_ge(built, 2)
            pool.tensor_copy(c.iota8[:, :, :], c.small[:, 0, :].bitcast(I32).rearrange("p (t e) -> p t e", t=HALVES))



LN_STEPS = 2


class Norm:

    def __init__(self, c, src, gain=None, stage="norm", turns=B):
        self.c, self.src, self.gain = c, src, gain
        names = ("var_ready", "rstd_ready", "xn_ready", "xT_in_psum", "xT_ready")
        (self.var_ready, self.rstd_ready, self.xn_ready, self.xT_in_psum,
         self.xT_ready), self.before = c.shared.take(stage, names, turns)

    def source(self, b, t):
        if self.src is None:
            return self.c.xn[:, t, :]
        return self.src[:, half(b, t)]

    def vector(self, v, b, step, turn=None):
        c, turn = self.c, (b if turn is None else turn) + self.before
        for t in range(HALVES):
            last = v.bn_stats(c.stats[:, t, :], self.source(b, t))
        step.after(last)
        v.memset(c.vareps[:, 30:31], 0.0)
        for t in range(HALVES):
            last = v.bn_aggr(c.mv[:, t, :], c.stats[:, t, :])
        step.after(last)
        v.tensor_scalar(c.vareps[:, 0:HALVES], c.mv[:, :, 1], LN_EPS, None, ALU.add).then_inc(self.var_ready, 1)
        v.wait_ge(self.rstd_ready, turn + 1)
        for t in range(HALVES):
            last = v.tensor_scalar(c.xn[:, t, :], self.source(b, t), c.mv[:, t, 0:1], c.rstd[:, t:t + 1],
                                   ALU.subtract, ALU.mult)
        last.then_inc(self.xn_ready, 1)

    def pool(self, g, turn):
        c, turn = self.c, turn + self.before
        g.wait_ge(self.var_ready, turn + 1)
        g.tensor_tensor(c.rstd[:, 0:HALVES], c.vareps[:, 0:HALVES], c.neg_half[:, 0:HALVES],
                        ALU.pow).then_inc(self.rstd_ready, 1)

    def tensor(self, pe, turn):
        c, turn = self.c, turn + self.before
        pe.wait_ge(self.xn_ready, turn + 1)
        for t in range(HALVES):
            last = pe.transpose(c.bank[6][:, t * P:(t + 1) * P], c.xn[:, t, :], c.ident[:, :])
        last.then_inc(self.xT_in_psum, 1)
        pe.wait_ge(self.xT_ready, turn + 1)

    def scalar(self, a, turn):
        c, turn = self.c, turn + self.before
        a.wait_ge(self.xT_in_psum, turn + 1)
        if self.gain is None:
            last = a.activation(c.xT[:, :], c.bank[6][:, 0:S], ACT.Identity)
        else:
            last = a.activation(c.xT[:, :], c.bank[6][:, 0:S], ACT.Identity, scale=self.gain[0], bias=self.gain[1])
        last.then_inc(self.xT_ready, 1)




class Core:

    def __init__(self, c, heads, blocks, operands, values, width, per_ctx, stage, turns=B):
        self.c, self.heads, self.blocks = c, heads, blocks
        self.operands, self.values, self.width, self.per_ctx = operands, values, width, per_ctx
        names = ("qk_ready", "scores_ready", "negmax_ready", "probs_ready", "probsT_in_psum", "probsT_ready",
                 "ctx_in_psum", "recip_ready", "ctx_ready")
        (self.qk_ready, self.scores_ready, self.negmax_ready, self.probs_ready, self.probsT_in_psum,
         self.probsT_ready, self.ctx_in_psum, self.recip_ready,
         self.ctx_ready), self.before = c.shared.take(stage, names, turns)
        self.n_ctx = heads // per_ctx
        self.at, n = [], 0
        for t in range(HALVES):
            for (kt, k0, kn, mask) in blocks[t]:
                self.at.append((t, kt, k0, kn, n))
                n += kn
        self.used = n
        self.span = [sum(x[2] for x in blocks[t]) for t in range(HALVES)]

    def scores(self, pe, turn, h):
        c = self.c
        out = c.bank[h % 2]
        at = 0
        for t in range(HALVES):
            q, k = self.operands(h)
            first = self.blocks[t][0]
            k0 = first[0] * P + first[1]
            n = self.span[t]
            masks = [x for x in self.blocks[t] if x[3] is not None]
            last = pe.matmul(out[:, at:at + n], q[:, t * P:(t + 1) * P], k[:, k0:k0 + n], start=True,
                             stop=not masks, skip_group_check=True)
            if masks:
                mask, off = masks[0][3]
                last = pe.matmul(out[:, at + off:at + n], self.c.identb[:, :], mask, start=False, stop=True,
                                 skip_group_check=True)
            at += n
        last.then_inc(self.scores_ready, 1)

    def turn_probs(self, pe, turn, h):
        c = self.c
        pe.wait_ge(self.probs_ready, turn * self.heads + h + 1)
        for i, (t, kt, k0, kn, at) in enumerate(self.at):
            last = pe.transpose(c.bank[2 + h % 2][0:kn, i * P:(i + 1) * P], c.probs[:, h % 2, at:at + kn],
                                c.ident[:, :])
        last.then_inc(self.probsT_in_psum, 1)

    def weigh(self, pe, turn, h):
        c = self.c
        n, w = self.per_ctx, self.width
        group = h // n
        pe.wait_ge(self.probsT_ready, turn * self.heads + h + 1)
        if h % n == 0 and group >= 2:
            pe.wait_ge(self.ctx_ready, turn * self.n_ctx + group - 1)
        for t in range(HALVES):
            mine = [(i, x) for i, x in enumerate(self.at) if x[0] == t]
            o = (t * n + h % n) * w
            for j, (i, (_, kt, k0, kn, at)) in enumerate(mine):
                last = pe.matmul(c.bank[4 + group % 2][:, o:o + w], c.probsT[k0:k0 + kn, h % 2, i * P:(i + 1) * P],
                                 self.values(h, kt)[k0:k0 + kn, :], start=(j == 0), stop=(j == len(mine) - 1))
        if h % n == n - 1:
            last.then_inc(self.ctx_in_psum, 1)

    def tensor(self, pe, turn):
        turn = turn + self.before
        pe.wait_ge(self.qk_ready, turn + 1)
        self.scores(pe, turn, 0)
        if self.heads > 1:
            self.scores(pe, turn, 1)
        for h in range(self.heads):
            self.turn_probs(pe, turn, h)
            if h + 2 < self.heads:
                self.scores(pe, turn, h + 2)
            if h >= 1:
                self.weigh(pe, turn, h - 1)
        self.weigh(pe, turn, self.heads - 1)

    def vector(self, v, turn):
        c, H, turn = self.c, self.heads, turn + self.before
        for h in range(H + 1):
            if h < H:
                v.wait_ge(self.scores_ready, turn * H + h + 1)
                at = 0
                for t in range(HALVES):
                    last = v.tensor_reduce(c.negmax[:, h, t:t + 1], c.bank[h % 2][:, at:at + self.span[t]], AX,
                                           ALU.max, negate=True)
                    at += self.span[t]
                last.then_inc(self.negmax_ready, 1)
            if h >= 1:
                self.copy_probs(v, turn, h - 1)
                if h % self.per_ctx == 0:
                    self.normalise(v, turn, h // self.per_ctx - 1)

    def copy_probs(self, v, turn, h):
        c, H = self.c, self.heads
        v.wait_ge(self.probsT_in_psum, turn * H + h + 1)
        src, dst = c.bank[2 + h % 2], c.probsT[:, h % 2, :]
        if all(x[3] == P for x in self.at):
            n = len(self.at) * P
            last = v.tensor_copy(dst[:, 0:n], src[:, 0:n])
        else:
            for i, (t, kt, k0, kn, at) in enumerate(self.at):
                last = v.tensor_copy(dst[k0:k0 + kn, i * P:(i + 1) * P], src[0:kn, i * P:(i + 1) * P])
        last.then_inc(self.probsT_ready, 1)

    def normalise(self, v, turn, group):
        c, n, w = self.c, self.per_ctx, self.width
        v.wait_ge(self.ctx_in_psum, turn * self.n_ctx + group + 1)
        src = c.bank[4 + group % 2][:, 0:HALVES * n * w].rearrange("p (t h w) -> p t h w", t=HALVES, h=n)
        rec = c.recip[:, group % 2, 0:HALVES * n].rearrange("p (t h) -> p t h", t=HALVES)
        v.reciprocal(rec, src[:, :, :, w - 1]).then_inc(self.recip_ready, 1)
        v.wait_ge(self.recip_ready, turn * self.n_ctx + group + 1)
        for t in range(HALVES):
            dst = c.ctx[:, t, group * n * (w - 1):(group + 1) * n * (w - 1)].rearrange("p (h w) -> p h w", h=n)
            last = v.tensor_tensor(dst, src[:, t, :, 0:w - 1],
                                   rec[:, t, :].unsqueeze(2).broadcast_to((P, n, w - 1)), ALU.mult)
        last.then_inc(self.ctx_ready, 1)

    def scalar(self, a, turn):
        c, H, turn = self.c, self.heads, turn + self.before
        for h in range(H):
            a.wait_ge(self.negmax_ready, turn * H + h + 1)
            at = 0
            for t in range(HALVES):
                last = a.activation(c.probs[:, h % 2, at:at + self.span[t]], c.bank[h % 2][:, at:at + self.span[t]],
                                    ACT.Exp, bias=c.negmax[:, h, t:t + 1])
                at += self.span[t]
            last.then_inc(self.probs_ready, 1)


def causal_blocks(c):
    tri = c.causal[:, :]
    return [[(0, 0, P, (tri, 0))], [(0, 0, P, None), (1, 0, P, (tri, P))]]


def full_blocks():
    return [[(0, 0, P, None), (1, 0, P, None)]] * 2




def plain_attention(nc, sem, c, name, io, x, causal, affine):
    w = io[name]
    norm = Norm(c, x, (c.cols[:, 8:9], c.cols[:, 9:10]) if affine else None)
    core = Core(c, NH, causal_blocks(c) if causal else full_blocks(),
                lambda h: (c.qT[32 * (h % 4):32 * (h % 4) + 32, h // 4, :], c.kT[32 * (h % 4):32 * (h % 4) + 32, h // 4, :]),
                lambda h, kt: c.V[:, kt, h, DH - HD:DH + 1], HD + 1, NH, "heads")
    loaded, bias_scaled = sem(name + "_weights"), sem(name + "_bias_scaled")
    proj_in_psum, proj_copied, step_v = sem(name + "_proj_in_psum"), sem(name + "_proj_copied"), sem(name + "_steps")
    v_in_psum, v_ready = sem(name + "_v_in_psum"), sem(name + "_v_ready")
    ctxT_in_psum, ctxT_ready = sem(name + "_ctxT_in_psum"), sem(name + "_ctxT_ready")
    out_in_psum = sem(name + "_out_in_psum")
    wq, wk = c.wA[:, 0:512], c.wA[:, 512:1024]
    wv, wo = c.wB[:, 0:D], c.wB[:, D:2 * D]
    scale = float(HD) ** -0.5
    with nc.Block() as block:

        @block.sync
        def _(sp):
            n = 0
            for dst, src in ((wq, w["wq"]), (wk, w["wk"]), (wv, w["wv"]), (wo, w["wo"]), (c.cols[:, 0:10], w["cols"]),
                             (c.rows[:, 0, :], w["bv"].partition_broadcast(P)),
                             (c.rows[:, 1, :], w["bo"].partition_broadcast(P))):
                sp.dma_start(dst, src).then_inc(loaded, 16)
                n += 16
            sp.wait_ge(loaded, n)

        @block.tensor
        def _(pe):
            pe.wait_ge(loaded, 112)
            with pe.Fori(0, B) as b:
                norm.tensor(pe, b)
                for u, (weights, g0) in enumerate(((wq, 0), (wq, 2), (wk, 0), (wk, 2))):
                    for g in range(2):
                        last = pe.matmul(c.bank[u][:, g * S:(g + 1) * S], weights[:, (g0 + g) * P:(g0 + g + 1) * P],
                                         c.xT[:, :], start=True, stop=True)
                    last.then_inc(proj_in_psum, 1)
                for t in range(HALVES):
                    last = pe.matmul(c.bank[7][:, t * D:(t + 1) * D], c.xT[:, t * P:(t + 1) * P], wv, start=True,
                                     stop=True)
                last.then_inc(v_in_psum, 1)
                pe.wait_ge(v_ready, b + 1)
                core.tensor(pe, b)
                pe.wait_ge(core.ctx_ready, core.before + b + 1)
                for t in range(HALVES):
                    last = pe.transpose(c.bank[6][:, t * P:(t + 1) * P], c.ctx[:, t, 0:D], c.ident[:, :])
                last.then_inc(ctxT_in_psum, 1)
                pe.wait_ge(ctxT_ready, b + 1)
                for t in range(HALVES):
                    last = pe.matmul(c.bank[7][:, t * D:(t + 1) * D], c.ctxT[:, 0, t * P:(t + 1) * P], wo, start=True,
                                     stop=True)
                last.then_inc(out_in_psum, 1)

        @block.gpsimd
        def _(g):
            with g.Fori(0, B) as b:
                norm.pool(g, b)

        @block.scalar
        def _(a):
            a.wait_ge(loaded, 112)
            a.mul(c.cols[:, 16:20], c.cols[:, 0:4], scale).then_inc(bias_scaled, 1)
            a.wait_ge(bias_scaled, 1)
            a.activation(c.cols[:, 30:31], c.cols[:, 0:1], ACT.Exp)
            with a.Fori(0, B) as b:
                norm.scalar(a, b)
                for u in range(4):
                    a.wait_ge(proj_in_psum, b * 4 + u + 1)
                    for g in range(2):
                        src, gg = c.bank[u][:, g * S:(g + 1) * S], 2 * (u % 2) + g
                        if u < 2:
                            last = a.activation(c.qT[:, gg, :], src, ACT.Identity, scale=scale,
                                                bias=c.cols[:, 16 + gg:17 + gg])
                        else:
                            last = a.activation(c.kT[:, gg, :], src, ACT.Identity, bias=c.cols[:, 4 + gg:5 + gg])
                last.then_inc(core.qk_ready, 1)
                core.scalar(a, b)
                a.wait_ge(ctxT_in_psum, b + 1)
                a.activation(c.ctxT[:, 0, :], c.bank[6][:, 0:S], ACT.Identity).then_inc(ctxT_ready, 1)

        @block.vector
        def _(v):
            v.wait_ge(loaded, 112)
            with v.Fori(0, B) as b:
                step = Steps(v, step_v, b, 3)
                norm.vector(v, b, step)
                v.wait_ge(v_in_psum, b + 1)
                v.tensor_tensor(c.V[:, :, :, DH - HD:DH],
                                c.bank[7][:, 0:S].rearrange("p (t h d) -> p t h d", t=HALVES, h=NH),
                                c.rows[:, 0, :].rearrange("p (h d) -> p h d", h=NH).unsqueeze(1)
                                .broadcast_to((P, HALVES, NH, HD)), ALU.add).then_inc(v_ready, 1)
                core.vector(v, b)
                v.wait_ge(out_in_psum, b + 1)
                add_rows(v, step, x, b, c.bank[7][:, 0:S], c.rows[:, 1, :])
                step.end()


def add_rows(v, step, x, b, more, bias=None):
    first = v.tensor_tensor(x[:, row(b)], x[:, row(b)], more, ALU.add)
    if bias is None:
        return first
    step.after(first)
    halves = x[:, row(b)].rearrange("p (t d) -> p t d", t=HALVES)
    return v.tensor_tensor(halves, halves, bias.unsqueeze(1).broadcast_to((P, HALVES, D)), ALU.add)


NEWTON_STEPS = 11


def rsqrt(v, step, c, x, y):
    n = x.shape[-1]
    ints, a, b, y2 = c.ints[:, 0:n], c.newton[:, 0, 0:n], c.newton[:, 1, 0:n], c.newton[:, 2, 0:n]
    step.after(v.tensor_scalar(ints, x.bitcast(I32), 1, None, ALU.logical_shift_right))
    step.after(v.tensor_scalar(a.bitcast(I32), ints, -1.0, MAGIC, ALU.mult, ALU.add))
    for src, dst in ((a, b), (b, a), (a, y)):
        step.after(v.tensor_tensor(y2, src, src, ALU.mult))
        step.after(v.scalar_tensor_tensor(out=y2, in0=y2, scalar=-0.5, in1=x, op0=ALU.mult, op1=ALU.mult))
        step.after(v.scalar_tensor_tensor(out=dst, in0=y2, scalar=1.5, in1=src, op0=ALU.add, op1=ALU.mult))




def experts(nc, sem, c, name, io, x, gated):
    w = io[name]
    F = 256 if gated else 512
    chunks = F // P
    norm = Norm(c, x, None if gated else (c.cols[:, 0:1], c.cols[:, 1:2]))
    loaded, step_v = sem(name + "_weights"), sem(name + "_steps")
    logits_in_psum, gap_ready, share_ready = sem(name + "_logits_in_psum"), sem(name + "_gap_ready"), sem(name + "_share_ready")
    onehot_ready, onehotT_in_psum, onehotT_ready = sem(name + "_onehot_ready"), sem(name + "_onehotT_in_psum"), sem(name + "_onehotT_ready")
    up_in_psum, act_ready, hidden_ready = sem(name + "_up_in_psum"), sem(name + "_act_ready"), sem(name + "_hidden_ready")
    down_in_psum, acc_done, bias_in_psum = sem(name + "_down_in_psum"), sem(name + "_acc_done"), sem(name + "_bias_in_psum")
    up, side = c.big[:, 0:EXPERTS * F], c.big[:, EXPERTS * F:2 * EXPERTS * F]
    down0 = 2 * EXPERTS * F if gated else EXPERTS * F
    down = c.big[:, down0:down0 + EXPERTS * F]
    router = c.wB[:, 0:EXPERTS]
    hidden = c.qk[:, :, 0, 0:chunks * S]

    def te(i):
        return c.small[:, i, :].rearrange("p (t e) -> p t e", t=HALVES)

    logits, equal, cand, best1, rest, best2, weight, tmp = [te(i) for i in range(1, 9)]
    top = c.small[:, 10, 0:12].rearrange("p (k t) -> p k t", t=HALVES)

    def over(col):
        return col.unsqueeze(2).broadcast_to((P, HALVES, EXPERTS))

    with nc.Block() as block:

        @block.sync
        def _(sp):
            n = 0
            todo = [(up, w["up"]), (down, w["down"]), (router, w["router"])]
            if gated:
                todo.append((side, w["side"]))
            else:
                todo += [(c.cols[:, 0:2], w["ln"]), (c.colsA[:, 0:32], w["b1"]), (c.bottom[:, :], w["b2"]),
                         (c.rows[:, 0, 0:EXPERTS], w["gate_b"].partition_broadcast(P))]
            for dst, src in todo:
                sp.dma_start(dst, src).then_inc(loaded, 16)
                n += 16
            sp.wait_ge(loaded, n)

        all_loaded = 16 * (4 if gated else 7)

        @block.tensor
        def _(pe):
            pe.wait_ge(loaded, all_loaded)

            def go_up(b, e):
                for k in range(chunks):
                    out = c.bank[2 * (e % 2) + (0 if gated else k // 2)][:, (k % 2) * S:(k % 2) * S + S]
                    last = pe.matmul(out, up[:, e * F + k * P:e * F + (k + 1) * P], c.xT[:, :], start=True, stop=True)
                if gated:
                    for k in range(chunks):
                        last = pe.matmul(c.bank[2 * (e % 2) + 1][:, k * S:(k + 1) * S],
                                         side[:, e * F + k * P:e * F + (k + 1) * P], c.xT[:, :], start=True, stop=True)
                last.then_inc(up_in_psum, 1)

            def go_down(b, e):
                pe.wait_ge(hidden_ready, b * EXPERTS + e + 1)
                if e >= 2:
                    pe.wait_ge(acc_done, b * EXPERTS + e - 1)
                for t in range(HALVES):
                    for k in range(chunks):
                        last = pe.matmul(c.bank[4 + e % 2][:, t * D:(t + 1) * D],
                                         hidden[:, e % 2, k * S + t * P:k * S + (t + 1) * P],
                                         down[:, e * F + k * D:e * F + (k + 1) * D], start=(k == 0),
                                         stop=(k == chunks - 1))
                last.then_inc(down_in_psum, 1)

            with pe.Fori(0, B) as b:
                norm.tensor(pe, b)
                for t in range(HALVES):
                    last = pe.matmul(c.bank[7][:, t * EXPERTS:(t + 1) * EXPERTS], c.xT[:, t * P:(t + 1) * P], router,
                                     start=True, stop=True)
                last.then_inc(logits_in_psum, 1)
                go_up(b, 0)
                for e in range(EXPERTS):
                    if e + 1 < EXPERTS:
                        if not gated and e + 1 >= 2:
                            pass
                        go_up(b, e + 1)
                    if e == 0 and not gated:
                        pe.wait_ge(onehot_ready, b + 1)
                        for t in range(HALVES):
                            last = pe.transpose(c.bank[7][0:EXPERTS, t * P:(t + 1) * P], best1[:, t, :],
                                                c.ident[:, :])
                        last.then_inc(onehotT_in_psum, 1)
                        pe.wait_ge(onehotT_ready, b + 1)
                        for t in range(HALVES):
                            last = pe.matmul(c.bank[7][:, S + t * D:S + (t + 1) * D],
                                             c.onehotT[:, t * P:(t + 1) * P], c.bottom[:, :], start=True, stop=True)
                        last.then_inc(bias_in_psum, 1)
                    go_down(b, e)

        @block.gpsimd
        def _(g):
            with g.Fori(0, B) as b:
                norm.pool(g, b)

        @block.scalar
        def _(a):
            a.wait_ge(loaded, all_loaded)
            a.activation(c.cols[:, 30:31], c.neg_half[:, 0:1], ACT.Silu if gated else ACT.Relu)
            with a.Fori(0, B) as b:
                norm.scalar(a, b)
                if gated:
                    a.wait_ge(gap_ready, b + 1)
                    a.activation(top[:, 3, :], top[:, 2, :], ACT.Tanh, scale=0.5).then_inc(share_ready, 1)
                for e in range(EXPERTS):
                    a.wait_ge(up_in_psum, b * EXPERTS + e + 1)
                    if gated:
                        if e >= 2:
                            a.wait_ge(hidden_ready, b * EXPERTS + e - 1)
                        a.activation(c.sq[:, e % 2, :], c.bank[2 * (e % 2)][:, :], ACT.Silu).then_inc(act_ready, 1)
                    else:
                        if e >= 2:
                            a.wait_ge(down_in_psum, b * EXPERTS + e - 1)
                        for k in range(chunks):
                            last = a.activation(hidden[:, e % 2, k * S:(k + 1) * S],
                                                c.bank[2 * (e % 2) + k // 2][:, (k % 2) * S:(k % 2) * S + S],
                                                ACT.Relu, bias=c.colsA[:, e * chunks + k:e * chunks + k + 1])
                        last.then_inc(hidden_ready, 1)

        @block.vector
        def _(v):
            v.wait_ge(loaded, all_loaded)

            def hottest(step, src, top_k, dst):
                step.after(v.tensor_reduce(top_k, src, AX, ALU.max))
                step.after(v.tensor_tensor(equal, src, over(top_k), ALU.is_equal))
                step.after(v.scalar_tensor_tensor(out=cand, in0=equal, scalar=-float(EXPERTS), in1=c.iota8[:, :, :],
                                                  op0=ALU.mult, op1=ALU.add))
                step.after(v.tensor_reduce(top[:, 5, :], cand, AX, ALU.min))
                step.after(v.tensor_tensor(dst, cand, over(top[:, 5, :]), ALU.is_equal))

            with v.Fori(0, B) as b:
                step = Steps(v, step_v, b, STEPS_GATED if gated else STEPS_PLAIN)
                norm.vector(v, b, step)
                v.wait_ge(logits_in_psum, b + 1)
                psum = c.bank[7][:, 0:HALVES * EXPERTS].rearrange("p (t e) -> p t e", t=HALVES)
                if gated:
                    step.after(v.tensor_copy(logits, psum))
                    hottest(step, logits, top[:, 0, :], best1)
                    step.after(v.scalar_tensor_tensor(out=rest, in0=best1, scalar=MASKED, in1=logits, op0=ALU.mult,
                                                      op1=ALU.add))
                    hottest(step, rest, top[:, 1, :], best2)
                    v.tensor_tensor(top[:, 2, :], top[:, 0, :], top[:, 1, :], ALU.subtract).then_inc(gap_ready, 1)
                    v.wait_ge(share_ready, b + 1)
                    step.after(v.tensor_scalar(top[:, 4, :], top[:, 3, :], 0.5, 0.5, ALU.mult, ALU.add))
                    step.after(v.tensor_scalar(top[:, 5, :], top[:, 3, :], -0.5, 0.5, ALU.mult, ALU.add))
                    step.after(v.tensor_tensor(weight, best1, over(top[:, 4, :]), ALU.mult))
                    step.after(v.tensor_tensor(tmp, best2, over(top[:, 5, :]), ALU.mult))
                    step.after(v.tensor_tensor(weight, weight, tmp, ALU.add))
                    share = weight
                else:
                    step.after(v.tensor_tensor(logits, psum, c.rows[:, 0, 0:EXPERTS].unsqueeze(1)
                                               .broadcast_to((P, HALVES, EXPERTS)), ALU.add))
                    hottest(step, logits, top[:, 0, :], best1)
                    last = v.memset(top[:, 1, 0:1], 0.0)
                    last.then_inc(onehot_ready, 1)
                    v.wait_ge(onehotT_in_psum, b + 1)
                    v.tensor_copy(c.onehotT[:, :], c.bank[7][0:EXPERTS, 0:S]).then_inc(onehotT_ready, 1)
                    share = best1

                def gather(e):
                    v.wait_ge(down_in_psum, b * EXPERTS + e + 1)
                    src = c.bank[4 + e % 2]
                    for t in range(HALVES):
                        part, acc = src[:, t * D:(t + 1) * D], c.ctx[:, t, 0:D]
                        if e == 0:
                            last = v.tensor_scalar(acc, part, share[:, t, e:e + 1], None, ALU.mult)
                        else:
                            last = v.scalar_tensor_tensor(out=acc, in0=part, scalar=share[:, t, e:e + 1], in1=acc,
                                                          op0=ALU.mult, op1=ALU.add)
                    last.then_inc(acc_done, 1)
                    v.wait_ge(acc_done, b * EXPERTS + e + 1)

                for e in range(EXPERTS):
                    if gated:
                        v.wait_ge(act_ready, b * EXPERTS + e + 1)
                        if e >= 2:
                            v.wait_ge(down_in_psum, b * EXPERTS + e - 1)
                        v.tensor_tensor(hidden[:, e % 2, :], c.sq[:, e % 2, :], c.bank[2 * (e % 2) + 1][:, :],
                                        ALU.mult).then_inc(hidden_ready, 1)
                    if e >= 1:
                        gather(e - 1)
                gather(EXPERTS - 1)
                halves = x[:, row(b)].rearrange("p (t d) -> p t d", t=HALVES)
                step.after(v.tensor_tensor(halves, halves, c.ctx[:, :, 0:D], ALU.add))
                if not gated:
                    v.wait_ge(bias_in_psum, b + 1)
                    step.after(v.tensor_tensor(x[:, row(b)], x[:, row(b)], c.bank[7][:, S:2 * S], ALU.add))
                step.end()


STEPS_GATED = LN_STEPS + 1 + 5 + 1 + 5 + 5 + 1
STEPS_PLAIN = LN_STEPS + 1 + 5 + 2




def linear_attention(nc, sem, c, name, io, x):
    w = io[name]
    norm = Norm(c, x)
    loaded, step_v = sem(name + "_weights"), sem(name + "_steps")
    proj_in_psum, low_ready, exp_ready, feat_ready = [sem(name + "_" + s) for s in
                                                      ("proj_in_psum", "low_ready", "exp_ready", "feat_ready")]
    kv_in_psum, kv_ready, out_in_psum, ctx_ready = [sem(name + "_" + s) for s in
                                                    ("kv_in_psum", "kv_ready", "num_in_psum", "ctx_ready")]
    ctxT_in_psum, ctxT_ready, proj2_in_psum = [sem(name + "_" + s) for s in
                                               ("ctxT_in_psum", "ctxT_ready", "out_in_psum")]
    wq, wkv, wp = c.wA[:, 0:D], c.wA[:, D:3 * D], c.wA[:, 3 * D:4 * D]
    qf, kf = c.turnA[:, 0, 0:S], c.turnA[:, 1, 0:S]
    lowq, lowk = c.turnB[:, 0, 0:S], c.turnB[:, 1, 0:S]
    expq, expk = c.sq[:, 0, 0:S], c.sq[:, 1, 0:S]
    with nc.Block() as block:

        @block.sync
        def _(sp):
            for dst, src in ((wq, w["wq"]), (wkv, w["wkv"]), (wp, w["wp"]),
                             (c.rows[:, 0, :], w["bp"].partition_broadcast(P))):
                sp.dma_start(dst, src).then_inc(loaded, 16)
            sp.wait_ge(loaded, 64)

        @block.tensor
        def _(pe):
            pe.wait_ge(loaded, 64)
            with pe.Fori(0, B) as b:
                norm.tensor(pe, b)
                pe.matmul(c.bank[0][:, 0:S], wq, c.xT[:, :], start=True, stop=True)
                for t in range(HALVES):
                    last = pe.matmul(c.bank[1 + t][:, 0:2 * D], c.xT[:, t * P:(t + 1) * P], wkv, start=True, stop=True)
                last.then_inc(proj_in_psum, 1)
                pe.wait_ge(feat_ready, b + 1)
                for t in range(HALVES):
                    last = pe.matmul(c.bank[3][:, 0:D + 1], kf[:, t * D:(t + 1) * D], c.v1[:, t, 0:D + 1],
                                     start=(t == 0), stop=(t == 1))
                last.then_inc(kv_in_psum, 1)
                pe.wait_ge(kv_ready, b + 1)
                for t in range(HALVES):
                    last = pe.matmul(c.bank[4][:, t * (D + NH):(t + 1) * (D + NH)], qf[:, t * P:(t + 1) * P],
                                     c.kvblock[:, :], start=True, stop=True)
                last.then_inc(out_in_psum, 1)
                pe.wait_ge(ctx_ready, b + 1)
                for t in range(HALVES):
                    last = pe.transpose(c.bank[6][:, t * P:(t + 1) * P], c.ctx[:, t, 0:D], c.ident[:, :])
                last.then_inc(ctxT_in_psum, 1)
                pe.wait_ge(ctxT_ready, b + 1)
                for t in range(HALVES):
                    last = pe.matmul(c.bank[7][:, t * D:(t + 1) * D], c.ctxT[:, 0, t * P:(t + 1) * P], wp, start=True,
                                     stop=True)
                last.then_inc(proj2_in_psum, 1)

        @block.gpsimd
        def _(g):
            with g.Fori(0, B) as b:
                norm.pool(g, b)

        @block.scalar
        def _(a):
            a.activation(c.cols[:, 30:31], c.neg_half[:, 0:1], ACT.Exp)
            with a.Fori(0, B) as b:
                norm.scalar(a, b)
                a.wait_ge(low_ready, b + 1)
                a.activation(expq, lowq, ACT.Exp)
                a.activation(expk, lowk, ACT.Exp).then_inc(exp_ready, 1)
                a.wait_ge(ctxT_in_psum, b + 1)
                a.activation(c.ctxT[:, 0, :], c.bank[6][:, 0:S], ACT.Identity).then_inc(ctxT_ready, 1)

        @block.vector
        def _(v):
            v.wait_ge(loaded, 64)
            with v.Fori(0, B) as b:
                step = Steps(v, step_v, b, LN_STEPS + 3)
                norm.vector(v, b, step)
                v.wait_ge(proj_in_psum, b + 1)
                v.tensor_scalar(lowq, c.bank[0][:, 0:S], 0.0, None, ALU.min)
                for t in range(HALVES):
                    last = v.tensor_scalar(lowk[:, t * D:(t + 1) * D], c.bank[1 + t][:, 0:D], 0.0, None, ALU.min)
                last.then_inc(low_ready, 1)
                for t in range(HALVES):
                    v.tensor_copy(c.v1[:, t, 0:D], c.bank[1 + t][:, D:2 * D])
                v.wait_ge(exp_ready, b + 1)
                v.scalar_tensor_tensor(out=qf, in0=c.bank[0][:, 0:S], scalar=0.0, in1=expq, op0=ALU.max, op1=ALU.add)
                for t in range(HALVES):
                    last = v.scalar_tensor_tensor(out=kf[:, t * D:(t + 1) * D], in0=c.bank[1 + t][:, 0:D], scalar=0.0,
                                                  in1=expk[:, t * D:(t + 1) * D], op0=ALU.max, op1=ALU.add)
                last.then_inc(feat_ready, 1)
                v.wait_ge(kv_in_psum, b + 1)
                v.tensor_tensor(c.kvblock[:, 0:D], c.bank[3][:, 0:D], c.headmask[:, :], ALU.mult)
                v.tensor_scalar(c.kvblock[:, D:D + NH], c.headcol[:, :], c.bank[3][:, D:D + 1], None,
                                ALU.mult).then_inc(kv_ready, 1)
                v.wait_ge(out_in_psum, b + 1)
                num = c.bank[4][:, 0:HALVES * (D + NH)].rearrange("p (t n) -> p t n", t=HALVES)
                den = c.recip[:, 0, 0:HALVES * NH].rearrange("p (t h) -> p t h", t=HALVES)
                step.after(v.tensor_scalar(den, num[:, :, D:D + NH], 1e-6, None, ALU.add))
                step.after(v.reciprocal(den, den))
                for t in range(HALVES):
                    last = v.tensor_tensor(c.ctx[:, t, 0:D].rearrange("p (h d) -> p h d", h=NH),
                                           num[:, t, 0:D].rearrange("p (h d) -> p h d", h=NH),
                                           den[:, t, :].unsqueeze(2).broadcast_to((P, NH, HD)), ALU.mult)
                last.then_inc(ctx_ready, 1)
                v.wait_ge(proj2_in_psum, b + 1)
                add_rows(v, step, x, b, c.bank[7][:, 0:S], c.rows[:, 0, :])
                step.end()




def rotary_attention(nc, sem, c, name, io, x):
    w = io[name]
    norm = Norm(c, x)
    core = Core(c, 1, causal_blocks(c), lambda h: (c.qT[:, 0, :], c.kT[:, 0, :]),
                lambda h, kt: c.v1[:, kt, 0:D + 1], D + 1, 1, "wide_head")
    loaded, step_v = sem(name + "_weights"), sem(name + "_steps")
    proj_in_psum, v_copied, qk_rotated, qkT_in_psum = [sem(name + "_" + s) for s in
                                                       ("proj_in_psum", "v_copied", "qk_rotated", "qkT_in_psum")]
    wqkv = c.wA[:, 0:3 * D]
    with nc.Block() as block:

        @block.sync
        def _(sp):
            sp.dma_start(wqkv, w["wqkv"]).then_inc(loaded, 16)
            sp.dma_start(c.rope[:, 0:2, :, :], w["rope"]).then_inc(loaded, 16)
            sp.wait_ge(loaded, 32)

        @block.tensor
        def _(pe):
            pe.wait_ge(loaded, 32)
            with pe.Fori(0, B) as b:
                norm.tensor(pe, b)
                for t in range(HALVES):
                    last = pe.matmul(c.bank[t][:, 0:3 * D], c.xT[:, t * P:(t + 1) * P], wqkv, start=True, stop=True)
                last.then_inc(proj_in_psum, 1)
                pe.wait_ge(qk_rotated, b + 1)
                for which in range(2):
                    for t in range(HALVES):
                        last = pe.transpose(c.bank[7][:, which * S + t * P:which * S + (t + 1) * P],
                                            c.qk[:, t, 0, which * D:(which + 1) * D], c.ident[:, :])
                last.then_inc(qkT_in_psum, 1)
                core.tensor(pe, b)

        @block.gpsimd
        def _(g):
            with g.Fori(0, B) as b:
                norm.pool(g, b)

        @block.scalar
        def _(a):
            a.activation(c.cols[:, 30:31], c.neg_half[:, 0:1], ACT.Exp)
            with a.Fori(0, B) as b:
                norm.scalar(a, b)
                a.wait_ge(proj_in_psum, b + 1)
                for t in range(HALVES):
                    last = a.activation(c.v1[:, t, 0:D], c.bank[t][:, 2 * D:3 * D], ACT.Identity)
                last.then_inc(v_copied, 1)
                a.wait_ge(qkT_in_psum, b + 1)
                a.activation(c.qT[:, 0, :], c.bank[7][:, 0:S], ACT.Identity, scale=float(D) ** -0.5)
                a.activation(c.kT[:, 0, :], c.bank[7][:, S:2 * S], ACT.Identity).then_inc(core.qk_ready, 1)
                core.scalar(a, b)

        @block.vector
        def _(v):
            v.wait_ge(loaded, 32)
            with v.Fori(0, B) as b:
                step = Steps(v, step_v, b, LN_STEPS + 1)
                norm.vector(v, b, step)
                v.wait_ge(v_copied, b + 1)
                for t in range(HALVES):
                    src = c.bank[t][:, 0:2 * D].rearrange("p (n d) -> p n d", n=2)
                    last = rotate(v, src, c.turnA[:, t, 0:2 * D], c.turnB[:, t, 0:2 * D], 2, D,
                                  c.rope[:, 0, t, :], c.rope[:, 1, t, :])
                step.after(last)
                for t in range(HALVES):
                    last = v.tensor_tensor(c.qk[:, t, 0, 0:2 * D], c.turnA[:, t, 0:2 * D], c.turnB[:, t, 0:2 * D],
                                           ALU.add)
                last.then_inc(qk_rotated, 1)
                core.vector(v, b)
                v.wait_ge(core.ctx_ready, core.before + b + 1)
                halves = x[:, row(b)].rearrange("p (t d) -> p t d", t=HALVES)
                v.tensor_tensor(halves, halves, c.ctx[:, :, 0:D], ALU.add)
                step.end()


def rotate(v, src, straight, crossed, n, width, cos, sin):
    h = width // 2
    straight = straight.rearrange("p (n d) -> p n d", n=n)
    crossed = crossed.rearrange("p (n d) -> p n d", n=n)

    def each(t):
        return t.unsqueeze(1).broadcast_to((P, n, t.shape[-1]))

    v.tensor_tensor(straight, src, each(cos), ALU.mult)
    v.tensor_tensor(crossed[:, :, 0:h], src[:, :, h:width], each(sin[:, 0:h]), ALU.mult)
    return v.tensor_tensor(crossed[:, :, h:width], src[:, :, 0:h], each(sin[:, h:width]), ALU.mult)




def latent_attention(nc, sem, c, name, io, x):
    w = io[name]
    norm = Norm(c, x)
    core = Core(c, NH, causal_blocks(c),
                lambda h: (c.qT[32 * (h % 4):32 * (h % 4) + 32, h // 4, :], c.kT[32 * (h % 4):32 * (h % 4) + 32, h // 4, :]),
                lambda h, kt: c.V[:, kt, h, DH - HD:DH + 1], HD + 1, NH, "heads")
    loaded, step_v, pads_zero = sem(name + "_weights"), sem(name + "_steps"), sem(name + "_pads_zero")
    products_in_psum, value_ready, value_in_psum, blocks_ready = [sem(name + "_" + s) for s in (
        "products_in_psum", "value_ready", "value_in_psum", "blocks_ready")]
    proj_in_psum, squared, normed, qkT_in_psum = [sem(name + "_" + s) for s in
                                                  ("proj_in_psum", "squared", "qk_normed", "qkT_in_psum")]
    blocks = c.wB[:, 0:4 * D]
    tiles = c.wA[:, 0:10 * D].rearrange("p (n d) -> p n d", n=10)
    pads = c.qk[:, :, :, 0:512].rearrange("p t w (h e) -> p t w h e", h=NH)
    with nc.Block() as block:

        @block.sync
        def _(sp):
            for dst, src in ((tiles[:, :, :], w["tiles"]), (c.rows[:, 0, 0:2 * HD], w["norms"].partition_broadcast(P))):
                sp.dma_start(dst, src).then_inc(loaded, 16)
            sp.wait_ge(loaded, 32)

        @block.tensor
        def _(pe):
            pe.wait_ge(loaded, 32)
            pe.matmul(c.bank[0][:, 0:D], tiles[0:DH, 0, :], tiles[0:DH, 1, :], start=True, stop=True)
            pe.matmul(c.bank[0][:, D:2 * D], tiles[:, 2, :], tiles[:, 3, :], start=True, stop=True)
            pe.matmul(c.bank[0][:, 2 * D:3 * D], tiles[0:DH, 4, :], tiles[0:DH, 5, :], start=True, stop=True)
            pe.matmul(c.bank[0][:, 3 * D:4 * D], tiles[:, 6, :], tiles[:, 2, :], start=True,
                      stop=True).then_inc(products_in_psum, 1)
            pe.wait_ge(value_ready, 1)
            pe.matmul(c.bank[1][:, 0:D], tiles[:, 8, :], tiles[:, 7, :], start=True,
                      stop=True).then_inc(value_in_psum, 1)
            pe.wait_ge(blocks_ready, 1)
            with pe.Fori(0, B) as b:
                norm.tensor(pe, b)
                for t in range(HALVES):
                    last = pe.matmul(c.bank[t][:, :], c.xT[:, t * P:(t + 1) * P], blocks, start=True, stop=True)
                last.then_inc(proj_in_psum, 1)
                pe.wait_ge(normed, b + 1)
                for which in range(2):
                    for g in range(GROUPS):
                        for t in range(HALVES):
                            o = ((g % 2) * HALVES + t) * P
                            last = pe.transpose(c.bank[2 + 2 * which + g // 2][:, o:o + P],
                                                c.qk[:, t, which, g * P:(g + 1) * P], c.ident[:, :])
                last.then_inc(qkT_in_psum, 1)
                core.tensor(pe, b)

        @block.gpsimd
        def _(g):
            with g.Fori(0, B) as b:
                norm.pool(g, b)

        @block.scalar
        def _(a):
            a.activation(c.cols[:, 30:31], c.neg_half[:, 0:1], ACT.Exp)
            with a.Fori(0, B) as b:
                norm.scalar(a, b)
                a.wait_ge(proj_in_psum, b + 1)
                for t in range(HALVES):
                    last = a.activation(c.sq[:, t, 0:2 * D], c.bank[t][:, 0:2 * D], ACT.Square)
                last.then_inc(squared, 1)
                a.wait_ge(qkT_in_psum, b + 1)
                for g in range(2):
                    a.activation(c.qT[:, 2 * g:2 * g + 2, :].rearrange("p g s -> p (g s)"), c.bank[2 + g][:, :],
                                 ACT.Identity, scale=float(HD) ** -0.5)
                for g in range(2):
                    last = a.activation(c.kT[:, 2 * g:2 * g + 2, :].rearrange("p g s -> p (g s)"), c.bank[4 + g][:, :],
                                        ACT.Identity)
                last.then_inc(core.qk_ready, 1)
                core.scalar(a, b)

        @block.vector
        def _(v):
            v.wait_ge(loaded, 32)
            v.memset(c.qk[:, :, :, :], 0.0)
            v.wait_ge(products_in_psum, 1)
            v.tensor_tensor(tiles[:, 8, :], c.bank[0][:, 3 * D:4 * D], c.headmask[:, :],
                            ALU.mult).then_inc(value_ready, 1)
            v.tensor_tensor(blocks[:, 0:3 * D].rearrange("p (n d) -> p n d", n=3),
                            c.bank[0][:, 0:3 * D].rearrange("p (n d) -> p n d", n=3),
                            c.headmask[:, :].unsqueeze(1).broadcast_to((P, 3, D)), ALU.mult)
            v.wait_ge(value_in_psum, 1)
            v.tensor_tensor(blocks[:, 3 * D:4 * D], c.bank[1][:, 0:D], c.headmask[:, :],
                            ALU.mult).then_inc(blocks_ready, 1)
            with v.Fori(0, B) as b:
                step = Steps(v, step_v, b, LN_STEPS + 1 + 1 + NEWTON_STEPS + 2 + 1)
                norm.vector(v, b, step)
                v.wait_ge(squared, b + 1)
                for t in range(HALVES):
                    last = v.tensor_reduce(c.ss[:, t, :], c.sq[:, t, 0:2 * D].rearrange("p (h d) -> p h d", d=HD), AX,
                                           ALU.add)
                step.after(last)
                ss = c.ss[:, :, :].rearrange("p t h -> p (t h)")
                step.after(v.tensor_scalar(ss, ss, 1.0 / HD, RMS_EPS, ALU.mult, ALU.add))
                rsqrt(v, step, c, ss, c.rs[:, 0, :, :].rearrange("p t h -> p (t h)"))
                for t in range(HALVES):
                    last = v.tensor_tensor(c.turnA[:, t, 0:2 * D].rearrange("p (h d) -> p h d", d=HD),
                                           c.bank[t][:, 0:2 * D].rearrange("p (h d) -> p h d", d=HD),
                                           c.rs[:, 0, t, :].unsqueeze(2).broadcast_to((P, 2 * NH, HD)), ALU.mult)
                step.after(last)
                for t in range(HALVES):
                    for which in range(2):
                        src = c.turnA[:, t, which * D:(which + 1) * D].rearrange("p (h d) -> p h d", d=HD)
                        dst = pads[:, t, 0, :, 0:HD] if which == 0 else src
                        last = v.tensor_tensor(dst, src, c.rows[:, 0, which * HD:(which + 1) * HD].unsqueeze(1)
                                               .broadcast_to((P, NH, HD)), ALU.mult)
                step.after(last)
                for t in range(HALVES):
                    v.tensor_tensor(pads[:, t, 1, :, 0:HD],
                                    c.turnA[:, t, D:2 * D].rearrange("p (h d) -> p h d", d=HD),
                                    c.bank[t][:, 2 * D:3 * D].rearrange("p (h d) -> p h d", d=HD), ALU.add)
                    last = v.tensor_copy(c.V[:, t, :, DH - HD:DH],
                                         c.bank[t][:, 3 * D:4 * D].rearrange("p (h d) -> p h d", d=HD))
                last.then_inc(normed, 1)
                core.vector(v, b)
                v.wait_ge(core.ctx_ready, core.before + b + 1)
                halves = x[:, row(b)].rearrange("p (t d) -> p t d", t=HALVES)
                step.after(v.tensor_tensor(halves, halves, c.ctx[:, :, 0:D], ALU.add))
                step.end()




def norm_rows(nc, c):
    (var_ready, rstd_ready, step_v), before = c.shared.take("rows", ("var_ready", "rstd_ready", "steps"), B)
    with nc.Block() as block:

        @block.gpsimd
        def _(g):
            with g.Fori(0, B) as b:
                g.wait_ge(var_ready, before + b + 1)
                g.tensor_tensor(c.rstd[:, 0:HALVES], c.vareps[:, 0:HALVES], c.neg_half[:, 0:HALVES],
                                ALU.pow).then_inc(rstd_ready, 1)

        @block.vector
        def _(v):
            with v.Fori(0, B) as b:
                step = Steps(v, step_v, before + b, LN_STEPS)
                for t in range(HALVES):
                    last = v.bn_stats(c.stats[:, t, :], c.X[:, half(b, t)])
                step.after(last)
                v.memset(c.vareps[:, 30:31], 0.0)
                for t in range(HALVES):
                    last = v.bn_aggr(c.mv[:, t, :], c.stats[:, t, :])
                step.after(last)
                v.tensor_scalar(c.vareps[:, 0:HALVES], c.mv[:, :, 1], LN_EPS, None, ALU.add).then_inc(var_ready, 1)
                v.wait_ge(rstd_ready, before + b + 1)
                for t in range(HALVES):
                    v.tensor_scalar(c.Y[:, half(b, t)], c.X[:, half(b, t)], c.mv[:, t, 0:1], c.rstd[:, t:t + 1],
                                    ALU.subtract, ALU.mult)
                step.end()


def add_back(nc, c):
    with nc.Block() as block:

        @block.vector
        def _(v):
            v.tensor_tensor(c.X[:, :], c.X[:, :], c.Y[:, :], ALU.add)




QK_CHUNKS = 4
CHUNKS = 3 * INNER // 512
ROTATED = HALVES * QK_CHUNKS
CHUNK_ORDER = [(0, 0), (0, 4), (0, 1), (0, 2), (0, 5), (0, 3), (1, 0), (1, 4), (1, 1), (1, 2), (1, 5), (1, 3)]
QK_ORDER = [x for x in CHUNK_ORDER if x[1] < QK_CHUNKS]
PE_XT_SLOT = 0
PE_CHUNK_SLOTS = {1 + j // 2: [j - j % 2, j - j % 2 + 1] for j in range(HALVES * CHUNKS)}
ACT_CHUNK_SLOTS = {1 + k: v for k, v in PE_CHUNK_SLOTS.items()}
DVE_ROTATE_SLOTS = {3 + m: m for m in range(ROTATED)}
DVE_RSQRT_SLOT = 11
PE_CTXT_SLOTS = {7: (0, 1), 8: (2, 3)}
COPY_CTXT_SLOTS = {8: (0, 1), 9: (2, 3)}
PE_OUT_SLOT, DVE_OUT_SLOT = 10, 12
PE_QKT_SLOTS = {12: (0, 1), 13: (2, 3), 14: (4, 5), 15: (6, 7)}
COPY_QKT_SLOTS = {12: (0,), 13: (1, 2), 14: (3, 4), 15: (5, 6, 7)}
SPAN = (P, P + WINDOW)
AT = (0, P)
FIRST_KEY = (0, P - WINDOW)
GROUPS_OF_2 = NH // 2


def windowed_transformers(nc, sem, c, name, io):
    w = io[name]
    names = ("attn_weights", "ff_weights", "tables_loaded", "tables_ready", "attn_added", "ff_added", "steps",
             "row_copied", "rowT_in_psum", "xT_ready", "chunk_in_psum", "chunk_copied", "chunk_squared",
             "chunk_rotated", "sum_ready", "rs_ready", "first_half_scaled", "second_half_scaled", "qkT_in_psum",
             "qT_copied", "kT_copied", "scores_ready", "negmax_ready", "probs_ready", "probsT_in_psum",
             "probsT_ready", "ctx_in_psum", "recip_ready", "ctx_ready", "ctxT_in_psum", "ctxT_by_scalar",
             "ctxT_by_vector", "out_in_psum", "shifted_in_psum", "shifted_ready", "kept_ready", "ff_in_psum",
             "gelu_ready", "hidden_ready", "ff_out_in_psum", "ff_steps")
    s = Chip()
    (s.attn_weights, s.ff_weights, tables_loaded, s.tables_ready, s.attn_added, s.ff_added, s.steps,
     s.row_copied, s.rowT_in_psum, s.xT_ready, s.chunk_in_psum, s.chunk_copied, s.chunk_squared,
     s.chunk_rotated, s.sum_ready, s.rs_ready, s.first_half_scaled, s.second_half_scaled, s.qkT_in_psum,
     s.qT_copied, s.kT_copied, s.scores_ready, s.negmax_ready, s.probs_ready, s.probsT_in_psum,
     s.probsT_ready, s.ctx_in_psum, s.recip_ready, s.ctx_ready, s.ctxT_in_psum, s.ctxT_by_scalar,
     s.ctxT_by_vector, s.out_in_psum, s.shifted_in_psum, s.shifted_ready, s.kept_ready, s.ff_in_psum,
     s.gelu_ready, s.hidden_ready, s.ff_out_in_psum, ff_steps) = [sem(name + "_" + n) for n in names]
    ff_norm = Norm(c, None, (c.cols[:, 0:1], c.cols[:, 1:2]), "window_norm", 0)
    wqkv, wo = c.wA[:, :], c.wB[:, :]
    w1, w2 = c.wC[:, :], c.wD[:, :]
    n_attn, n_ff = 16 * 3, 16 * 3
    vn, tn = HALVES * NH * (DH + 1), 8 * S
    V = (c.V, c.big[:, 0:vn].rearrange("p (t h e) -> p t h e", t=HALVES, h=NH))
    qT = (c.qT, c.big[:, vn:vn + tn].rearrange("p (k s) -> p k s", k=8))
    kT = (c.kT, c.big[:, vn + tn:vn + 2 * tn].rearrange("p (k s) -> p k s", k=8))
    ctx = (c.ctx, c.ctx2)
    bands = ((c.band0[:, :]), (c.band1[:, :]))
    blocks = ((0, 0, 0, P, 0, 0), (1, 1, 0, P, P + WINDOW, P), (1, 0, P - WINDOW, WINDOW, P, 2 * P))

    def scale_half(eng, t):
        both = c.qk[:, t, :, :].rearrange("p w (h d) -> p (w h) d", d=DH)
        return eng.tensor_tensor(both, both, c.rs[:, 0, t, :].unsqueeze(2).broadcast_to((P, 2 * NH, DH)), ALU.mult)

    def part_of(buffer, pp):
        return buffer[:, 2 * pp:2 * pp + 2, :].rearrange("p k s -> p (k s)")



    def pe_scores(pe, turn, j, h):
        if h % 4 == 0:
            pe.wait_ge(s.qT_copied, turn * 4 + h // 4 + 1)
            pe.wait_ge(s.kT_copied, turn * 4 + h // 4 + 1)
        row0 = DH * (h % 2)
        q, k, out = qT[j][row0:row0 + DH, h // 2, :], kT[j][row0:row0 + DH, h // 2, :], c.bank[h % 2]
        for t in range(HALVES):
            dst = out[:, AT[t]:AT[t] + SPAN[t]]
            pe.matmul(dst, q[:, t * P:(t + 1) * P], k[:, FIRST_KEY[t]:FIRST_KEY[t] + SPAN[t]], start=True, stop=False,
                      skip_group_check=True)
            last = pe.matmul(dst, c.identb[:, :], bands[t], start=False, stop=True, skip_group_check=True)
        last.then_inc(s.scores_ready, 1)

    def pe_turn_probs(pe, turn, h):
        pe.wait_ge(s.probs_ready, turn * NH + h + 1)
        for (tq, tk, k0, kn, at, to) in blocks:
            last = pe.transpose(c.bank[2 + h % 2][0:kn, to:to + P], c.probs[:, h % 2, at:at + kn], c.ident[:, :])
        last.then_inc(s.probsT_in_psum, 1)

    def pe_weigh(pe, turn, j, h, first):
        group, w = h // 2, DH + 1
        pe.wait_ge(s.probsT_ready, turn * NH + h + 1)
        if h % 2 == 0 and not (first and group < 2):
            pe.wait_ge(s.ctx_ready, turn * GROUPS_OF_2 + group - 1)
        out = c.bank[4 + group % 2]
        for t in range(HALVES):
            mine = [x for x in blocks if x[0] == t]
            o = (t * 2 + h % 2) * w
            for i, (tq, tk, k0, kn, at, to) in enumerate(mine):
                last = pe.matmul(out[:, o:o + w], c.probsT[k0:k0 + kn, h % 2, to:to + P], V[j][k0:k0 + kn, tk, h, :],
                                 start=(i == 0), stop=(i == len(mine) - 1))
        if h % 2 == 1:
            last.then_inc(s.ctx_in_psum, 1)

    def pe_prepare(pe, q, slot, alone=False, start=False):
        if slot == PE_XT_SLOT:
            pe.wait_ge(s.row_copied, q + 1)
            if not alone:
                pe.wait_ge(s.qT_copied, q * 4)
                pe.wait_ge(s.kT_copied, q * 4)
            for t in range(HALVES):
                last = pe.transpose(c.bank[6][:, t * P:(t + 1) * P], c.xn[:, t, :], c.ident[:, :])
            last.then_inc(s.rowT_in_psum, 1)
        for i in PE_CHUNK_SLOTS.get(slot, ()):
            t, k = CHUNK_ORDER[i]
            if i == 0:
                pe.wait_ge(s.xT_ready, q + 1)
            if i >= 2:
                pe.wait_ge(s.chunk_copied, q * len(CHUNK_ORDER) + i - 1)
            pe.matmul(c.bank[7 - i % 2][:, :], c.xT[:, t * P:(t + 1) * P], wqkv[:, k * 512:(k + 1) * 512], start=True,
                      stop=True).then_inc(s.chunk_in_psum, 1)
        for i in PE_QKT_SLOTS.get(slot, ()):
            if i == 0:
                pe.wait_ge(s.first_half_scaled, q + 1)
                pe.wait_ge(s.second_half_scaled, q + 1)
                pe.wait_ge(s.chunk_copied, (q + 1) * len(CHUNK_ORDER))
            elif i >= 2:
                pe.wait_ge((s.qT_copied, s.kT_copied)[i % 2], q * 4 + i // 2)
            which, pp = i % 2, i // 2
            if i == 1 and not start:
                pe.wait_ge(s.attn_added, q)
            for k in range(2):
                for t in range(HALVES):
                    at = (2 * pp + k) * P
                    last = pe.transpose(c.bank[6 + i % 2][:, (2 * k + t) * P:(2 * k + t + 1) * P],
                                        c.qk[:, t, which, at:at + P], c.ident[:, :])
            last.then_inc(s.qkT_in_psum, 1)

    def pe_finish(pe, turn, j, slot, alone=False):
        for i in PE_CTXT_SLOTS.get(slot, ()):
            if i == 0:
                pe.wait_ge(s.ctx_ready, (turn + 1) * GROUPS_OF_2)
                if not alone:
                    pe.wait_ge(s.chunk_copied, (turn + 3) * len(CHUNK_ORDER))
            elif i >= 2:
                pe.wait_ge((s.ctxT_by_scalar, s.ctxT_by_vector)[i % 2], turn * 2 + i // 2)
            for k in range(2):
                for t in range(HALVES):
                    at = (2 * i + k) * P
                    last = pe.transpose(c.bank[7 - i % 2][:, (2 * k + t) * P:(2 * k + t + 1) * P],
                                        ctx[j][:, t, at:at + P], c.ident[:, :])
            last.then_inc(s.ctxT_in_psum, 1)
        if slot == PE_OUT_SLOT:
            pe.wait_ge(s.ctxT_by_scalar, (turn + 1) * 2)
            pe.wait_ge(s.ctxT_by_vector, (turn + 1) * 2)
            for t in range(HALVES):
                for k in range(8):
                    last = pe.matmul(c.bank[7][:, t * D:(t + 1) * D], c.ctxT[:, k, t * P:(t + 1) * P],
                                     wo[:, k * D:(k + 1) * D], start=(k == 0), stop=(k == 7))
            last.then_inc(s.out_in_psum, 1)

    def pe_window(pe, turn, j, first=False, last=False):
        for h in range(NH):
            pe_turn_probs(pe, turn, h)
            if h + 2 < NH:
                pe_scores(pe, turn, j, h + 2)
            elif not last:
                pe_scores(pe, turn + 1, 1 - j, h + 2 - NH)
            if h >= 1:
                pe_weigh(pe, turn, j, h - 1, first)
            elif not first:
                pe_weigh(pe, turn - 1, 1 - j, NH - 1, False)
            if not first:
                pe_finish(pe, turn - 1, 1 - j, h, last)
            if not last:
                pe_prepare(pe, turn + 1, h, False, first)
        if last:
            pe_weigh(pe, turn, j, NH - 1, False)
            for slot in range(NH):
                pe_finish(pe, turn, j, slot, True)


    def pool_prepare(g, q, b):
        g.tensor_copy(c.xn[:, :, :].rearrange("p t d -> p (t d)"), c.Y[:, row(b)]).then_inc(s.row_copied, 1)
        for m in range(ROTATED + 1):
            if m < ROTATED:
                i = CHUNK_ORDER.index(QK_ORDER[m])
                g.wait_ge(s.chunk_copied, q * len(CHUNK_ORDER) + i + 1)
                if m >= 2:
                    g.wait_ge(s.chunk_rotated, q * ROTATED + m - 1)
                g.tensor_tensor(c.sq[:, m % 2, :], c.raw[:, m % 4, :], c.raw[:, m % 4, :],
                                ALU.mult).then_inc(s.chunk_squared, 1)
            if m >= 1:
                t, k = QK_ORDER[m - 1]
                g.wait_ge(s.chunk_rotated, q * ROTATED + m)
                g.tensor_tensor(c.qk[:, t, k // 2, (k % 2) * 512:(k % 2) * 512 + 512], c.turnA[:, (m - 1) % 2, :],
                                c.turnB[:, (m - 1) % 2, :], ALU.add).then_inc(s.sum_ready, 1)
        g.wait_ge(s.rs_ready, q + 1)
        g.wait_ge(s.sum_ready, (q + 1) * ROTATED)
        scale_half(g, 0).then_inc(s.first_half_scaled, 1)


    def act_probs(a, turn, h):
        a.wait_ge(s.negmax_ready, turn * NH + h + 1)
        for t in range(HALVES):
            last = a.activation(c.probs[:, h % 2, AT[t]:AT[t] + SPAN[t]], c.bank[h % 2][:, AT[t]:AT[t] + SPAN[t]],
                                ACT.Exp, bias=c.negmax[:, h, t:t + 1])
        last.then_inc(s.probs_ready, 1)

    def act_copy_probs(a, turn, h):
        a.wait_ge(s.probsT_in_psum, turn * NH + h + 1)
        k0, kn, to = blocks[2][2:4] + blocks[2][5:6]
        a.activation(c.probsT[:, h % 2, 0:2 * P], c.bank[2 + h % 2][:, 0:2 * P], ACT.Identity)
        a.activation(c.probsT[k0:k0 + kn, h % 2, to:to + P], c.bank[2 + h % 2][0:kn, to:to + P],
                     ACT.Identity).then_inc(s.probsT_ready, 1)

    def act_prepare(a, q, j, slot):
        hi = D // 2
        if slot == PE_XT_SLOT:
            a.wait_ge(s.rowT_in_psum, q + 1)
            a.activation(c.xT[0:hi, :], c.bank[6][0:hi, 0:S], ACT.Identity)
            a.activation(c.xT[hi:D, 0:1], c.bank[6][hi:D, 0:1], ACT.Copy, scale=0.0)
            a.activation(c.xT[hi:D, 1:S], c.bank[6][hi:D, 0:S - 1], ACT.Identity).then_inc(s.xT_ready, 1)
        for i in ACT_CHUNK_SLOTS.get(slot, ()):
            t, k = CHUNK_ORDER[i]
            a.wait_ge(s.chunk_in_psum, q * len(CHUNK_ORDER) + i + 1)
            src = c.bank[7 - i % 2][:, :]
            if k < QK_CHUNKS:
                m = QK_ORDER.index((t, k))
                if m >= 4:
                    a.wait_ge(s.chunk_rotated, q * ROTATED + m - 3)
                last = a.activation(c.raw[:, m % 4, :], src, ACT.Identity)
            else:
                h0 = 8 * (k - QK_CHUNKS)
                last = a.activation(V[j][:, t, h0:h0 + 8, 0:DH], src.rearrange("p (h d) -> p h d", h=8), ACT.Identity)
            last.then_inc(s.chunk_copied, 1)
        for i in COPY_QKT_SLOTS.get(slot, ()):
            if i % 2 == 0:
                a.wait_ge(s.qkT_in_psum, q * 8 + i + 1)
                a.activation(part_of(qT[j], i // 2), c.bank[6][:, :], ACT.Identity).then_inc(s.qT_copied, 1)

    def act_finish(a, turn, slot):
        for i in COPY_CTXT_SLOTS.get(slot, ()):
            if i % 2 == 0:
                a.wait_ge(s.ctxT_in_psum, turn * 4 + i + 1)
                a.activation(part_of(c.ctxT, i), c.bank[7][:, :], ACT.Identity).then_inc(s.ctxT_by_scalar, 1)

    def act_window(a, turn, j, first=False, last=False):
        for h in range(NH):
            if h + 1 < NH:
                act_probs(a, turn, h + 1)
            elif not last:
                act_probs(a, turn + 1, 0)
            act_copy_probs(a, turn, h)
            if not first:
                act_finish(a, turn - 1, h)
            if not last:
                act_prepare(a, turn + 1, 1 - j, h)
        if last:
            for slot in range(NH):
                act_finish(a, turn, slot)


    def dve_negmax(v, turn, h):
        v.wait_ge(s.scores_ready, turn * NH + h + 1)
        for t in range(HALVES):
            last = v.tensor_reduce(c.negmax[:, h, t:t + 1], c.bank[h % 2][:, AT[t]:AT[t] + SPAN[t]], AX, ALU.max,
                                   negate=True)
        last.then_inc(s.negmax_ready, 1)

    def dve_normalise(v, turn, j, group):
        w = DH + 1
        v.wait_ge(s.ctx_in_psum, turn * GROUPS_OF_2 + group + 1)
        src = c.bank[4 + group % 2][:, 0:4 * w].rearrange("p (n w) -> p n w", n=4)
        rec = c.recip[:, group % 2, 0:4]
        v.reciprocal(rec, src[:, :, w - 1]).then_inc(s.recip_ready, 1)
        v.wait_ge(s.recip_ready, turn * GROUPS_OF_2 + group + 1)
        dst = ctx[j][:, :, 2 * group * DH:(2 * group + 2) * DH].rearrange("p t (h d) -> p t h d", h=2)
        v.tensor_tensor(dst, src[:, :, 0:DH].rearrange("p (t h) d -> p t h d", t=HALVES),
                        rec.rearrange("p (t h) -> p t h", t=HALVES).unsqueeze(3).broadcast_to((P, HALVES, 2, DH)),
                        ALU.mult).then_inc(s.ctx_ready, 1)

    def dve_prepare(v, step, q, j, slot):
        if slot in DVE_ROTATE_SLOTS:
            m = DVE_ROTATE_SLOTS[slot]
            t, k = QK_ORDER[m]
            v.wait_ge(s.chunk_squared, q * ROTATED + m + 1)
            v.tensor_reduce(c.ss[:, t, 8 * k:8 * k + 8], c.sq[:, m % 2, :].rearrange("p (h d) -> p h d", h=8), AX,
                            ALU.add)
            if m >= 2:
                v.wait_ge(s.sum_ready, q * ROTATED + m - 1)
            tab = 2 * (k // 2)
            rotate(v, c.raw[:, m % 4, :].rearrange("p (h d) -> p h d", h=8), c.turnA[:, m % 2, :],
                   c.turnB[:, m % 2, :], 8, DH, c.ropes[:, tab, t, :], c.ropes[:, tab + 1, t, :]
                   ).then_inc(s.chunk_rotated, 1)
        if slot == DVE_RSQRT_SLOT:
            v.wait_ge(s.chunk_rotated, (q + 1) * ROTATED)
            ss = c.ss[:, :, :].rearrange("p t h -> p (t h)")
            step.after(v.tensor_scalar(ss, ss, 1e-24, None, ALU.max))
            rsqrt(v, step, c, ss, c.rs[:, 0, :, :].rearrange("p t h -> p (t h)"))
            v.memset(c.recip[:, 0, 31:32], 0.0).then_inc(s.rs_ready, 1)
            v.wait_ge(s.sum_ready, (q + 1) * ROTATED)
            scale_half(v, 1).then_inc(s.second_half_scaled, 1)
        for i in COPY_QKT_SLOTS.get(slot, ()):
            if i % 2 == 1:
                v.wait_ge(s.qkT_in_psum, q * 8 + i + 1)
                v.tensor_copy(part_of(kT[j], i // 2), c.bank[7][:, :]).then_inc(s.kT_copied, 1)

    def dve_finish(v, turn, b, slot):
        for i in COPY_CTXT_SLOTS.get(slot, ()):
            if i % 2 == 1:
                v.wait_ge(s.ctxT_in_psum, turn * 4 + i + 1)
                v.tensor_copy(part_of(c.ctxT, i), c.bank[6][:, :]).then_inc(s.ctxT_by_vector, 1)
        if slot == DVE_OUT_SLOT:
            v.wait_ge(s.out_in_psum, turn + 1)
            v.tensor_tensor(c.Y[:, row(b)], c.Y[:, row(b)], c.bank[7][:, 0:S], ALU.add).then_inc(s.attn_added, 1)

    def dve_steps(v, q):
        return Steps(v, s.steps, q, 1 + NEWTON_STEPS)

    def dve_window(v, turn, b, j, first=False, last=False):
        step = None if last else dve_steps(v, turn + 1)
        for h in range(NH):
            if h + 1 < NH:
                dve_negmax(v, turn, h + 1)
            elif not last:
                dve_negmax(v, turn + 1, 0)
            if h % 2 == 1 and h >= 3:
                dve_normalise(v, turn, j, (h - 3) // 2)
            elif h == 1 and not first:
                dve_normalise(v, turn - 1, 1 - j, GROUPS_OF_2 - 1)
            if not first:
                dve_finish(v, turn - 1, b - 1, h)
            if not last:
                dve_prepare(v, step, turn + 1, 1 - j, h)
        if last:
            dve_normalise(v, turn, j, GROUPS_OF_2 - 1)
            for slot in range(NH):
                dve_finish(v, turn, b, slot)
        else:
            step.end()

    def run(number):
        layer0, layer1 = number * DEPTH, (number + 1) * DEPTH
        with nc.Block() as block:

            @block.sync
            def _(sp):
                sp.dma_start(c.rope[:, :, :, 0:DH], w["rope"]).then_inc(tables_loaded, 16)
                with sp.Fori(layer0, layer1) as d:
                    sp.wait_ge(s.attn_added, d * B + 1)
                    sp.dma_start(wqkv, w["wqkv"][bass.ds(d, 1)].rearrange("a p n -> (a p) n")).then_inc(s.attn_weights, 16)
                    sp.dma_start(wo, w["wo"][bass.ds(d, 1)].rearrange("a p n -> (a p) n")).then_inc(s.attn_weights, 16)
                    sp.dma_start(c.scl[:, :, :].rearrange("p a b -> p (a b)"),
                                 w["scales"][bass.ds(d, 1)].rearrange("a n -> (a n)").partition_broadcast(P)).then_inc(s.attn_weights, 16)
                    sp.wait_ge(s.ff_added, d * B + 1)
                    sp.dma_start(w1, w["w1"][bass.ds(d, 1)].rearrange("a p n -> (a p) n")).then_inc(s.ff_weights, 16)
                    sp.dma_start(w2, w["w2"][bass.ds(d, 1)].rearrange("a p n -> (a p) n")).then_inc(s.ff_weights, 16)
                    sp.dma_start(c.cols[:, 0:8], w["cols"][bass.ds(d, 1)].rearrange("a p n -> (a p) n")).then_inc(s.ff_weights, 16)
                sp.wait_ge(s.attn_weights, n_attn * layer1)
                sp.wait_ge(s.ff_weights, n_ff * layer1)

            @block.tensor
            def _(pe):
                with pe.Fori(layer0, layer1) as d:
                    turn = d * B
                    pe.wait_ge(s.attn_weights, d * n_attn + n_attn)
                    for slot in range(NH):
                        pe_prepare(pe, turn, slot, True, True)
                    pe_scores(pe, turn, 0, 0)
                    pe_scores(pe, turn, 0, 1)
                    pe_window(pe, turn, 0, first=True)
                    with pe.Fori(0, B // 2 - 1) as pair:
                        pe_window(pe, turn + pair * 2 + 1, 1)
                        pe_window(pe, turn + pair * 2 + 2, 0)
                    pe_window(pe, turn + B - 1, 1, last=True)
                    with pe.Fori(0, B) as b:
                        turn = d * B + b
                        pe.wait_ge(s.ff_weights, d * n_ff + n_ff)
                        pe.wait_ge(s.attn_added, turn + 2)
                        hi = D // 2
                        for t in range(HALVES):
                            last = pe.matmul(c.bank[6][:, t * hi:(t + 1) * hi], c.shift[:, :],
                                             c.Y[:, bass.ds(b * ROW + t * D + hi, hi)], start=True, stop=(t == 0))
                            if t == 1:
                                last = pe.matmul(c.bank[6][:, t * hi:(t + 1) * hi], c.carry[:, :],
                                                 c.Y[:, bass.ds(b * ROW + hi, hi)], start=False, stop=True)
                        last.then_inc(s.shifted_in_psum, 1)
                        ff_norm.tensor(pe, turn)
                        for k, (at, n) in enumerate(FF_CHUNKS):
                            for side in range(2):
                                last = pe.matmul(c.bank[k][0:n, side * S:(side + 1) * S],
                                                 w1[:, side * FF + at:side * FF + at + n], c.xT[:, :], start=True, stop=True)
                            last.then_inc(s.ff_in_psum, 1)
                        pe.wait_ge(s.hidden_ready, (turn + 1) * 3)
                        for t in range(HALVES):
                            for k, (at, n) in enumerate(FF_CHUNKS):
                                m = n + (k == 2)
                                last = pe.matmul(c.bank[7][:, t * D:(t + 1) * D], c.hT[0:m, k, t * P:(t + 1) * P],
                                                 w2[0:m, k * D:(k + 1) * D], start=(k == 0), stop=(k == 2))
                        last.then_inc(s.ff_out_in_psum, 1)

            @block.gpsimd
            def _(g):
                with g.Fori(layer0, layer1) as d:
                    with g.Fori(0, B) as b:
                        g.wait_ge(s.ff_added, d * B + 1)
                        pool_prepare(g, d * B + b, b)
                    with g.Fori(0, B) as b:
                        turn = d * B + b
                        g.wait_ge(s.attn_added, turn + 2)
                        g.wait_ge(s.ff_added, turn + 1)
                        hi = D // 2
                        g.tensor_copy(c.xn[:, :, 0:hi],
                                      c.Y[:, row(b)].rearrange("p (t d) -> p t d", t=HALVES)[:, :, 0:hi]).then_inc(s.kept_ready, 1)
                        ff_norm.pool(g, turn)

            @block.scalar
            def _(a):
                hi = D // 2
                with a.Fori(layer0, layer1) as d:
                    a.activation(c.cols[:, 30:31], c.neg_half[:, 0:1], ACT.Exp)
                    turn = d * B
                    for slot in range(NH):
                        act_prepare(a, turn, 0, slot)
                    act_probs(a, turn, 0)
                    act_window(a, turn, 0, first=True)
                    with a.Fori(0, B // 2 - 1) as pair:
                        act_window(a, turn + pair * 2 + 1, 1)
                        act_window(a, turn + pair * 2 + 2, 0)
                    act_window(a, turn + B - 1, 1, last=True)
                    a.wait_ge(s.ff_weights, d * n_ff + n_ff)
                    a.activation(c.cols[:, 30:31], c.neg_half[:, 0:1], ACT.Gelu)
                    with a.Fori(0, B) as b:
                        turn = d * B + b
                        a.wait_ge(s.shifted_in_psum, turn + 1)
                        a.activation(c.xn[:, :, hi:D], c.bank[6][:, 0:D].rearrange("p (t d) -> p t d", t=HALVES),
                                     ACT.Identity).then_inc(s.shifted_ready, 1)
                        ff_norm.scalar(a, turn)
                        for k, (at, n) in enumerate(FF_CHUNKS):
                            a.wait_ge(s.ff_in_psum, turn * 3 + k + 1)
                            a.activation(c.probs[0:n, :, :].rearrange("p a b -> p (a b)")[:, k * S:(k + 1) * S],
                                         c.bank[k][0:n, S:2 * S], ACT.Gelu,
                                         bias=c.cols[0:n, 5 + k:6 + k]).then_inc(s.gelu_ready, 1)

            @block.vector
            def _(v):
                if number == 0:
                    v.sem_inc(s.attn_added, 1)
                    v.sem_inc(s.ff_added, 1)
                v.wait_ge(tables_loaded, 16 * (number + 1))
                v.memset(c.recip[:, 0, 31:32], 0.0)
                v.memset(V[1][:, :, :, :], 1.0)
                with v.Fori(layer0, layer1) as d:
                    v.wait_ge(s.attn_weights, d * n_attn + n_attn)
                    v.tensor_tensor(c.ropes[:, :, :, :], c.rope[:, :, :, 0:DH],
                                    c.scl[:, :, :].unsqueeze(2).broadcast_to((P, 4, HALVES, DH)),
                                    ALU.mult).then_inc(s.tables_ready, 1)
                    v.wait_ge(s.tables_ready, d + 1)
                    turn = d * B
                    step = dve_steps(v, turn)
                    for slot in range(NH):
                        dve_prepare(v, step, turn, 0, slot)
                    step.end()
                    dve_negmax(v, turn, 0)
                    dve_window(v, turn, 0, 0, first=True)
                    with v.Fori(0, B // 2 - 1) as pair:
                        dve_window(v, turn + pair * 2 + 1, pair * 2 + 1, 1)
                        dve_window(v, turn + pair * 2 + 2, pair * 2 + 2, 0)
                    dve_window(v, turn + B - 1, B - 1, 1, last=True)
                    with v.Fori(0, B) as b:
                        turn = d * B + b
                        v.wait_ge(s.ff_weights, d * n_ff + n_ff)
                        step = Steps(v, ff_steps, turn, LN_STEPS)
                        v.wait_ge(s.shifted_ready, turn + 1)
                        v.wait_ge(s.kept_ready, turn + 1)
                        ff_norm.vector(v, b, step, turn)
                        for k, (at, n) in enumerate(FF_CHUNKS):
                            v.wait_ge(s.gelu_ready, turn * 3 + k + 1)
                            v.scalar_tensor_tensor(out=c.hT[0:n, k, :], in0=c.bank[k][0:n, 0:S],
                                                   scalar=c.cols[0:n, 2 + k:3 + k],
                                                   in1=c.probs[0:n, :, :].rearrange("p a b -> p (a b)")[:, k * S:(k + 1) * S],
                                                   op0=ALU.add, op1=ALU.mult).then_inc(s.hidden_ready, 1)
                        v.wait_ge(s.ff_out_in_psum, turn + 1)
                        v.tensor_tensor(c.Y[:, row(b)], c.Y[:, row(b)], c.bank[7][:, 0:S], ALU.add).then_inc(s.ff_added, 1)
                        step.end()

    return run


def store(nc, sem, c, io):
    stored = sem("stored")
    with nc.Block() as block:

        @block.sync
        def _(sp):
            for b in range(B):
                sp.dma_start(io["out"][b].rearrange("(t p) d -> p t d", p=P),
                             c.X[:, b * ROW:(b + 1) * ROW].rearrange("p (t d) -> p t d", t=HALVES)).then_inc(stored, 16)
            sp.wait_ge(stored, 16 * B)


STOP = 99


def program(nc, io):
    with ExitStack() as ctx:
        c = allocate(nc, ctx)

        def sem(name):
            return ctx.enter_context(nc.semaphore(name))

        c.shared = Shared(sem)
        setup(nc, sem, c, io)

        transformer = windowed_transformers(nc, sem, c, "wt", io)

        def layer_on_Y(body):
            norm_rows(nc, c)
            body()
            add_back(nc, c)

        def last_block():
            plain_attention(nc, sem, c, "a3", io, c.Y, False, True)
            experts(nc, sem, c, "e3", io, c.Y, False)

        parts = [
            lambda: plain_attention(nc, sem, c, "a0", io, c.X, True, False),
            lambda: experts(nc, sem, c, "e0", io, c.X, True),
            lambda: linear_attention(nc, sem, c, "l1", io, c.X),
            lambda: layer_on_Y(lambda: transformer(0)),
            lambda: rotary_attention(nc, sem, c, "r2", io, c.X),
            lambda: layer_on_Y(lambda: transformer(1)),
            lambda: latent_attention(nc, sem, c, "m3", io, c.X),
            lambda: layer_on_Y(last_block),
        ]
        for part in parts[:STOP]:
            part()
        store(nc, sem, c, io)




def _heads_apart(w, np):
    out = np.zeros((w.shape[0], NH, 32), w.dtype)
    out[:, :, 0:HD] = w.reshape(w.shape[0], NH, HD)
    return out.reshape(w.shape[0], NH * 32)


def kernel(**inputs):
    import numpy as np
    import concourse.bacc as bacc
    from concourse.bass_utils import run_bass_kernel_spmd

    a = {k: np.ascontiguousarray(v) for k, v in inputs.items()}
    nc = bacc.Bacc("TRN2", target_bir_lowering=False, num_devices=1)
    arrays = {}

    def give(name, array):
        array = np.ascontiguousarray(array)
        name = "in_" + name
        arrays[name] = array
        return nc.dram_tensor(name, array.shape, mybir.dt.from_np(array.dtype), kind="ExternalInput").ap()

    def plain(name, wq, wk, wv, wo, bq, bk, bv, bo, g=None, bln=None):
        cols = np.zeros((P, 10), np.float32)
        cols[:, 0:4] = _heads_apart(bq[None], np).reshape(4, P).T
        cols[:, 4:8] = _heads_apart(bk[None], np).reshape(4, P).T
        if g is not None:
            cols[:, 8], cols[:, 9] = g, bln
        return {"wq": give(name + "_wq", _heads_apart(wq, np)), "wk": give(name + "_wk", _heads_apart(wk, np)),
                "wv": give(name + "_wv", wv), "wo": give(name + "_wo", wo), "cols": give(name + "_cols", cols),
                "bv": give(name + "_bv", bv), "bo": give(name + "_bo", bo)}

    def chunks(w, n, m):
        return w.reshape(n, P, m).transpose(1, 0, 2).reshape(P, n * m)

    def halves(t):
        return t.reshape(HALVES, P, -1).transpose(1, 0, 2)

    f32 = np.float32
    hd = np.arange(0, DH, 2, dtype=f32)
    inv_freq = (f32(1.0) / np.power(f32(10000.0), hd / f32(DH))).astype(f32)
    tok = np.arange(S, dtype=f32)
    fr = tok[:, None] * inv_freq[None, :]
    cos, sin = np.cos(fr).astype(f32), np.sin(fr).astype(f32)
    base = ((hd + f32(0.4 * DH)) / f32(1.4 * DH)).astype(f32)
    power = ((tok - S // 2) / (WINDOW // 2)).astype(f32)
    sc = np.power(base[None, :], power[:, None]).astype(f32)
    inv = (f32(1.0) / sc).astype(f32)
    tabs = []
    for m in (sc * f32(8.0), inv):
        tabs.append(np.concatenate([cos * m, cos * m], 1))
        tabs.append(np.concatenate([-(sin * m), sin * m], 1))
    window_rope = np.stack([halves(t) for t in tabs], 1).astype(f32)
    i = np.arange(D // 2, dtype=f32)
    ang = tok[:, None] * np.power(f32(10000.0), (f32(-2.0) * (i - f32(1.0)) / f32(D))).astype(f32)[None, :]
    c2, s2 = np.cos(ang).astype(f32), np.sin(ang).astype(f32)
    wide_rope = np.stack([halves(np.concatenate([c2, c2], 1)), halves(np.concatenate([s2, -s2], 1))], 1).astype(f32)

    def windowed(p):
        def swap(x):
            return np.concatenate([x[:, DH // 2:], x[:, :DH // 2]], 1)

        qs, ks = a[p + "q_scale"], a[p + "k_scale"]
        w1, w2, b1 = a[p + "W1"], a[p + "W2"], a[p + "b1"]
        w2p = np.zeros((DEPTH, P, 3, D), f32)
        cols = np.zeros((DEPTH, P, 8), f32)
        cols[:, :, 0], cols[:, :, 1] = a[p + "ln_g"], a[p + "ln_b"]
        for k, (at, n) in enumerate(FF_CHUNKS):
            w2p[:, 0:n, k] = w2[:, at:at + n]
            cols[:, 0:n, 2 + k] = b1[:, at:at + n]
            cols[:, 0:n, 5 + k] = b1[:, FF + at:FF + at + n]
        w2p[:, FF_CHUNKS[2][1], 2] = a[p + "b2"]
        return (a[p + "Wqkv"], a[p + "Wo"].reshape(DEPTH, 8, P, D).transpose(0, 2, 1, 3).reshape(DEPTH, P, 8 * D),
                np.concatenate([qs, swap(qs), ks, swap(ks)], 1), w1, w2p.reshape(DEPTH, P, 3 * D), cols)

    stacks = [np.concatenate(both) for both in zip(windowed("L1_ffn_"), windowed("L2_ffn_"))]
    window_io = {k: give("wt_" + k, v) for k, v in zip(("wqkv", "wo", "scales", "w1", "w2", "cols"), stacks)}
    window_io["rope"] = give("window_rope", window_rope)
    evens_first = np.concatenate([np.arange(0, D, 2), np.arange(1, D, 2)])
    wqkv1 = a["L1_attn_Wqkv"]
    tiles = np.zeros((P, 10, D), f32)
    m3 = {k: a["L3_attn_" + k] for k in ("W_DQ", "W_UQ", "W_DKV", "W_UKV", "W_QR", "W_KR", "W_O")}
    for n, t in enumerate((m3["W_DQ"], m3["W_UQ"].T, m3["W_DKV"], m3["W_UKV"][0:HD].T, m3["W_KR"], m3["W_QR"],
                           m3["W_UKV"][HD:2 * HD].T)):
        tiles[0:t.shape[0], n] = np.tile(t, (1, NH))
    tiles[:, 7] = np.tile(m3["W_O"].T, (NH, NH))
    eye = np.arange(D) // HD
    io = {
        "x": give("x", a["L0_attn_x"]),
        "headmask": give("headmask", (eye[:, None] == eye[None, :]).astype(np.float32)),
        "headcol": give("headcol", (eye[:, None] == np.arange(NH)[None, :]).astype(np.float32)),
        "a0": plain("a0", *[a["L0_attn_" + k] for k in ("Wq", "Wk", "Wv", "Wo", "bq", "bk", "bv", "bo")]),
    }
    io["e0"] = {"up": give("e0_up", a["L0_ffn_w1"].T), "side": give("e0_side", a["L0_ffn_v1"].T),
                "down": give("e0_down", chunks(a["L0_ffn_w2"], EXPERTS * 2, D)),
                "router": give("e0_router", a["L0_ffn_router_w"].T)}
    io["l1"] = {"wq": give("l1_wq", wqkv1[0:D].T), "wkv": give("l1_wkv", wqkv1[D:3 * D].T),
                "wp": give("l1_wp", a["L1_attn_Wproj"].T), "bp": give("l1_bp", a["L1_attn_bproj"])}
    io["wt"] = window_io
    io["r2"] = {"wqkv": give("r2_wqkv", np.concatenate([a["L2_attn_wq"].T[:, evens_first],
                                                        a["L2_attn_wk"].T[:, evens_first], a["L2_attn_wv"].T], 1)),
                "rope": give("r2_rope", wide_rope)}
    io["m3"] = {"tiles": give("m3_tiles", tiles),
                "norms": give("m3_norms", np.concatenate([a["L3_attn_q_norm_w"], a["L3_attn_k_norm_w"]]))}
    f = "L3_ffn_"
    io["a3"] = plain("a3", *[a[f + k] for k in ("wq", "wk", "wv", "wo", "bq", "bk", "bv", "bo", "ln1_g", "ln1_b")])
    io["e3"] = {"up": give("e3_up", a[f + "w1"].transpose(1, 0, 2).reshape(D, EXPERTS * 512)),
                "down": give("e3_down", chunks(a[f + "w2"].reshape(EXPERTS * 512, D), EXPERTS * 4, D)),
                "router": give("e3_router", a[f + "gate_w"]), "gate_b": give("e3_gate_b", a[f + "gate_b"]),
                "b1": give("e3_b1", a[f + "b1"].reshape(EXPERTS * 4, P).T), "b2": give("e3_b2", a[f + "b2"]),
                "ln": give("e3_ln", np.stack([a[f + "ln2_g"], a[f + "ln2_b"]], 1))}
    io["out"] = nc.dram_tensor("out", (B, S, D), F32, kind="ExternalOutput").ap()
    program(nc, io)
    result = run_bass_kernel_spmd(nc, [arrays], core_ids=[0])
    return result.results[0]["out"].reshape(B, S, D)
```

```python
import concourse.bass as bass
from concourse import mybir
from contextlib import ExitStack

F32 = mybir.dt.float32
I32 = mybir.dt.int32
BF16 = mybir.dt.bfloat16
ALU = mybir.AluOpType
ACT = mybir.ActivationFunctionType
AX = mybir.AxisListType.X

P = 128
B, S, D = 8, 256, 128
HALVES = S // P
ROW = S * D // P
NH = 16
HD = D // NH
DEPTH = 6
DH = 64
INNER = NH * DH
WINDOW = 32
FF = 341
FF_CHUNKS = [(0, 128), (128, 128), (256, 85)]
EXPERTS = 8
MASKED = -1e30
MAGIC = float(0x5F3759DF)
LN_EPS = 1e-5
RMS_EPS = 1.1920929e-07


def row(b, n=ROW, at=0):
    return bass.ds(b * n + at, n if at == 0 else n)


def half(b, t):
    return bass.ds(b * ROW + t * D, D)


class Steps:

    def __init__(self, eng, sem, turn, per_turn, before=0):
        self.eng, self.sem, self.turn, self.per_turn, self.n = eng, sem, turn, per_turn, 0
        self.before = before

    def after(self, instruction):
        self.n += 1
        instruction.then_inc(self.sem, 1)
        self.eng.wait_ge(self.sem, self.turn * self.per_turn + self.n + self.before)

    def end(self):
        assert self.n == self.per_turn, (self.n, self.per_turn)


class Shared:

    def __init__(self, sem):
        self.sem, self.kept, self.turns = sem, {}, {}

    def take(self, stage, names, turns):
        if stage not in self.kept:
            self.kept[stage], self.turns[stage] = [self.sem(stage + "_" + n) for n in names], 0
        before = self.turns[stage]
        self.turns[stage] += turns
        return self.kept[stage], before


class Chip:
    pass


def allocate(nc, ctx):
    c = Chip()

    def sb(name, shape, dt=F32):
        return ctx.enter_context(nc.sbuf_tensor(name, shape, dt))

    c.X = sb("X", [P, B * ROW])
    c.Y = sb("Y", [P, B * ROW])
    c.ident = sb("ident", [P, P])
    c.identb = sb("identb", [P, P], BF16)
    c.causal = sb("causal", [P, P], BF16)
    c.bands = sb("bands", [P, 2 * P + WINDOW], BF16)
    c.shift = sb("shift", [P, P])
    c.carry = sb("carry", [P, P])
    c.headmask = sb("headmask", [P, P])
    c.headcol = sb("headcol", [P, NH])
    c.iota8 = sb("iota8", [P, HALVES, EXPERTS])
    c.neg_half = sb("neg_half", [P, 64])
    c.stats = sb("stats", [P, HALVES, 6])
    c.mv = sb("mv", [P, HALVES, 2])
    c.vareps = sb("vareps", [P, 32])
    c.rstd = sb("rstd", [P, 32])
    c.xn = sb("xn", [P, HALVES, D])
    c.xT = sb("xT", [P, S])
    c.next_row = sb("next_row", [P, HALVES, D])
    c.next_rowT = sb("next_rowT", [P, S])
    c.qT = sb("qT", [P, 8, S])
    c.kT = sb("kT", [P, 8, S])
    c.V = sb("V", [P, HALVES, NH, DH + 1])
    c.one = sb("one", [P, 1])
    c.sums = sb("sums", [P, HALVES, NH])
    c.negmax = sb("negmax", [P, NH, HALVES])
    c.probs = sb("probs", [P, 2, 512])
    c.probsT = sb("probsT", [P, 2, 512])
    c.recip = sb("recip", [P, 2, 32])
    c.ctx = sb("ctx", [P, HALVES, INNER])
    c.ctx2 = sb("ctx2", [P, HALVES, INNER])
    c.raw = sb("raw", [P, 4, 512])
    c.ctxT = sb("ctxT", [P, 8, S])
    c.wA = sb("wA", [P, 3 * INNER])
    c.wB = sb("wB", [P, 8 * D])
    c.wC = sb("wC", [P, 2 * FF])
    c.wD = sb("wD", [P, 3 * D])
    c.rope = sb("rope", [P, 4, HALVES, 2 * DH])
    c.ropes = sb("ropes", [P, 4, HALVES, DH])
    c.scl = sb("scl", [P, 4, DH])
    c.cols = sb("cols", [P, 32])
    c.colsA = sb("colsA", [P, 8 * DEPTH])
    c.rows = sb("rows", [P, 4, D])
    c.big = sb("big", [P, 2 * EXPERTS * 512])
    c.sq = sb("sq", [P, 2, 512])
    c.turnA = sb("turnA", [P, 2, 512])
    c.turnB = sb("turnB", [P, 2, 512])
    c.qk = sb("qk", [P, HALVES, 2, INNER])
    c.ss = sb("ss", [P, HALVES, 32])
    c.rs = sb("rs", [P, 3, HALVES, 32])
    c.v1 = sb("v1", [P, HALVES, D + 4])
    c.kvblock = sb("kvblock", [P, D + NH])
    c.hT = sb("hT", [P, 3, S])
    c.onehotT = sb("onehotT", [EXPERTS, S])
    c.bottom = sb("bottom", [EXPERTS, D])
    c.ints = sb("ints", [P, 64], I32)
    c.newton = sb("newton", [P, 3, 64])
    c.small = sb("small", [P, 16, HALVES * EXPERTS])
    c.bank = [ctx.enter_context(nc.psum_tensor(f"bank{i}", [P, 512], F32)) for i in range(8)]
    return c




def setup(nc, sem, c, io):
    loaded, zeroed, built = sem("x_loaded"), sem("consts_zeroed"), sem("consts_built")
    with nc.Block() as block:

        @block.sync
        def _(sp):
            for b in range(B):
                sp.dma_start(c.X[:, b * ROW:(b + 1) * ROW].rearrange("p (t d) -> p t d", t=HALVES),
                             io["x"][b].rearrange("(t p) d -> p t d", p=P)).then_inc(loaded, 16)
            sp.dma_start(c.headmask[:, :], io["headmask"]).then_inc(loaded, 16)
            sp.dma_start(c.headcol[:, :], io["headcol"]).then_inc(loaded, 16)
            sp.wait_ge(loaded, 16 * (B + 2))

        @block.vector
        def _(v):
            for tile, value in ((c.ident, 0.0), (c.identb, 0.0), (c.causal, 0.0), (c.bands, 0.0),
                                (c.shift, 0.0), (c.carry, 0.0), (c.one, 1.0), (c.neg_half, -0.5)):
                last = v.memset(tile[:, :], value)
            v.memset(c.V[:, :, :, :], 1.0)
            v.memset(c.xT[:, :], 0.0)
            v.memset(c.v1[:, :, :], 1.0)
            v.memset(c.hT[:, :, :], 1.0)
            last = v.memset(c.probsT[:, :, :], 0.0)
            last.then_inc(zeroed, 1)

        @block.gpsimd
        def _(pool):
            pool.wait_ge(zeroed, 1)

            def where(tile, n, keep, base, mult, step, fill):
                return pool.affine_select(out=tile, in_=tile, pattern=[[step, n]], compare_op=keep, fill=fill,
                                          base=base, channel_multiplier=mult)

            where(c.ident[:, :], P, ALU.not_equal, 0, 1, -1, 1.0)
            where(c.identb[:, :], P, ALU.not_equal, 0, 1, -1, 1.0)
            where(c.shift[:, :], P, ALU.not_equal, 1, 1, -1, 1.0)
            where(c.carry[:, :], P, ALU.not_equal, 1 - P, 1, -P, 1.0)
            where(c.causal[:, :], P, ALU.is_ge, 0, 1, -1, MASKED)
            first_half, second_half = c.bands[:, 0:P], c.bands[:, P:2 * P + WINDOW]
            where(first_half, P, ALU.is_ge, 0, 1, -1, MASKED)
            other = where(second_half, P + WINDOW, ALU.is_ge, WINDOW, 1, -1, MASKED)
            other.then_inc(built, 1)
            pool.wait_ge(built, 1)
            where(first_half, P, ALU.is_ge, WINDOW, -1, 1, MASKED)
            where(second_half, P + WINDOW, ALU.is_ge, 0, -1, 1, MASKED)
            pool.iota(c.small[:, 0, :].bitcast(I32), pattern=[[0, HALVES], [1, EXPERTS]], base=0,
                      channel_multiplier=0).then_inc(built, 1)
            pool.wait_ge(built, 2)
            pool.tensor_copy(c.iota8[:, :, :], c.small[:, 0, :].bitcast(I32).rearrange("p (t e) -> p t e", t=HALVES))



LN_STEPS = 2


class Norm:

    def __init__(self, c, src, gain=None, stage="norm", turns=B, bank=6):
        self.c, self.src, self.gain, self.bank = c, src, gain, c.bank[bank]
        names = ("var_ready", "rstd_ready", "xn_ready", "xT_in_psum", "xT_ready")
        (self.var_ready, self.rstd_ready, self.xn_ready, self.xT_in_psum,
         self.xT_ready), self.before = c.shared.take(stage, names, turns)

    def source(self, b, t):
        if self.src is None:
            return self.c.xn[:, t, :]
        return self.src[:, half(b, t)]

    def vector(self, v, b, step, turn=None):
        c, turn = self.c, (b if turn is None else turn) + self.before
        for t in range(HALVES):
            last = v.bn_stats(c.stats[:, t, :], self.source(b, t))
        step.after(last)
        v.memset(c.vareps[:, 30:31], 0.0)
        for t in range(HALVES):
            last = v.bn_aggr(c.mv[:, t, :], c.stats[:, t, :])
        step.after(last)
        v.tensor_scalar(c.vareps[:, 0:HALVES], c.mv[:, :, 1], LN_EPS, None, ALU.add).then_inc(self.var_ready, 1)
        v.wait_ge(self.rstd_ready, turn + 1)
        for t in range(HALVES):
            last = v.tensor_scalar(c.xn[:, t, :], self.source(b, t), c.mv[:, t, 0:1], c.rstd[:, t:t + 1],
                                   ALU.subtract, ALU.mult)
        last.then_inc(self.xn_ready, 1)

    def pool(self, g, turn):
        c, turn = self.c, turn + self.before
        g.wait_ge(self.var_ready, turn + 1)
        g.tensor_tensor(c.rstd[:, 0:HALVES], c.vareps[:, 0:HALVES], c.neg_half[:, 0:HALVES],
                        ALU.pow).then_inc(self.rstd_ready, 1)

    def tensor(self, pe, turn):
        self.transpose(pe, turn)
        self.wait_transposed(pe, turn)

    def transpose(self, pe, turn):
        c, turn = self.c, turn + self.before
        pe.wait_ge(self.xn_ready, turn + 1)
        for t in range(HALVES):
            last = pe.transpose(self.bank[:, t * P:(t + 1) * P], c.xn[:, t, :], c.ident[:, :])
        last.then_inc(self.xT_in_psum, 1)

    def wait_transposed(self, pe, turn):
        pe.wait_ge(self.xT_ready, turn + self.before + 1)

    def scalar(self, a, turn):
        c, turn = self.c, turn + self.before
        a.wait_ge(self.xT_in_psum, turn + 1)
        if self.gain is None:
            last = a.activation(c.xT[:, :], self.bank[:, 0:S], ACT.Identity)
        else:
            last = a.activation(c.xT[:, :], self.bank[:, 0:S], ACT.Identity, scale=self.gain[0], bias=self.gain[1])
        last.then_inc(self.xT_ready, 1)




class Core:

    def __init__(self, c, heads, blocks, operands, values, width, per_ctx, stage, turns=B):
        self.c, self.heads, self.blocks = c, heads, blocks
        self.operands, self.values, self.width, self.per_ctx = operands, values, width, per_ctx
        names = ("qk_ready", "scores_ready", "negmax_ready", "probs_ready", "probsT_in_psum", "probsT_ready",
                 "ctx_in_psum", "recip_ready", "ctx_ready")
        (self.qk_ready, self.scores_ready, self.negmax_ready, self.probs_ready, self.probsT_in_psum,
         self.probsT_ready, self.ctx_in_psum, self.recip_ready,
         self.ctx_ready), self.before = c.shared.take(stage, names, turns)
        self.n_ctx = heads // per_ctx
        self.at, n = [], 0
        for t in range(HALVES):
            for (kt, k0, kn, mask) in blocks[t]:
                self.at.append((t, kt, k0, kn, n))
                n += kn
        self.used = n
        self.span = [sum(x[2] for x in blocks[t]) for t in range(HALVES)]

    def scores(self, pe, turn, h):
        c = self.c
        out = c.bank[h % 2]
        at = 0
        for t in range(HALVES):
            q, k = self.operands(h)
            first = self.blocks[t][0]
            k0 = first[0] * P + first[1]
            n = self.span[t]
            masks = [x for x in self.blocks[t] if x[3] is not None]
            last = pe.matmul(out[:, at:at + n], q[:, t * P:(t + 1) * P], k[:, k0:k0 + n], start=True,
                             stop=not masks, skip_group_check=True)
            if masks:
                mask, off = masks[0][3]
                last = pe.matmul(out[:, at + off:at + n], self.c.identb[:, :], mask, start=False, stop=True,
                                 skip_group_check=True)
            at += n
        last.then_inc(self.scores_ready, 1)

    def turn_probs(self, pe, turn, h):
        c = self.c
        pe.wait_ge(self.probs_ready, turn * self.heads + h + 1)
        for i, (t, kt, k0, kn, at) in enumerate(self.at):
            last = pe.transpose(c.bank[2 + h % 2][0:kn, i * P:(i + 1) * P], c.probs[:, h % 2, at:at + kn],
                                c.ident[:, :])
        last.then_inc(self.probsT_in_psum, 1)

    def weigh(self, pe, turn, h):
        c = self.c
        n, w = self.per_ctx, self.width
        group = h // n
        pe.wait_ge(self.probsT_ready, turn * self.heads + h + 1)
        if h % n == 0 and group >= 2:
            pe.wait_ge(self.ctx_ready, turn * self.n_ctx + group - 1)
        for t in range(HALVES):
            mine = [(i, x) for i, x in enumerate(self.at) if x[0] == t]
            o = (t * n + h % n) * w
            for j, (i, (_, kt, k0, kn, at)) in enumerate(mine):
                last = pe.matmul(c.bank[4 + group % 2][:, o:o + w], c.probsT[k0:k0 + kn, h % 2, i * P:(i + 1) * P],
                                 self.values(h, kt)[k0:k0 + kn, :], start=(j == 0), stop=(j == len(mine) - 1))
        if h % n == n - 1:
            last.then_inc(self.ctx_in_psum, 1)

    def tensor(self, pe, turn):
        turn = turn + self.before
        pe.wait_ge(self.qk_ready, turn + 1)
        self.scores(pe, turn, 0)
        if self.heads > 1:
            self.scores(pe, turn, 1)
        for h in range(self.heads):
            self.turn_probs(pe, turn, h)
            if h + 2 < self.heads:
                self.scores(pe, turn, h + 2)
            if h >= 1:
                self.weigh(pe, turn, h - 1)
        self.weigh(pe, turn, self.heads - 1)

    def vector(self, v, turn):
        c, H, turn = self.c, self.heads, turn + self.before
        for h in range(H + 1):
            if h < H:
                v.wait_ge(self.scores_ready, turn * H + h + 1)
                at = 0
                for t in range(HALVES):
                    last = v.tensor_reduce(c.negmax[:, h, t:t + 1], c.bank[h % 2][:, at:at + self.span[t]], AX,
                                           ALU.max, negate=True)
                    at += self.span[t]
                last.then_inc(self.negmax_ready, 1)
            if h >= 1:
                self.copy_probs(v, turn, h - 1)
                if h % self.per_ctx == 0:
                    self.normalise(v, turn, h // self.per_ctx - 1)

    def copy_probs(self, v, turn, h):
        c, H = self.c, self.heads
        v.wait_ge(self.probsT_in_psum, turn * H + h + 1)
        src, dst = c.bank[2 + h % 2], c.probsT[:, h % 2, :]
        if all(x[3] == P for x in self.at):
            n = len(self.at) * P
            last = v.tensor_copy(dst[:, 0:n], src[:, 0:n])
        else:
            for i, (t, kt, k0, kn, at) in enumerate(self.at):
                last = v.tensor_copy(dst[k0:k0 + kn, i * P:(i + 1) * P], src[0:kn, i * P:(i + 1) * P])
        last.then_inc(self.probsT_ready, 1)

    def normalise(self, v, turn, group):
        c, n, w = self.c, self.per_ctx, self.width
        v.wait_ge(self.ctx_in_psum, turn * self.n_ctx + group + 1)
        src = c.bank[4 + group % 2][:, 0:HALVES * n * w].rearrange("p (t h w) -> p t h w", t=HALVES, h=n)
        rec = c.recip[:, group % 2, 0:HALVES * n].rearrange("p (t h) -> p t h", t=HALVES)
        v.reciprocal(rec, src[:, :, :, w - 1]).then_inc(self.recip_ready, 1)
        v.wait_ge(self.recip_ready, turn * self.n_ctx + group + 1)
        for t in range(HALVES):
            dst = c.ctx[:, t, group * n * (w - 1):(group + 1) * n * (w - 1)].rearrange("p (h w) -> p h w", h=n)
            last = v.tensor_tensor(dst, src[:, t, :, 0:w - 1],
                                   rec[:, t, :].unsqueeze(2).broadcast_to((P, n, w - 1)), ALU.mult)
        last.then_inc(self.ctx_ready, 1)

    def scalar(self, a, turn):
        c, H, turn = self.c, self.heads, turn + self.before
        for h in range(H):
            a.wait_ge(self.negmax_ready, turn * H + h + 1)
            at = 0
            for t in range(HALVES):
                last = a.activation(c.probs[:, h % 2, at:at + self.span[t]], c.bank[h % 2][:, at:at + self.span[t]],
                                    ACT.Exp, bias=c.negmax[:, h, t:t + 1])
                at += self.span[t]
            last.then_inc(self.probs_ready, 1)


def causal_blocks(c):
    tri = c.causal[:, :]
    return [[(0, 0, P, (tri, 0))], [(0, 0, P, None), (1, 0, P, (tri, P))]]


class NarrowHeads:

    BESIDE = (10, 6, 11)

    def __init__(self, c, causal):
        self.c, self.causal = c, causal
        names = ("qk_ready", "q_alone", "scores_ready", "negmax_ready", "probs_ready", "probsT_in_psum",
                 "probsT_ready", "ctx_in_psum", "recip_ready", "shares_ready", "sharesT_in_psum", "sharesT_ready", "ctxT_ready")
        (self.qk_ready, self.q_alone, self.scores_ready, self.negmax_ready, self.probs_ready, self.probsT_in_psum,
         self.probsT_ready, self.ctx_in_psum, self.recip_ready, self.shares_ready, self.sharesT_in_psum,
         self.sharesT_ready, self.ctxT_ready), self.before = c.shared.take("heads", names, B)
        self.span = (P, S) if causal else (S, S)
        self.at = (0, self.span[0])
        self.blocks = [(kt, t) for kt in range(HALVES) for t in range(HALVES) if kt * P < self.span[t]]
        self.width = len(self.blocks) * P

    def clear_values(self, v):
        v.memset(self.c.big[:, 0:HALVES * NH * D], 0.0)

    def spread_values(self, t):
        a = t * NH * D
        return self.c.big[:, a:a + NH * (D + HD)].rearrange("p (h x) -> p h x", h=NH)[:, :, 0:HD]

    def scores(self, pe, turn, h):
        c, out = self.c, self.c.bank[h % 2]
        pe.wait_ge(self.q_alone, turn * NH + h + 1)
        for t in range(HALVES):
            at, n = self.at[t], self.span[t]
            last = pe.matmul(out[:, at:at + n], c.qT[:, 1 + h % 4, t * P:(t + 1) * P], c.kT[:, 0, 0:n],
                             start=True, stop=not self.causal, skip_group_check=True)
            if self.causal:
                last = pe.matmul(out[:, at + n - P:at + n], c.identb[:, :], c.causal[:, :], start=False, stop=True,
                                 skip_group_check=True)
        last.then_inc(self.scores_ready, 1)

    def turn_probs(self, pe, turn, h):
        c = self.c
        pe.wait_ge(self.probs_ready, turn * NH + h + 1)
        for i, (kt, t) in enumerate(self.blocks):
            at = self.at[t] + kt * P
            last = pe.transpose(c.bank[2 + h % 2][:, i * P:(i + 1) * P], c.probs[:, h % 2, at:at + P], c.ident[:, :])
        last.then_inc(self.probsT_in_psum, 1)

    def weigh(self, pe, turn, h):
        c = self.c
        pe.wait_ge(self.probsT_ready, turn * NH + h + 1)
        for kt in range(HALVES):
            mine = [i for i, x in enumerate(self.blocks) if x[0] == kt]
            q0 = S - len(mine) * P
            last = pe.matmul(c.bank[4][:, q0:S], c.big[:, (kt * NH + h) * D:(kt * NH + h + 1) * D],
                             c.probsT[:, h % 2, mine[0] * P:(mine[-1] + 1) * P], start=(h == 0 and kt == 0),
                             stop=(h == NH - 1 and kt == HALVES - 1), skip_group_check=True)
        if h == NH - 1:
            last.then_inc(self.ctx_in_psum, 1)

    def tensor(self, pe, turn, beside):
        c, turn = self.c, turn + self.before
        pe.wait_ge(self.qk_ready, turn + 1)
        self.scores(pe, turn, 0)
        self.scores(pe, turn, 1)
        for h in range(NH):
            self.turn_probs(pe, turn, h)
            if h + 2 < NH:
                self.scores(pe, turn, h + 2)
            if h >= 1:
                self.weigh(pe, turn, h - 1)
            if h == self.BESIDE[0]:
                beside()
        self.weigh(pe, turn, NH - 1)
        pe.wait_ge(self.shares_ready, turn + 1)
        for t in range(HALVES):
            last = pe.transpose(c.bank[5][:, t * P:(t + 1) * P], c.ctx[:, t, 0:D], c.ident[:, :])
        last.then_inc(self.sharesT_in_psum, 1)
        pe.wait_ge(self.ctxT_ready, turn + 1)

    def pick_q(self, v, turn, h):
        c = self.c
        v.tensor_scalar(c.qT[:, 1 + h % 4, :], c.qT[:, 0, :], c.headcol[:, h:h + 1], None,
                        ALU.mult).then_inc(self.q_alone, 1)

    def vector(self, v, turn, beside):
        c, turn = self.c, turn + self.before
        v.wait_ge(self.qk_ready, turn + 1)
        for h in range(4):
            self.pick_q(v, turn, h)
        for h in range(NH):
            v.wait_ge(self.scores_ready, turn * NH + h + 1)
            for t in range(HALVES):
                last = v.tensor_reduce(c.negmax[:, h, t:t + 1], c.bank[h % 2][:, self.at[t]:self.at[t] + self.span[t]],
                                       AX, ALU.max, negate=True)
            last.then_inc(self.negmax_ready, 1)
            if h + 4 < NH:
                self.pick_q(v, turn, h + 4)
            if h == self.BESIDE[1]:
                beside()
        v.wait_ge(self.probs_ready, (turn + 1) * NH)
        rec = c.recip[:, 0, 0:2 * NH].rearrange("p (t h) -> p t h", t=HALVES)
        v.reciprocal(rec, c.sums[:, :, :]).then_inc(self.recip_ready, 1)
        v.wait_ge(self.recip_ready, turn + 1)
        for t in range(HALVES):
            last = v.tensor_copy(c.ctx[:, t, 0:D].rearrange("p (h d) -> p h d", h=NH),
                                 rec[:, t, :].unsqueeze(2).broadcast_to((P, NH, HD)))
        last.then_inc(self.shares_ready, 1)
        v.wait_ge(self.ctx_in_psum, turn + 1)
        v.wait_ge(self.sharesT_ready, turn + 1)
        v.tensor_tensor(c.ctxT[:, 0, :], c.bank[4][:, 0:S], c.ctxT[:, 1, :], ALU.mult).then_inc(self.ctxT_ready, 1)

    def exp(self, a, turn, h):
        c = self.c
        a.wait_ge(self.negmax_ready, turn * NH + h + 1)
        for t in range(HALVES):
            at, n = self.at[t], self.span[t]
            last = a.activation(c.probs[:, h % 2, at:at + n], c.bank[h % 2][:, at:at + n], ACT.Exp,
                                bias=c.negmax[:, h, t:t + 1], accum_out=c.sums[:, t, h:h + 1])
        last.then_inc(self.probs_ready, 1)

    def scalar(self, a, turn, beside):
        c, turn = self.c, turn + self.before
        self.exp(a, turn, 0)
        for h in range(NH):
            if h + 1 < NH:
                self.exp(a, turn, h + 1)
            a.wait_ge(self.probsT_in_psum, turn * NH + h + 1)
            a.activation(c.probsT[:, h % 2, 0:self.width], c.bank[2 + h % 2][:, 0:self.width],
                         ACT.Identity).then_inc(self.probsT_ready, 1)
            if h == self.BESIDE[2]:
                beside()
        a.wait_ge(self.sharesT_in_psum, turn + 1)
        a.activation(c.ctxT[:, 1, :], c.bank[5][:, 0:S], ACT.Identity).then_inc(self.sharesT_ready, 1)




def plain_attention(nc, sem, c, name, io, x, causal, affine):
    w = io[name]
    norm = Norm(c, x, (c.cols[:, 2:3], c.cols[:, 3:4]) if affine else None)
    core = NarrowHeads(c, causal)
    loaded, bias_scaled = sem(name + "_weights"), sem(name + "_bias_scaled")
    proj_in_psum, step_v = sem(name + "_proj_in_psum"), sem(name + "_steps")
    v_in_psum, v_ready = sem(name + "_v_in_psum"), sem(name + "_v_ready")
    out_in_psum = sem(name + "_out_in_psum")
    wq, wk = c.wA[:, 0:D], c.wA[:, D:2 * D]
    wv, wo = c.wB[:, 0:D], c.wB[:, D:2 * D]
    scale = float(HD) ** -0.5
    with nc.Block() as block:

        @block.sync
        def _(sp):
            n = 0
            for dst, src in ((wq, w["wq"]), (wk, w["wk"]), (wv, w["wv"]), (wo, w["wo"]), (c.cols[:, 0:4], w["cols"]),
                             (c.rows[:, 0, :], w["bv"].partition_broadcast(P)),
                             (c.rows[:, 1, :], w["bo"].partition_broadcast(P))):
                sp.dma_start(dst, src).then_inc(loaded, 16)
                n += 16
            sp.wait_ge(loaded, n)

        @block.tensor
        def _(pe):
            pe.wait_ge(loaded, 112)
            norm.transpose(pe, 0)

            def one_row(b, final):
                norm.wait_transposed(pe, b)
                for u, weights in enumerate((wq, wk)):
                    pe.matmul(c.bank[u][:, 0:S], weights, c.xT[:, :], start=True, stop=True).then_inc(proj_in_psum, 1)
                for t in range(HALVES):
                    last = pe.matmul(c.bank[6][:, t * D:(t + 1) * D], c.xT[:, t * P:(t + 1) * P], wv, start=True,
                                     stop=True)
                last.then_inc(v_in_psum, 1)
                pe.wait_ge(v_ready, b + 1)
                core.tensor(pe, b, lambda: final or norm.transpose(pe, b + 1))
                for t in range(HALVES):
                    last = pe.matmul(c.bank[7][:, t * D:(t + 1) * D], c.ctxT[:, 0, t * P:(t + 1) * P], wo, start=True,
                                     stop=True)
                last.then_inc(out_in_psum, 1)

            with pe.Fori(0, B - 1) as b:
                one_row(b, False)
            one_row(B - 1, True)

        @block.gpsimd
        def _(g):
            with g.Fori(0, B) as b:
                norm.pool(g, b)

        @block.scalar
        def _(a):
            a.wait_ge(loaded, 112)
            a.mul(c.cols[:, 16:17], c.cols[:, 0:1], scale).then_inc(bias_scaled, 1)
            a.wait_ge(bias_scaled, 1)
            a.activation(c.cols[:, 30:31], c.cols[:, 0:1], ACT.Exp)
            norm.scalar(a, 0)

            def one_row(b, final):
                a.wait_ge(proj_in_psum, b * 2 + 1)
                a.activation(c.qT[:, 0, :], c.bank[0][:, 0:S], ACT.Identity, scale=scale, bias=c.cols[:, 16:17])
                a.wait_ge(proj_in_psum, b * 2 + 2)
                a.activation(c.kT[:, 0, :], c.bank[1][:, 0:S], ACT.Identity, bias=c.cols[:, 1:2]).then_inc(core.qk_ready, 1)
                core.scalar(a, b, lambda: final or norm.scalar(a, b + 1))

            with a.Fori(0, B - 1) as b:
                one_row(b, False)
            one_row(B - 1, True)

        @block.vector
        def _(v):
            core.clear_values(v)
            v.wait_ge(loaded, 112)
            norm.vector(v, 0, Steps(v, step_v, 0, LN_STEPS))

            def one_row(b, final):
                step = Steps(v, step_v, b, 3, LN_STEPS)
                v.wait_ge(v_in_psum, b + 1)
                for t in range(HALVES):
                    last = v.tensor_tensor(core.spread_values(t),
                                           c.bank[6][:, t * D:(t + 1) * D].rearrange("p (h d) -> p h d", h=NH),
                                           c.rows[:, 0, :].rearrange("p (h d) -> p h d", h=NH), ALU.add)
                last.then_inc(v_ready, 1)
                core.vector(v, b, lambda: final or norm.vector(v, b + 1, step))
                v.wait_ge(out_in_psum, b + 1)
                add_rows(v, step, x, b, c.bank[7][:, 0:S], c.rows[:, 1, :])
                if not final:
                    step.end()

            with v.Fori(0, B - 1) as b:
                one_row(b, False)
            one_row(B - 1, True)


def add_rows(v, step, x, b, more, bias=None):
    first = v.tensor_tensor(x[:, row(b)], x[:, row(b)], more, ALU.add)
    if bias is None:
        return first
    step.after(first)
    halves = x[:, row(b)].rearrange("p (t d) -> p t d", t=HALVES)
    return v.tensor_tensor(halves, halves, bias.unsqueeze(1).broadcast_to((P, HALVES, D)), ALU.add)


NEWTON_STEPS = 11


def rsqrt(v, step, c, x, y, part=None):
    n = x.shape[-1]
    ints, a, b, y2 = c.ints[:, 0:n], c.newton[:, 0, 0:n], c.newton[:, 1, 0:n], c.newton[:, 2, 0:n]
    if part != 1:
        step.after(v.tensor_scalar(ints, x.bitcast(I32), 1, None, ALU.logical_shift_right))
        step.after(v.tensor_scalar(a.bitcast(I32), ints, -1.0, MAGIC, ALU.mult, ALU.add))
    newton = ((a, b), (b, a), (a, y))
    for src, dst in newton if part is None else (newton[0:1], newton[1:])[part]:
        step.after(v.tensor_tensor(y2, src, src, ALU.mult))
        step.after(v.scalar_tensor_tensor(out=y2, in0=y2, scalar=-0.5, in1=x, op0=ALU.mult, op1=ALU.mult))
        step.after(v.scalar_tensor_tensor(out=dst, in0=y2, scalar=1.5, in1=src, op0=ALU.add, op1=ALU.mult))




def experts(nc, sem, c, name, io, x, gated):
    w = io[name]
    F = 256 if gated else 512
    chunks = F // P
    norm = Norm(c, x, None if gated else (c.cols[:, 0:1], c.cols[:, 1:2]))
    loaded, step_v = sem(name + "_weights"), sem(name + "_steps")
    logits_in_psum, gap_ready, share_ready = sem(name + "_logits_in_psum"), sem(name + "_gap_ready"), sem(name + "_share_ready")
    onehot_ready, onehotT_in_psum, onehotT_ready = sem(name + "_onehot_ready"), sem(name + "_onehotT_in_psum"), sem(name + "_onehotT_ready")
    up_in_psum, act_ready, hidden_ready = sem(name + "_up_in_psum"), sem(name + "_act_ready"), sem(name + "_hidden_ready")
    down_in_psum, acc_done, bias_in_psum = sem(name + "_down_in_psum"), sem(name + "_acc_done"), sem(name + "_bias_in_psum")
    up, side = c.big[:, 0:EXPERTS * F], c.big[:, EXPERTS * F:2 * EXPERTS * F]
    down0 = 2 * EXPERTS * F if gated else EXPERTS * F
    down = c.big[:, down0:down0 + EXPERTS * F]
    router = c.wB[:, 0:EXPERTS]
    hidden = c.qk[:, :, 0, 0:chunks * S]

    def te(i):
        return c.small[:, i, :].rearrange("p (t e) -> p t e", t=HALVES)

    logits, equal, cand, best1, rest, best2, weight, tmp = [te(i) for i in range(1, 9)]
    top = c.small[:, 10, 0:12].rearrange("p (k t) -> p k t", t=HALVES)

    def over(col):
        return col.unsqueeze(2).broadcast_to((P, HALVES, EXPERTS))

    with nc.Block() as block:

        @block.sync
        def _(sp):
            n = 0
            todo = [(up, w["up"]), (down, w["down"]), (router, w["router"])]
            if gated:
                todo.append((side, w["side"]))
            else:
                todo += [(c.cols[:, 0:2], w["ln"]), (c.colsA[:, 0:32], w["b1"]), (c.bottom[:, :], w["b2"]),
                         (c.rows[:, 0, 0:EXPERTS], w["gate_b"].partition_broadcast(P))]
            for dst, src in todo:
                sp.dma_start(dst, src).then_inc(loaded, 16)
                n += 16
            sp.wait_ge(loaded, n)

        all_loaded = 16 * (4 if gated else 7)

        @block.tensor
        def _(pe):
            pe.wait_ge(loaded, all_loaded)

            def go_up(b, e):
                for k in range(chunks):
                    out = c.bank[2 * (e % 2) + (0 if gated else k // 2)][:, (k % 2) * S:(k % 2) * S + S]
                    last = pe.matmul(out, up[:, e * F + k * P:e * F + (k + 1) * P], c.xT[:, :], start=True, stop=True)
                if gated:
                    for k in range(chunks):
                        last = pe.matmul(c.bank[2 * (e % 2) + 1][:, k * S:(k + 1) * S],
                                         side[:, e * F + k * P:e * F + (k + 1) * P], c.xT[:, :], start=True, stop=True)
                last.then_inc(up_in_psum, 1)

            def go_down(b, e):
                pe.wait_ge(hidden_ready, b * EXPERTS + e + 1)
                if e >= 2:
                    pe.wait_ge(acc_done, b * EXPERTS + e - 1)
                for t in range(HALVES):
                    for k in range(chunks):
                        last = pe.matmul(c.bank[4 + e % 2][:, t * D:(t + 1) * D],
                                         hidden[:, e % 2, k * S + t * P:k * S + (t + 1) * P],
                                         down[:, e * F + k * D:e * F + (k + 1) * D], start=(k == 0),
                                         stop=(k == chunks - 1))
                last.then_inc(down_in_psum, 1)

            norm.transpose(pe, 0)

            def one_row(b, final):
                norm.wait_transposed(pe, b)
                for t in range(HALVES):
                    last = pe.matmul(c.bank[6][:, t * EXPERTS:(t + 1) * EXPERTS], c.xT[:, t * P:(t + 1) * P], router,
                                     start=True, stop=True)
                last.then_inc(logits_in_psum, 1)
                go_up(b, 0)
                for e in range(EXPERTS):
                    if e + 1 < EXPERTS:
                        go_up(b, e + 1)
                    if e + 1 == EXPERTS - 1 and not final:
                        norm.transpose(pe, b + 1)
                    if e == 0 and not gated:
                        pe.wait_ge(onehot_ready, b + 1)
                        for t in range(HALVES):
                            last = pe.transpose(c.bank[7][0:EXPERTS, t * P:(t + 1) * P], best1[:, t, :],
                                                c.ident[:, :])
                        last.then_inc(onehotT_in_psum, 1)
                        pe.wait_ge(onehotT_ready, b + 1)
                        for t in range(HALVES):
                            last = pe.matmul(c.bank[7][:, S + t * D:S + (t + 1) * D],
                                             c.onehotT[:, t * P:(t + 1) * P], c.bottom[:, :], start=True, stop=True)
                        last.then_inc(bias_in_psum, 1)
                    go_down(b, e)

            with pe.Fori(0, B - 1) as b:
                one_row(b, False)
            one_row(B - 1, True)

        @block.gpsimd
        def _(g):
            with g.Fori(0, B) as b:
                norm.pool(g, b)

        @block.scalar
        def _(a):
            a.wait_ge(loaded, all_loaded)
            a.activation(c.cols[:, 30:31], c.neg_half[:, 0:1], ACT.Silu if gated else ACT.Relu)
            norm.scalar(a, 0)

            def one_row(b, final):
                if gated:
                    a.wait_ge(gap_ready, b + 1)
                    a.activation(top[:, 3, :], top[:, 2, :], ACT.Tanh, scale=0.5).then_inc(share_ready, 1)
                for e in range(EXPERTS):
                    if e == EXPERTS - 1 and not final:
                        norm.scalar(a, b + 1)
                    a.wait_ge(up_in_psum, b * EXPERTS + e + 1)
                    if gated:
                        if e >= 2:
                            a.wait_ge(hidden_ready, b * EXPERTS + e - 1)
                        a.activation(c.sq[:, e % 2, :], c.bank[2 * (e % 2)][:, :], ACT.Silu).then_inc(act_ready, 1)
                    else:
                        if e >= 2:
                            a.wait_ge(down_in_psum, b * EXPERTS + e - 1)
                        for k in range(chunks):
                            last = a.activation(hidden[:, e % 2, k * S:(k + 1) * S],
                                                c.bank[2 * (e % 2) + k // 2][:, (k % 2) * S:(k % 2) * S + S],
                                                ACT.Relu, bias=c.colsA[:, e * chunks + k:e * chunks + k + 1])
                        last.then_inc(hidden_ready, 1)

            with a.Fori(0, B - 1) as b:
                one_row(b, False)
            one_row(B - 1, True)

        @block.vector
        def _(v):
            v.wait_ge(loaded, all_loaded)

            def hottest(step, src, top_k, dst):
                step.after(v.tensor_reduce(top_k, src, AX, ALU.max))
                step.after(v.tensor_tensor(equal, src, over(top_k), ALU.is_equal))
                step.after(v.scalar_tensor_tensor(out=cand, in0=equal, scalar=-float(EXPERTS), in1=c.iota8[:, :, :],
                                                  op0=ALU.mult, op1=ALU.add))
                step.after(v.tensor_reduce(top[:, 5, :], cand, AX, ALU.min))
                step.after(v.tensor_tensor(dst, cand, over(top[:, 5, :]), ALU.is_equal))

            norm.vector(v, 0, Steps(v, step_v, 0, LN_STEPS))

            def one_row(b, final):
                step = Steps(v, step_v, b, STEPS_GATED if gated else STEPS_PLAIN, LN_STEPS)
                v.wait_ge(logits_in_psum, b + 1)
                psum = c.bank[6][:, 0:HALVES * EXPERTS].rearrange("p (t e) -> p t e", t=HALVES)
                if gated:
                    step.after(v.tensor_copy(logits, psum))
                    hottest(step, logits, top[:, 0, :], best1)
                    step.after(v.scalar_tensor_tensor(out=rest, in0=best1, scalar=MASKED, in1=logits, op0=ALU.mult,
                                                      op1=ALU.add))
                    hottest(step, rest, top[:, 1, :], best2)
                    v.tensor_tensor(top[:, 2, :], top[:, 0, :], top[:, 1, :], ALU.subtract).then_inc(gap_ready, 1)
                    v.wait_ge(share_ready, b + 1)
                    step.after(v.tensor_scalar(top[:, 4, :], top[:, 3, :], 0.5, 0.5, ALU.mult, ALU.add))
                    step.after(v.tensor_scalar(top[:, 5, :], top[:, 3, :], -0.5, 0.5, ALU.mult, ALU.add))
                    step.after(v.tensor_tensor(weight, best1, over(top[:, 4, :]), ALU.mult))
                    step.after(v.tensor_tensor(tmp, best2, over(top[:, 5, :]), ALU.mult))
                    step.after(v.tensor_tensor(weight, weight, tmp, ALU.add))
                    share = weight
                else:
                    step.after(v.tensor_tensor(logits, psum, c.rows[:, 0, 0:EXPERTS].unsqueeze(1)
                                               .broadcast_to((P, HALVES, EXPERTS)), ALU.add))
                    hottest(step, logits, top[:, 0, :], best1)
                    v.memset(top[:, 1, 0:1], 0.0).then_inc(onehot_ready, 1)
                    v.wait_ge(onehotT_in_psum, b + 1)
                    v.tensor_copy(c.onehotT[:, :], c.bank[7][0:EXPERTS, 0:S]).then_inc(onehotT_ready, 1)
                    share = best1

                def gather(e):
                    v.wait_ge(down_in_psum, b * EXPERTS + e + 1)
                    src = c.bank[4 + e % 2]
                    for t in range(HALVES):
                        part, acc = src[:, t * D:(t + 1) * D], c.ctx[:, t, 0:D]
                        if e == 0:
                            last = v.tensor_scalar(acc, part, share[:, t, e:e + 1], None, ALU.mult)
                        else:
                            last = v.scalar_tensor_tensor(out=acc, in0=part, scalar=share[:, t, e:e + 1], in1=acc,
                                                          op0=ALU.mult, op1=ALU.add)
                    last.then_inc(acc_done, 1)
                    v.wait_ge(acc_done, b * EXPERTS + e + 1)

                for e in range(EXPERTS):
                    if gated:
                        v.wait_ge(act_ready, b * EXPERTS + e + 1)
                        if e >= 2:
                            v.wait_ge(down_in_psum, b * EXPERTS + e - 1)
                        v.tensor_tensor(hidden[:, e % 2, :], c.sq[:, e % 2, :], c.bank[2 * (e % 2) + 1][:, :],
                                        ALU.mult).then_inc(hidden_ready, 1)
                    if e >= 1:
                        gather(e - 1)
                    if e == EXPERTS // 2 and not final:
                        norm.vector(v, b + 1, step)
                gather(EXPERTS - 1)
                halves = x[:, row(b)].rearrange("p (t d) -> p t d", t=HALVES)
                step.after(v.tensor_tensor(halves, halves, c.ctx[:, :, 0:D], ALU.add))
                if not gated:
                    v.wait_ge(bias_in_psum, b + 1)
                    step.after(v.tensor_tensor(x[:, row(b)], x[:, row(b)], c.bank[7][:, S:2 * S], ALU.add))
                if not final:
                    step.end()

            with v.Fori(0, B - 1) as b:
                one_row(b, False)
            one_row(B - 1, True)


STEPS_GATED = LN_STEPS + 1 + 5 + 1 + 5 + 5 + 1
STEPS_PLAIN = LN_STEPS + 1 + 5 + 2




def linear_attention(nc, sem, c, name, io, x):
    w = io[name]
    norm = Norm(c, x)
    loaded, step_v = sem(name + "_weights"), sem(name + "_steps")
    proj_in_psum, low_ready, exp_ready, feat_ready = [sem(name + "_" + s) for s in
                                                      ("proj_in_psum", "low_ready", "exp_ready", "feat_ready")]
    kv_in_psum, kv_ready, out_in_psum, ctx_ready = [sem(name + "_" + s) for s in
                                                    ("kv_in_psum", "kv_ready", "num_in_psum", "ctx_ready")]
    ctxT_in_psum, ctxT_ready, proj2_in_psum = [sem(name + "_" + s) for s in
                                               ("ctxT_in_psum", "ctxT_ready", "out_in_psum")]
    wq, wkv, wp = c.wA[:, 0:D], c.wA[:, D:3 * D], c.wA[:, 3 * D:4 * D]
    qf, kf = c.turnA[:, 0, 0:S], c.turnA[:, 1, 0:S]
    lowq, lowk = c.turnB[:, 0, 0:S], c.turnB[:, 1, 0:S]
    expq, expk = c.sq[:, 0, 0:S], c.sq[:, 1, 0:S]
    with nc.Block() as block:

        @block.sync
        def _(sp):
            for dst, src in ((wq, w["wq"]), (wkv, w["wkv"]), (wp, w["wp"]),
                             (c.rows[:, 0, :], w["bp"].partition_broadcast(P))):
                sp.dma_start(dst, src).then_inc(loaded, 16)
            sp.wait_ge(loaded, 64)

        @block.tensor
        def _(pe):
            pe.wait_ge(loaded, 64)
            with pe.Fori(0, B) as b:
                norm.tensor(pe, b)
                pe.matmul(c.bank[0][:, 0:S], wq, c.xT[:, :], start=True, stop=True)
                for t in range(HALVES):
                    last = pe.matmul(c.bank[1 + t][:, 0:2 * D], c.xT[:, t * P:(t + 1) * P], wkv, start=True, stop=True)
                last.then_inc(proj_in_psum, 1)
                pe.wait_ge(feat_ready, b + 1)
                for t in range(HALVES):
                    last = pe.matmul(c.bank[3][:, 0:D + 1], kf[:, t * D:(t + 1) * D], c.v1[:, t, 0:D + 1],
                                     start=(t == 0), stop=(t == 1))
                last.then_inc(kv_in_psum, 1)
                pe.wait_ge(kv_ready, b + 1)
                for t in range(HALVES):
                    last = pe.matmul(c.bank[4][:, t * (D + NH):(t + 1) * (D + NH)], qf[:, t * P:(t + 1) * P],
                                     c.kvblock[:, :], start=True, stop=True)
                last.then_inc(out_in_psum, 1)
                pe.wait_ge(ctx_ready, b + 1)
                for t in range(HALVES):
                    last = pe.transpose(c.bank[6][:, t * P:(t + 1) * P], c.ctx[:, t, 0:D], c.ident[:, :])
                last.then_inc(ctxT_in_psum, 1)
                pe.wait_ge(ctxT_ready, b + 1)
                for t in range(HALVES):
                    last = pe.matmul(c.bank[7][:, t * D:(t + 1) * D], c.ctxT[:, 0, t * P:(t + 1) * P], wp, start=True,
                                     stop=True)
                last.then_inc(proj2_in_psum, 1)

        @block.gpsimd
        def _(g):
            with g.Fori(0, B) as b:
                norm.pool(g, b)

        @block.scalar
        def _(a):
            a.activation(c.cols[:, 30:31], c.neg_half[:, 0:1], ACT.Exp)
            with a.Fori(0, B) as b:
                norm.scalar(a, b)
                a.wait_ge(low_ready, b + 1)
                a.activation(expq, lowq, ACT.Exp)
                a.activation(expk, lowk, ACT.Exp).then_inc(exp_ready, 1)
                a.wait_ge(ctxT_in_psum, b + 1)
                a.activation(c.ctxT[:, 0, :], c.bank[6][:, 0:S], ACT.Identity).then_inc(ctxT_ready, 1)

        @block.vector
        def _(v):
            v.wait_ge(loaded, 64)
            with v.Fori(0, B) as b:
                step = Steps(v, step_v, b, LN_STEPS + 3)
                norm.vector(v, b, step)
                v.wait_ge(proj_in_psum, b + 1)
                v.tensor_scalar(lowq, c.bank[0][:, 0:S], 0.0, None, ALU.min)
                for t in range(HALVES):
                    last = v.tensor_scalar(lowk[:, t * D:(t + 1) * D], c.bank[1 + t][:, 0:D], 0.0, None, ALU.min)
                last.then_inc(low_ready, 1)
                for t in range(HALVES):
                    v.tensor_copy(c.v1[:, t, 0:D], c.bank[1 + t][:, D:2 * D])
                v.wait_ge(exp_ready, b + 1)
                v.scalar_tensor_tensor(out=qf, in0=c.bank[0][:, 0:S], scalar=0.0, in1=expq, op0=ALU.max, op1=ALU.add)
                for t in range(HALVES):
                    last = v.scalar_tensor_tensor(out=kf[:, t * D:(t + 1) * D], in0=c.bank[1 + t][:, 0:D], scalar=0.0,
                                                  in1=expk[:, t * D:(t + 1) * D], op0=ALU.max, op1=ALU.add)
                last.then_inc(feat_ready, 1)
                v.wait_ge(kv_in_psum, b + 1)
                v.tensor_tensor(c.kvblock[:, 0:D], c.bank[3][:, 0:D], c.headmask[:, :], ALU.mult)
                v.tensor_scalar(c.kvblock[:, D:D + NH], c.headcol[:, :], c.bank[3][:, D:D + 1], None,
                                ALU.mult).then_inc(kv_ready, 1)
                v.wait_ge(out_in_psum, b + 1)
                num = c.bank[4][:, 0:HALVES * (D + NH)].rearrange("p (t n) -> p t n", t=HALVES)
                den = c.recip[:, 0, 0:HALVES * NH].rearrange("p (t h) -> p t h", t=HALVES)
                step.after(v.tensor_scalar(den, num[:, :, D:D + NH], 1e-6, None, ALU.add))
                step.after(v.reciprocal(den, den))
                for t in range(HALVES):
                    last = v.tensor_tensor(c.ctx[:, t, 0:D].rearrange("p (h d) -> p h d", h=NH),
                                           num[:, t, 0:D].rearrange("p (h d) -> p h d", h=NH),
                                           den[:, t, :].unsqueeze(2).broadcast_to((P, NH, HD)), ALU.mult)
                last.then_inc(ctx_ready, 1)
                v.wait_ge(proj2_in_psum, b + 1)
                add_rows(v, step, x, b, c.bank[7][:, 0:S], c.rows[:, 0, :])
                step.end()




def rotary_attention(nc, sem, c, name, io, x):
    w = io[name]
    norm = Norm(c, x)
    core = Core(c, 1, causal_blocks(c), lambda h: (c.qT[:, 0, :], c.kT[:, 0, :]),
                lambda h, kt: c.v1[:, kt, 0:D + 1], D + 1, 1, "wide_head")
    loaded, step_v = sem(name + "_weights"), sem(name + "_steps")
    proj_in_psum, v_copied, qk_rotated, qkT_in_psum = [sem(name + "_" + s) for s in
                                                       ("proj_in_psum", "v_copied", "qk_rotated", "qkT_in_psum")]
    wqkv = c.wA[:, 0:3 * D]
    with nc.Block() as block:

        @block.sync
        def _(sp):
            sp.dma_start(wqkv, w["wqkv"]).then_inc(loaded, 16)
            sp.dma_start(c.rope[:, 0:2, :, :], w["rope"]).then_inc(loaded, 16)
            sp.wait_ge(loaded, 32)

        @block.tensor
        def _(pe):
            pe.wait_ge(loaded, 32)
            with pe.Fori(0, B) as b:
                norm.tensor(pe, b)
                for t in range(HALVES):
                    last = pe.matmul(c.bank[t][:, 0:3 * D], c.xT[:, t * P:(t + 1) * P], wqkv, start=True, stop=True)
                last.then_inc(proj_in_psum, 1)
                pe.wait_ge(qk_rotated, b + 1)
                for which in range(2):
                    for t in range(HALVES):
                        last = pe.transpose(c.bank[7][:, which * S + t * P:which * S + (t + 1) * P],
                                            c.qk[:, t, 0, which * D:(which + 1) * D], c.ident[:, :])
                last.then_inc(qkT_in_psum, 1)
                core.tensor(pe, b)

        @block.gpsimd
        def _(g):
            with g.Fori(0, B) as b:
                norm.pool(g, b)

        @block.scalar
        def _(a):
            a.activation(c.cols[:, 30:31], c.neg_half[:, 0:1], ACT.Exp)
            with a.Fori(0, B) as b:
                norm.scalar(a, b)
                a.wait_ge(proj_in_psum, b + 1)
                for t in range(HALVES):
                    last = a.activation(c.v1[:, t, 0:D], c.bank[t][:, 2 * D:3 * D], ACT.Identity)
                last.then_inc(v_copied, 1)
                a.wait_ge(qkT_in_psum, b + 1)
                a.activation(c.qT[:, 0, :], c.bank[7][:, 0:S], ACT.Identity, scale=float(D) ** -0.5)
                a.activation(c.kT[:, 0, :], c.bank[7][:, S:2 * S], ACT.Identity).then_inc(core.qk_ready, 1)
                core.scalar(a, b)

        @block.vector
        def _(v):
            v.wait_ge(loaded, 32)
            with v.Fori(0, B) as b:
                step = Steps(v, step_v, b, LN_STEPS + 1)
                norm.vector(v, b, step)
                v.wait_ge(v_copied, b + 1)
                for t in range(HALVES):
                    src = c.bank[t][:, 0:2 * D].rearrange("p (n d) -> p n d", n=2)
                    last = rotate(v, src, c.turnA[:, t, 0:2 * D], c.turnB[:, t, 0:2 * D], 2, D,
                                  c.rope[:, 0, t, :], c.rope[:, 1, t, :])
                step.after(last)
                for t in range(HALVES):
                    last = v.tensor_tensor(c.qk[:, t, 0, 0:2 * D], c.turnA[:, t, 0:2 * D], c.turnB[:, t, 0:2 * D],
                                           ALU.add)
                last.then_inc(qk_rotated, 1)
                core.vector(v, b)
                v.wait_ge(core.ctx_ready, core.before + b + 1)
                halves = x[:, row(b)].rearrange("p (t d) -> p t d", t=HALVES)
                v.tensor_tensor(halves, halves, c.ctx[:, :, 0:D], ALU.add)
                step.end()


def rotate(v, src, straight, crossed, n, width, cos, sin):
    h = width // 2
    straight = straight.rearrange("p (n d) -> p n d", n=n)
    crossed = crossed.rearrange("p (n d) -> p n d", n=n)

    def each(t):
        return t.unsqueeze(1).broadcast_to((P, n, t.shape[-1]))

    v.tensor_tensor(straight, src, each(cos), ALU.mult)
    v.tensor_tensor(crossed[:, :, 0:h], src[:, :, h:width], each(sin[:, 0:h]), ALU.mult)
    return v.tensor_tensor(crossed[:, :, h:width], src[:, :, 0:h], each(sin[:, h:width]), ALU.mult)




def latent_attention(nc, sem, c, name, io, x):
    w = io[name]
    norm = Norm(c, x)
    core = NarrowHeads(c, True)
    loaded, step_v, ctx_in_psum = sem(name + "_weights"), sem(name + "_steps"), sem(name + "_ctx_in_psum")
    products_in_psum, value_ready, value_in_psum, blocks_ready = [sem(name + "_" + s) for s in (
        "products_in_psum", "value_ready", "value_in_psum", "blocks_ready")]
    proj_in_psum, squared, normed, qkT_in_psum = [sem(name + "_" + s) for s in
                                                  ("proj_in_psum", "squared", "qk_normed", "qkT_in_psum")]
    blocks = c.wB[:, 0:4 * D]
    tiles = c.wA[:, 0:10 * D].rearrange("p (n d) -> p n d", n=10)
    qk = c.qk[:, :, :, 0:D].rearrange("p t w (h d) -> p t w h d", h=NH)
    with nc.Block() as block:

        @block.sync
        def _(sp):
            for dst, src in ((tiles[:, :, :], w["tiles"]), (c.rows[:, 0, 0:2 * HD], w["norms"].partition_broadcast(P))):
                sp.dma_start(dst, src).then_inc(loaded, 16)
            sp.wait_ge(loaded, 32)

        @block.tensor
        def _(pe):
            pe.wait_ge(loaded, 32)
            pe.matmul(c.bank[0][:, 0:D], tiles[0:DH, 0, :], tiles[0:DH, 1, :], start=True, stop=True)
            pe.matmul(c.bank[0][:, D:2 * D], tiles[:, 2, :], tiles[:, 3, :], start=True, stop=True)
            pe.matmul(c.bank[0][:, 2 * D:3 * D], tiles[0:DH, 4, :], tiles[0:DH, 5, :], start=True, stop=True)
            pe.matmul(c.bank[0][:, 3 * D:4 * D], tiles[:, 6, :], tiles[:, 2, :], start=True,
                      stop=True).then_inc(products_in_psum, 1)
            pe.wait_ge(value_ready, 1)
            pe.matmul(c.bank[1][:, 0:D], tiles[:, 8, :], tiles[:, 7, :], start=True,
                      stop=True).then_inc(value_in_psum, 1)
            pe.wait_ge(blocks_ready, 1)
            norm.transpose(pe, 0)

            def one_row(b, final):
                norm.wait_transposed(pe, b)
                for t in range(HALVES):
                    last = pe.matmul(c.bank[t][:, :], c.xT[:, t * P:(t + 1) * P], blocks, start=True, stop=True)
                last.then_inc(proj_in_psum, 1)
                pe.wait_ge(normed, b + 1)
                for which in range(2):
                    for t in range(HALVES):
                        last = pe.transpose(c.bank[2 + which][:, t * P:(t + 1) * P], c.qk[:, t, which, 0:D],
                                            c.ident[:, :])
                last.then_inc(qkT_in_psum, 1)
                core.tensor(pe, b, lambda: final or norm.transpose(pe, b + 1))
                for t in range(HALVES):
                    last = pe.transpose(c.bank[7][:, t * D:(t + 1) * D], c.ctxT[:, 0, t * P:(t + 1) * P], c.ident[:, :])
                last.then_inc(ctx_in_psum, 1)

            with pe.Fori(0, B - 1) as b:
                one_row(b, False)
            one_row(B - 1, True)

        @block.gpsimd
        def _(g):
            with g.Fori(0, B) as b:
                norm.pool(g, b)

        @block.scalar
        def _(a):
            a.activation(c.cols[:, 30:31], c.neg_half[:, 0:1], ACT.Exp)
            norm.scalar(a, 0)

            def one_row(b, final):
                a.wait_ge(proj_in_psum, b + 1)
                for t in range(HALVES):
                    last = a.activation(c.sq[:, t, 0:2 * D], c.bank[t][:, 0:2 * D], ACT.Square)
                last.then_inc(squared, 1)
                a.wait_ge(qkT_in_psum, b + 1)
                a.activation(c.qT[:, 0, :], c.bank[2][:, 0:S], ACT.Identity, scale=float(HD) ** -0.5)
                a.activation(c.kT[:, 0, :], c.bank[3][:, 0:S], ACT.Identity).then_inc(core.qk_ready, 1)
                core.scalar(a, b, lambda: final or norm.scalar(a, b + 1))

            with a.Fori(0, B - 1) as b:
                one_row(b, False)
            one_row(B - 1, True)

        @block.vector
        def _(v):
            v.wait_ge(loaded, 32)
            core.clear_values(v)
            v.wait_ge(products_in_psum, 1)
            v.tensor_tensor(tiles[:, 8, :], c.bank[0][:, 3 * D:4 * D], c.headmask[:, :],
                            ALU.mult).then_inc(value_ready, 1)
            v.tensor_tensor(blocks[:, 0:3 * D].rearrange("p (n d) -> p n d", n=3),
                            c.bank[0][:, 0:3 * D].rearrange("p (n d) -> p n d", n=3),
                            c.headmask[:, :].unsqueeze(1).broadcast_to((P, 3, D)), ALU.mult)
            v.wait_ge(value_in_psum, 1)
            v.tensor_tensor(blocks[:, 3 * D:4 * D], c.bank[1][:, 0:D], c.headmask[:, :],
                            ALU.mult).then_inc(blocks_ready, 1)
            norm.vector(v, 0, Steps(v, step_v, 0, LN_STEPS))

            def one_row(b, final):
                step = Steps(v, step_v, b, LN_STEPS + 1 + 1 + NEWTON_STEPS + 2, LN_STEPS)
                v.wait_ge(squared, b + 1)
                for t in range(HALVES):
                    last = v.tensor_reduce(c.ss[:, t, :], c.sq[:, t, 0:2 * D].rearrange("p (h d) -> p h d", d=HD), AX,
                                           ALU.add)
                step.after(last)
                ss = c.ss[:, :, :].rearrange("p t h -> p (t h)")
                step.after(v.tensor_scalar(ss, ss, 1.0 / HD, RMS_EPS, ALU.mult, ALU.add))
                rsqrt(v, step, c, ss, c.rs[:, 0, :, :].rearrange("p t h -> p (t h)"))
                for t in range(HALVES):
                    last = v.tensor_tensor(c.turnA[:, t, 0:2 * D].rearrange("p (h d) -> p h d", d=HD),
                                           c.bank[t][:, 0:2 * D].rearrange("p (h d) -> p h d", d=HD),
                                           c.rs[:, 0, t, :].unsqueeze(2).broadcast_to((P, 2 * NH, HD)), ALU.mult)
                step.after(last)
                for t in range(HALVES):
                    for which in range(2):
                        src = c.turnA[:, t, which * D:(which + 1) * D].rearrange("p (h d) -> p h d", d=HD)
                        dst = qk[:, t, 0] if which == 0 else src
                        last = v.tensor_tensor(dst, src, c.rows[:, 0, which * HD:(which + 1) * HD].unsqueeze(1)
                                               .broadcast_to((P, NH, HD)), ALU.mult)
                step.after(last)
                for t in range(HALVES):
                    v.tensor_tensor(qk[:, t, 1],
                                    c.turnA[:, t, D:2 * D].rearrange("p (h d) -> p h d", d=HD),
                                    c.bank[t][:, 2 * D:3 * D].rearrange("p (h d) -> p h d", d=HD), ALU.add)
                    last = v.tensor_copy(core.spread_values(t),
                                         c.bank[t][:, 3 * D:4 * D].rearrange("p (h d) -> p h d", d=HD))
                last.then_inc(normed, 1)
                core.vector(v, b, lambda: final or norm.vector(v, b + 1, step))
                v.wait_ge(ctx_in_psum, b + 1)
                v.tensor_tensor(x[:, row(b)], x[:, row(b)], c.bank[7][:, 0:S], ALU.add)
                if not final:
                    step.end()

            with v.Fori(0, B - 1) as b:
                one_row(b, False)
            one_row(B - 1, True)




def norm_rows(nc, c):
    (stats_ready, var_ready, rstd_ready), before = c.shared.take("rows", ("stats_ready", "var_ready", "rstd_ready"), 1)
    halves = B * HALVES
    stats = c.turnA[:, 0, 0:6 * halves].rearrange("p (n k) -> p n k", n=halves)
    mv = c.turnA[:, 1, 0:2 * halves].rearrange("p (n k) -> p n k", n=halves)
    with nc.Block() as block:

        @block.gpsimd
        def _(g):
            g.wait_ge(var_ready, before + 1)
            g.tensor_tensor(c.rstd[:, 0:halves], c.vareps[:, 0:halves], c.neg_half[:, 0:halves],
                            ALU.pow).then_inc(rstd_ready, 1)

        @block.vector
        def _(v):
            for n in range(halves):
                last = v.bn_stats(stats[:, n, :], c.X[:, n * D:(n + 1) * D])
            last.then_inc(stats_ready, 1)
            v.wait_ge(stats_ready, 2 * before + 1)
            for n in range(halves):
                last = v.bn_aggr(mv[:, n, :], stats[:, n, :])
            last.then_inc(stats_ready, 1)
            v.wait_ge(stats_ready, 2 * before + 2)
            v.tensor_scalar(c.vareps[:, 0:halves], mv[:, :, 1], LN_EPS, None, ALU.add).then_inc(var_ready, 1)
            v.wait_ge(rstd_ready, before + 1)
            for n in range(halves):
                v.tensor_scalar(c.Y[:, n * D:(n + 1) * D], c.X[:, n * D:(n + 1) * D], mv[:, n, 0:1],
                                c.rstd[:, n:n + 1], ALU.subtract, ALU.mult)


def add_back(nc, c):
    with nc.Block() as block:

        @block.vector
        def _(v):
            v.tensor_tensor(c.X[:, :], c.X[:, :], c.Y[:, :], ALU.add)




QK_CHUNKS = 4
CHUNKS = 3 * INNER // 512
ROTATED = HALVES * QK_CHUNKS
CHUNK_ORDER = [(0, 0), (0, 4), (0, 1), (0, 2), (0, 5), (0, 3), (1, 0), (1, 4), (1, 1), (1, 2), (1, 5), (1, 3)]
QK_ORDER = [x for x in CHUNK_ORDER if x[1] < QK_CHUNKS]
PE_XT_SLOT, PE_CHUNK_SLOT = 0, 1
PE_CHUNK_SLOTS = {1 + j // 2: [j - j % 2, j - j % 2 + 1] for j in range(HALVES * CHUNKS)}
ACT_CHUNK_SLOTS = {1 + k: v for k, v in PE_CHUNK_SLOTS.items()}
DVE_ROTATE_SLOTS = {3: (0,), 4: (1, 2), 5: (3,), 6: (4,), 7: (5, 6), 8: (7,)}
DVE_RSQRT_SLOT = 9
PE_CTXT_SLOTS = {7: (0, 1), 8: (2, 3)}
COPY_CTXT_SLOTS = {8: (0, 1), 9: (2, 3)}
COPY_LAST_SLOT = max(COPY_CTXT_SLOTS)
PE_OUT_SLOT, DVE_OUT_SLOT = 10, 11
PE_QKT_SLOTS = {12: (0, 1), 13: (2, 3), 14: (4, 5), 15: (6, 7)}
COPY_QKT_SLOTS = {12: (0,), 13: (1, 2), 14: (3, 4), 15: (5, 6, 7)}
PREPARE_IN_FF = {2: ((0,), (1,)), 3: ((2,), (3,)), 4: ((4,), (5,)), 5: ((6,), (7, 8)), 6: ((9, 10), (11,)),
                 7: ((12, 13), (14, 15))}
POOL_ROTATE_SLOTS = {2: (0,), 3: (1,), 4: (2, 3), 5: (4,), 6: (5,), 7: (6, 7), 8: (8,)}
POOL_SCALE_SLOT = 10
ATTN_FROM, FF_FROM = 2, B
SPAN = (P, P + WINDOW)
AT = (0, P)
FIRST_KEY = (0, P - WINDOW)
GROUPS_OF_2 = NH // 2


def windowed_transformers(nc, sem, c, name, io):
    w = io[name]
    names = ("attn_weights", "ff_weights", "tables_loaded", "tables_ready", "attn_added", "ff_added", "steps",
             "row_copied", "rowT_in_psum", "xT_ready", "chunk_in_psum", "chunk_copied", "chunk_squared",
             "straight_ready", "chunk_rotated", "sum_ready", "rs_ready", "first_half_scaled", "second_half_scaled",
             "qkT_in_psum",
             "qT_copied", "kT_copied", "scores_ready", "negmax_ready", "probs_ready", "probsT_in_psum",
             "probsT_ready", "ctx_in_psum", "recip_ready", "ctx_ready", "ctxT_in_psum", "ctxT_by_scalar",
             "ctxT_by_vector", "out_in_psum", "shifted_in_psum", "shifted_ready", "kept_ready", "ff_in_psum",
             "gelu_ready", "hidden_ready", "ff_out_in_psum", "ff_steps")
    s = Chip()
    (s.attn_weights, s.ff_weights, tables_loaded, s.tables_ready, s.attn_added, s.ff_added, s.steps,
     s.row_copied, s.rowT_in_psum, s.xT_ready, s.chunk_in_psum, s.chunk_copied, s.chunk_squared,
     s.straight_ready, s.chunk_rotated, s.sum_ready, s.rs_ready, s.first_half_scaled, s.second_half_scaled,
     s.qkT_in_psum,
     s.qT_copied, s.kT_copied, s.scores_ready, s.negmax_ready, s.probs_ready, s.probsT_in_psum,
     s.probsT_ready, s.ctx_in_psum, s.recip_ready, s.ctx_ready, s.ctxT_in_psum, s.ctxT_by_scalar,
     s.ctxT_by_vector, s.out_in_psum, s.shifted_in_psum, s.shifted_ready, s.kept_ready, s.ff_in_psum,
     s.gelu_ready, s.hidden_ready, s.ff_out_in_psum, ff_steps) = [sem(name + "_" + n) for n in names]
    ff_norm = Norm(c, None, (c.cols[:, 0:1], c.cols[:, 1:2]), "window_norm", 0, 4)
    wqkv, wo = c.wA[:, :], c.wB[:, :]
    w1, w2 = c.wC[:, :], c.wD[:, :]
    n_attn, n_ff = 16 * 3, 16 * 3
    vn, tn = HALVES * NH * (DH + 1), 8 * S
    V = (c.V, c.big[:, 0:vn].rearrange("p (t h e) -> p t h e", t=HALVES, h=NH))
    qT = (c.qT, c.big[:, vn:vn + tn].rearrange("p (k s) -> p k s", k=8))
    kT = (c.kT, c.big[:, vn + tn:vn + 2 * tn].rearrange("p (k s) -> p k s", k=8))
    ctx = (c.ctx, c.ctx2)
    at = vn + 2 * tn
    hT = (c.hT, c.big[:, at:at + 3 * S].rearrange("p (k s) -> p k s", k=3))
    at += 3 * S
    sq = (c.sq[:, 0, :], c.sq[:, 1, :], c.big[:, at:at + 512], c.big[:, at + 512:at + 1024])
    blocks = ((0, 0, 0, P, 0, 0), (1, 1, 0, P, P + WINDOW, P), (1, 0, P - WINDOW, WINDOW, P, 2 * P))

    def scale(eng, t, w0, w1):
        n = (w1 - w0) * NH
        both = c.qk[:, t, w0:w1, :].rearrange("p w (h d) -> p (w h) d", d=DH)
        return eng.tensor_tensor(both, both, c.rs[:, 0, t, w0 * NH:w1 * NH].unsqueeze(2).broadcast_to((P, n, DH)),
                                 ALU.mult)

    def part_of(buffer, pp):
        return buffer[:, 2 * pp:2 * pp + 2, :].rearrange("p k s -> p (k s)")



    def pe_scores(pe, turn, j, h):
        if h % 4 == 0:
            pe.wait_ge(s.qT_copied, turn * 4 + h // 4 + 1)
            pe.wait_ge(s.kT_copied, turn * 4 + h // 4 + 1)
        row0 = DH * (h % 2)
        q, k, out = qT[j][row0:row0 + DH, h // 2, :], kT[j][row0:row0 + DH, h // 2, :], c.bank[h % 2]
        pe.matmul(out[:, 0:SPAN[0] + SPAN[1]], c.identb[:, :], c.bands[:, :], start=True, stop=False,
                  skip_group_check=True)
        for t in range(HALVES):
            last = pe.matmul(out[:, AT[t]:AT[t] + SPAN[t]], q[:, t * P:(t + 1) * P],
                             k[:, FIRST_KEY[t]:FIRST_KEY[t] + SPAN[t]], start=False, stop=(t == 1),
                             skip_group_check=True)
        last.then_inc(s.scores_ready, 1)

    def pe_turn_probs(pe, turn, h):
        pe.wait_ge(s.probs_ready, turn * NH + h + 1)
        for (tq, tk, k0, kn, at, to) in blocks:
            last = pe.transpose(c.bank[2 + h % 2][0:kn, to:to + P], c.probs[:, h % 2, at:at + kn], c.ident[:, :])
        last.then_inc(s.probsT_in_psum, 1)

    def pe_weigh(pe, turn, j, h, first):
        group, w = h // 2, DH + 1
        pe.wait_ge(s.probsT_ready, turn * NH + h + 1)
        if h % 2 == 0 and not (first and group < 2):
            pe.wait_ge(s.ctx_ready, turn * GROUPS_OF_2 + group - 1)
        if h == 2 and first:
            pe.wait_ge(s.ff_added, FF_FROM + turn)
        out = c.bank[4 + group % 2]
        for t in range(HALVES):
            mine = [x for x in blocks if x[0] == t]
            o = (t * 2 + h % 2) * w
            for i, (tq, tk, k0, kn, at, to) in enumerate(mine):
                last = pe.matmul(out[:, o:o + w], c.probsT[k0:k0 + kn, h % 2, to:to + P], V[j][k0:k0 + kn, tk, h, :],
                                 start=(i == 0), stop=(i == len(mine) - 1))
        if h % 2 == 1:
            last.then_inc(s.ctx_in_psum, 1)

    def pe_prepare(pe, q, slot, alone=False, start=False):
        if slot == PE_XT_SLOT:
            pe.wait_ge(s.row_copied, q + 1)
            if not alone:
                pe.wait_ge(s.qT_copied, q * 4)
                pe.wait_ge(s.kT_copied, q * 4)
            else:
                pe.wait_ge(s.attn_added, ATTN_FROM + q)
            for t in range(HALVES):
                last = pe.transpose(c.bank[6][:, t * P:(t + 1) * P], c.next_row[:, t, :], c.ident[:, :])
            last.then_inc(s.rowT_in_psum, 1)
        for i in PE_CHUNK_SLOTS.get(slot, ()):
            t, k = CHUNK_ORDER[i]
            if i == 0:
                pe.wait_ge(s.xT_ready, q + 1)
            if i >= 2:
                pe.wait_ge(s.chunk_copied, q * len(CHUNK_ORDER) + i - 1)
            pe.matmul(c.bank[7 - i % 2][:, :], c.next_rowT[:, t * P:(t + 1) * P], wqkv[:, k * 512:(k + 1) * 512], start=True,
                      stop=True).then_inc(s.chunk_in_psum, 1)
        for i in PE_QKT_SLOTS.get(slot, ()):
            if i == 0:
                pe.wait_ge(s.first_half_scaled, q + 1)
                pe.wait_ge(s.second_half_scaled, q + 1)
                pe.wait_ge(s.chunk_copied, (q + 1) * len(CHUNK_ORDER))
            elif i >= 2:
                pe.wait_ge((s.qT_copied, s.kT_copied)[i % 2], q * 4 + i // 2)
            which, pp = i % 2, i // 2
            if i == 1 and not start:
                pe.wait_ge(s.attn_added, ATTN_FROM + q - 1)
            for k in range(2):
                for t in range(HALVES):
                    at = (2 * pp + k) * P
                    last = pe.transpose(c.bank[6 + i % 2][:, (2 * k + t) * P:(2 * k + t + 1) * P],
                                        c.qk[:, t, which, at:at + P], c.ident[:, :])
            last.then_inc(s.qkT_in_psum, 1)

    def pe_finish(pe, turn, j, slot, alone=False):
        for i in PE_CTXT_SLOTS.get(slot, ()):
            if i == 0:
                pe.wait_ge(s.ctx_ready, (turn + 1) * GROUPS_OF_2)
                if not alone:
                    pe.wait_ge(s.chunk_copied, (turn + 3) * len(CHUNK_ORDER))
            elif i >= 2:
                pe.wait_ge((s.ctxT_by_scalar, s.ctxT_by_vector)[i % 2], turn * 2 + i // 2)
            for k in range(2):
                for t in range(HALVES):
                    at = (2 * i + k) * P
                    last = pe.transpose(c.bank[7 - i % 2][:, (2 * k + t) * P:(2 * k + t + 1) * P],
                                        ctx[j][:, t, at:at + P], c.ident[:, :])
            last.then_inc(s.ctxT_in_psum, 1)
        if slot == PE_OUT_SLOT:
            pe.wait_ge(s.ctxT_by_scalar, (turn + 1) * 2)
            pe.wait_ge(s.ctxT_by_vector, (turn + 1) * 2)
            for t in range(HALVES):
                for k in range(8):
                    last = pe.matmul(c.bank[7][:, t * D:(t + 1) * D], c.ctxT[:, k, t * P:(t + 1) * P],
                                     wo[:, k * D:(k + 1) * D], start=(k == 0), stop=(k == 7))
            last.then_inc(s.out_in_psum, 1)

    def pe_window(pe, turn, j, first=False, last=False):
        for h in range(NH):
            pe_turn_probs(pe, turn, h)
            if h + 2 < NH:
                pe_scores(pe, turn, j, h + 2)
            elif not last:
                pe_scores(pe, turn + 1, 1 - j, h + 2 - NH)
            if h >= 1:
                pe_weigh(pe, turn, j, h - 1, first)
            elif not first:
                pe_weigh(pe, turn - 1, 1 - j, NH - 1, False)
            if not first:
                pe_finish(pe, turn - 1, 1 - j, h, last)
            if not last:
                pe_prepare(pe, turn + 1, h, False, first)
        if last:
            pe_weigh(pe, turn, j, NH - 1, False)
            pe_shift(pe, turn - (B - 1), 0)
            for slot in range(NH):
                pe_finish(pe, turn, j, slot, True)
            ff_norm.transpose(pe, turn - (B - 1))


    def pool_prepare(g, q, b, slot):
        if slot == PE_XT_SLOT:
            g.wait_ge(s.ff_added, FF_FROM + q - B + 1)
            g.tensor_tensor(c.next_row[:, :, :].rearrange("p t d -> p (t d)"), c.Y[:, row(b)],
                            c.one[:, 0:1].broadcast_to((P, ROW)), ALU.mult).then_inc(s.row_copied, 1)
        for m in POOL_ROTATE_SLOTS.get(slot, ()):
            if m < ROTATED:
                t, k = QK_ORDER[m]
                g.wait_ge(s.chunk_copied, q * len(CHUNK_ORDER) + CHUNK_ORDER.index((t, k)) + 1)
                if m >= 2:
                    g.wait_ge(s.sum_ready, q * ROTATED + m - 1)
                cos = c.ropes[:, 2 * (k // 2), t, :].unsqueeze(1).broadcast_to((P, 8, DH))
                g.tensor_tensor(c.turnA[:, m % 2, :].rearrange("p (h d) -> p h d", h=8),
                                c.raw[:, m % 4, :].rearrange("p (h d) -> p h d", h=8), cos,
                                ALU.mult).then_inc(s.straight_ready, 1)
            if m >= 1:
                t, k = QK_ORDER[m - 1]
                g.wait_ge(s.straight_ready, q * ROTATED + m)
                g.wait_ge(s.chunk_rotated, q * ROTATED + m)
                g.tensor_tensor(c.qk[:, t, k // 2, (k % 2) * 512:(k % 2) * 512 + 512], c.turnA[:, (m - 1) % 2, :],
                                c.turnB[:, (m - 1) % 2, :], ALU.add).then_inc(s.sum_ready, 1)
        if slot == POOL_SCALE_SLOT:
            g.wait_ge(s.rs_ready, q + 1)
            g.wait_ge(s.sum_ready, (q + 1) * ROTATED)
            scale(g, 0, 0, 2).then_inc(s.first_half_scaled, 1)


    def act_probs(a, turn, h):
        a.wait_ge(s.negmax_ready, turn * NH + h + 1)
        for t in range(HALVES):
            last = a.activation(c.probs[:, h % 2, AT[t]:AT[t] + SPAN[t]], c.bank[h % 2][:, AT[t]:AT[t] + SPAN[t]],
                                ACT.Exp, bias=c.negmax[:, h, t:t + 1])
        last.then_inc(s.probs_ready, 1)

    def act_copy_probs(a, turn, h):
        a.wait_ge(s.probsT_in_psum, turn * NH + h + 1)
        k0, kn, to = blocks[2][2:4] + blocks[2][5:6]
        a.activation(c.probsT[:, h % 2, 0:2 * P], c.bank[2 + h % 2][:, 0:2 * P], ACT.Identity)
        a.activation(c.probsT[k0:k0 + kn, h % 2, to:to + P], c.bank[2 + h % 2][0:kn, to:to + P],
                     ACT.Identity).then_inc(s.probsT_ready, 1)

    def act_copy_chunks(a, q, j, slot):
        for i in ACT_CHUNK_SLOTS.get(slot, ()):
            t, k = CHUNK_ORDER[i]
            a.wait_ge(s.chunk_in_psum, q * len(CHUNK_ORDER) + i + 1)
            src = c.bank[7 - i % 2][:, :]
            if k < QK_CHUNKS:
                m = QK_ORDER.index((t, k))
                if m >= 4:
                    a.wait_ge(s.sum_ready, q * ROTATED + m - 3)
                a.activation(sq[m % 4], src, ACT.Square).then_inc(s.chunk_squared, 1)
                last = a.activation(c.raw[:, m % 4, :], src, ACT.Identity)
            else:
                h0 = 8 * (k - QK_CHUNKS)
                last = a.activation(V[j][:, t, h0:h0 + 8, 0:DH], src.rearrange("p (h d) -> p h d", h=8), ACT.Identity)
            last.then_inc(s.chunk_copied, 1)

    def act_prepare(a, q, j, slot):
        hi = D // 2
        if slot == PE_XT_SLOT:
            a.wait_ge(s.rowT_in_psum, q + 1)
            a.activation(c.next_rowT[0:hi, :], c.bank[6][0:hi, 0:S], ACT.Identity)
            a.activation(c.next_rowT[hi:D, 0:1], c.bank[6][hi:D, 0:1], ACT.Copy, scale=0.0)
            a.activation(c.next_rowT[hi:D, 1:S], c.bank[6][hi:D, 0:S - 1], ACT.Identity).then_inc(s.xT_ready, 1)
        for i in COPY_QKT_SLOTS.get(slot, ()):
            if i % 2 == 0:
                a.wait_ge(s.qkT_in_psum, q * 8 + i + 1)
                a.activation(part_of(qT[j], i // 2), c.bank[6][:, :], ACT.Identity).then_inc(s.qT_copied, 1)

    def act_finish(a, turn, slot):
        for i in COPY_CTXT_SLOTS.get(slot, ()):
            if i % 2 == 0:
                a.wait_ge(s.ctxT_in_psum, turn * 4 + i + 1)
                a.activation(part_of(c.ctxT, i), c.bank[7][:, :], ACT.Identity).then_inc(s.ctxT_by_scalar, 1)

    def act_window(a, turn, j, first=False, last=False):
        for h in range(NH):
            if not last:
                act_copy_chunks(a, turn + 1, 1 - j, h)
            if h + 1 < NH:
                act_probs(a, turn, h + 1)
            elif not last:
                act_probs(a, turn + 1, 0)
            act_copy_probs(a, turn, h)
            if not first:
                act_finish(a, turn - 1, h)
            if not last:
                act_prepare(a, turn + 1, 1 - j, h)
        if last:
            act_shifted(a, turn - (B - 1))
            for slot in range(NH):
                act_finish(a, turn, slot)
            ff_norm.scalar(a, turn - (B - 1))


    def dve_negmax(v, turn, h):
        v.wait_ge(s.scores_ready, turn * NH + h + 1)
        for t in range(HALVES):
            last = v.tensor_reduce(c.negmax[:, h, t:t + 1], c.bank[h % 2][:, AT[t]:AT[t] + SPAN[t]], AX, ALU.max,
                                   negate=True)
        last.then_inc(s.negmax_ready, 1)

    def dve_normalise(v, turn, j, group):
        w = DH + 1
        v.wait_ge(s.ctx_in_psum, turn * GROUPS_OF_2 + group + 1)
        src = c.bank[4 + group % 2][:, 0:4 * w].rearrange("p (n w) -> p n w", n=4)
        rec = c.recip[:, group % 2, 0:4]
        v.reciprocal(rec, src[:, :, w - 1]).then_inc(s.recip_ready, 1)
        v.wait_ge(s.recip_ready, turn * GROUPS_OF_2 + group + 1)
        dst = ctx[j][:, :, 2 * group * DH:(2 * group + 2) * DH].rearrange("p t (h d) -> p t h d", h=2)
        v.tensor_tensor(dst, src[:, :, 0:DH].rearrange("p (t h) d -> p t h d", t=HALVES),
                        rec.rearrange("p (t h) -> p t h", t=HALVES).unsqueeze(3).broadcast_to((P, HALVES, 2, DH)),
                        ALU.mult).then_inc(s.ctx_ready, 1)

    def dve_prepare(v, step, q, j, slot):
        ss, rs = c.ss[:, :, :].rearrange("p t h -> p (t h)"), c.rs[:, 0, :, :].rearrange("p t h -> p (t h)")
        for m in DVE_ROTATE_SLOTS.get(slot, ()):
            t, k = QK_ORDER[m]
            v.wait_ge(s.chunk_squared, q * ROTATED + m + 1)
            v.tensor_reduce(c.ss[:, t, 8 * k:8 * k + 8], sq[m % 4].rearrange("p (h d) -> p h d", h=8), AX, ALU.add)
            if m >= 2:
                v.wait_ge(s.sum_ready, q * ROTATED + m - 1)
            v.wait_ge(s.chunk_copied, q * len(CHUNK_ORDER) + CHUNK_ORDER.index((t, k)) + 1)
            src = c.raw[:, m % 4, :].rearrange("p (h d) -> p h d", h=8)
            out = c.turnB[:, m % 2, :].rearrange("p (h d) -> p h d", h=8)
            sin, h2 = c.ropes[:, 2 * (k // 2) + 1, t, :], DH // 2
            for to, frm in ((0, h2), (h2, 0)):
                last = v.tensor_tensor(out[:, :, to:to + h2], src[:, :, frm:frm + h2],
                                       sin[:, to:to + h2].unsqueeze(1).broadcast_to((P, 8, h2)), ALU.mult)
            last.then_inc(s.chunk_rotated, 1)
        if slot == DVE_RSQRT_SLOT:
            v.wait_ge(s.chunk_rotated, (q + 1) * ROTATED)
            step.after(v.tensor_scalar(ss, ss, 1e-24, None, ALU.max))
            rsqrt(v, step, c, ss, rs, 0)
        if slot == DVE_RSQRT_SLOT + 1:
            rsqrt(v, step, c, ss, rs, 1)
            v.memset(c.recip[:, 0, 31:32], 0.0).then_inc(s.rs_ready, 1)
            v.wait_ge(s.sum_ready, (q + 1) * ROTATED)
            scale(v, 1, 0, 1)
        if slot == DVE_RSQRT_SLOT + 2:
            scale(v, 1, 1, 2).then_inc(s.second_half_scaled, 1)
        for i in COPY_QKT_SLOTS.get(slot, ()):
            if i % 2 == 1:
                v.wait_ge(s.qkT_in_psum, q * 8 + i + 1)
                v.tensor_copy(part_of(kT[j], i // 2), c.bank[7][:, :]).then_inc(s.kT_copied, 1)

    def dve_finish(v, turn, b, slot):
        for i in COPY_CTXT_SLOTS.get(slot, ()):
            if i % 2 == 1:
                v.wait_ge(s.ctxT_in_psum, turn * 4 + i + 1)
                v.tensor_copy(part_of(c.ctxT, i), c.bank[6][:, :]).then_inc(s.ctxT_by_vector, 1)
        if slot == DVE_OUT_SLOT:
            v.wait_ge(s.out_in_psum, turn + 1)
            v.tensor_tensor(c.Y[:, row(b)], c.Y[:, row(b)], c.bank[7][:, 0:S], ALU.add).then_inc(s.attn_added, 1)

    def dve_steps(v, q):
        return Steps(v, s.steps, q, 1 + NEWTON_STEPS)

    def dve_window(v, turn, b, j, first=False, last=False):
        step = None if last else dve_steps(v, turn + 1)
        for h in range(NH):
            if h + 1 < NH:
                dve_negmax(v, turn, h + 1)
            elif not last:
                dve_negmax(v, turn + 1, 0)
            if h % 2 == 1 and h >= 3:
                dve_normalise(v, turn, j, (h - 3) // 2)
            elif h == 1 and not first:
                dve_normalise(v, turn - 1, 1 - j, GROUPS_OF_2 - 1)
            if not first:
                dve_finish(v, turn - 1, b - 1, h)
            if not last:
                dve_prepare(v, step, turn + 1, 1 - j, h)
        if last:
            dve_normalise(v, turn, j, GROUPS_OF_2 - 1)
            for slot in range(NH):
                dve_finish(v, turn, b, slot)
                if slot == COPY_LAST_SLOT:
                    dve_ff_norm(v, turn - (B - 1), 0)
        else:
            step.end()


    def beside_ff(step, part):
        return PREPARE_IN_FF[step][part] if step in PREPARE_IN_FF else ()

    def pe_shift(pe, turn, b):
        pe.wait_ge(s.attn_added, ATTN_FROM + turn + 1)
        hi = D // 2
        for t in range(HALVES):
            last = pe.matmul(c.bank[3][:, t * hi:(t + 1) * hi], c.shift[:, :],
                             c.Y[:, bass.ds(b * ROW + t * D + hi, hi)], start=True, stop=(t == 0))
            if t == 1:
                last = pe.matmul(c.bank[3][:, t * hi:(t + 1) * hi], c.carry[:, :],
                                 c.Y[:, bass.ds(b * ROW + hi, hi)], start=False, stop=True)
        last.then_inc(s.shifted_in_psum, 1)

    def pe_ff_out(pe, turn, j):
        pe.wait_ge(s.hidden_ready, (turn + 1) * 3)
        pe.wait_ge(s.ff_added, FF_FROM + turn)
        for t in range(HALVES):
            for k, (at, n) in enumerate(FF_CHUNKS):
                m = n + (k == 2)
                last = pe.matmul(c.bank[5][:, t * D:(t + 1) * D], hT[j][0:m, k, t * P:(t + 1) * P],
                                 w2[0:m, k * D:(k + 1) * D], start=(k == 0), stop=(k == 2))
        last.then_inc(s.ff_out_in_psum, 1)

    def pe_ff_step(pe, turn, b, j, first, last, beside):
        if not last:
            pe_shift(pe, turn + 1, b + 1)
        ff_norm.wait_transposed(pe, turn)
        for k, (at, n) in enumerate(FF_CHUNKS):
            if not first:
                pe.wait_ge(s.hidden_ready, turn * 3 + k - 2)
            for side in range(2):
                done = pe.matmul(c.bank[k][0:n, side * S:(side + 1) * S],
                                 w1[:, side * FF + at:side * FF + at + n], c.xT[:, :], start=True, stop=True)
            done.then_inc(s.ff_in_psum, 1)
        beside(b, 0)
        if not first:
            pe_ff_out(pe, turn - 1, 1 - j)
        if not last:
            ff_norm.transpose(pe, turn + 1)
        beside(b, 1)

    def pool_ff(g, turn, b):
        g.wait_ge(s.shifted_in_psum, turn + 1)
        hi = D // 2
        kept = c.Y[:, row(b)].rearrange("p (t d) -> p t d", t=HALVES)[:, :, 0:hi]
        one = c.one[:, 0:1].unsqueeze(1).broadcast_to((P, HALVES, hi))
        g.tensor_tensor(c.xn[:, :, 0:hi], kept, one, ALU.mult).then_inc(s.kept_ready, 1)
        ff_norm.pool(g, turn)

    def act_shifted(a, turn):
        hi = D // 2
        a.wait_ge(s.shifted_in_psum, turn + 1)
        a.activation(c.xn[:, :, hi:D], c.bank[3][:, 0:D].rearrange("p (t d) -> p t d", t=HALVES),
                     ACT.Identity).then_inc(s.shifted_ready, 1)

    def act_ff_step(a, turn, b, last, beside):
        if not last:
            act_shifted(a, turn + 1)
        for k, (at, n) in enumerate(FF_CHUNKS):
            a.wait_ge(s.ff_in_psum, turn * 3 + k + 1)
            a.activation(c.probs[0:n, :, :].rearrange("p a b -> p (a b)")[:, k * S:(k + 1) * S],
                         c.bank[k][0:n, S:2 * S], ACT.Gelu,
                         bias=c.cols[0:n, 5 + k:6 + k]).then_inc(s.gelu_ready, 1)
        beside(b, 0)
        if not last:
            ff_norm.scalar(a, turn + 1)
        beside(b, 1)

    def dve_ff_norm(v, turn, b):
        step = Steps(v, ff_steps, turn, LN_STEPS)
        v.wait_ge(s.shifted_ready, turn + 1)
        v.wait_ge(s.kept_ready, turn + 1)
        ff_norm.vector(v, b, step, turn)
        step.end()

    def dve_ff_add(v, turn, b):
        v.wait_ge(s.ff_out_in_psum, turn + 1)
        v.tensor_tensor(c.Y[:, row(b)], c.Y[:, row(b)], c.bank[5][:, 0:S], ALU.add).then_inc(s.ff_added, 1)

    def dve_ff_step(v, turn, b, j, first, last, beside):
        if not last:
            dve_ff_norm(v, turn + 1, b + 1)
        for k, (at, n) in enumerate(FF_CHUNKS):
            v.wait_ge(s.gelu_ready, turn * 3 + k + 1)
            v.scalar_tensor_tensor(out=hT[j][0:n, k, :], in0=c.bank[k][0:n, 0:S],
                                   scalar=c.cols[0:n, 2 + k:3 + k],
                                   in1=c.probs[0:n, :, :].rearrange("p a b -> p (a b)")[:, k * S:(k + 1) * S],
                                   op0=ALU.add, op1=ALU.mult).then_inc(s.hidden_ready, 1)
        beside(b, 0)
        if not first:
            dve_ff_add(v, turn - 1, b - 1)
        beside(b, 1)

    def run(number):
        layer0, layer1 = number * DEPTH, (number + 1) * DEPTH
        with nc.Block() as block:

            @block.sync
            def _(sp):
                sp.dma_start(c.rope[:, :, :, 0:DH], w["rope"]).then_inc(tables_loaded, 16)
                with sp.Fori(layer0, layer1) as d:
                    sp.wait_ge(s.attn_added, ATTN_FROM + d * B - 1)
                    sp.dma_start(wqkv, w["wqkv"][bass.ds(d, 1)].rearrange("a p n -> (a p) n")).then_inc(s.attn_weights, 16)
                    sp.dma_start(c.scl[:, :, :].rearrange("p a b -> p (a b)"),
                                 w["scales"][bass.ds(d, 1)].rearrange("a n -> (a n)").partition_broadcast(P)).then_inc(s.attn_weights, 16)
                    sp.wait_ge(s.attn_added, ATTN_FROM + d * B)
                    sp.dma_start(wo, w["wo"][bass.ds(d, 1)].rearrange("a p n -> (a p) n")).then_inc(s.attn_weights, 16)
                    sp.wait_ge(s.ff_added, FF_FROM + d * B)
                    sp.dma_start(w1, w["w1"][bass.ds(d, 1)].rearrange("a p n -> (a p) n")).then_inc(s.ff_weights, 16)
                    sp.dma_start(w2, w["w2"][bass.ds(d, 1)].rearrange("a p n -> (a p) n")).then_inc(s.ff_weights, 16)
                    sp.dma_start(c.cols[:, 0:8], w["cols"][bass.ds(d, 1)].rearrange("a p n -> (a p) n")).then_inc(s.ff_weights, 16)
                sp.wait_ge(s.attn_weights, n_attn * layer1)
                sp.wait_ge(s.ff_weights, n_ff * layer1)

            @block.tensor
            def _(pe):
                def layer(d, last):
                    turn = d * B
                    pe_scores(pe, turn, 0, 0)
                    pe_scores(pe, turn, 0, 1)
                    pe_window(pe, turn, 0, first=True)
                    with pe.Fori(0, B // 2 - 1) as pair:
                        pe_window(pe, turn + pair * 2 + 1, 1)
                        pe_window(pe, turn + pair * 2 + 2, 0)
                    pe_window(pe, turn + B - 1, 1, last=True)
                    pe.wait_ge(s.ff_weights, d * n_ff + n_ff)
                    for b in range(B):
                        pe_ff_step(pe, turn + b, b, b % 2, b == 0, b == B - 1, lambda step, part: last or prepare(
                            turn + B, beside_ff(step, part), (d + 2) * n_attn))
                    pe_ff_out(pe, turn + B - 1, 1)

                def prepare(turn, slots, weights):
                    for slot in slots:
                        if slot == PE_CHUNK_SLOT:
                            pe.wait_ge(s.attn_weights, weights)
                        pe_prepare(pe, turn, slot, True, True)

                prepare(layer0 * B, range(NH), (layer0 + 1) * n_attn)
                with pe.Fori(layer0, layer1 - 1) as d:
                    layer(d, False)
                layer(layer1 - 1, True)

            @block.gpsimd
            def _(g):
                def prepare(d, slots):
                    for slot in slots:
                        if slot == PE_XT_SLOT:
                            g.wait_ge(s.tables_ready, d + 1)
                        pool_prepare(g, d * B, 0, slot)

                def layer(d, last):
                    with g.Fori(1, B) as b:
                        for slot in range(NH):
                            pool_prepare(g, d * B + b, b, slot)
                    pool_ff(g, d * B, 0)
                    for b in range(B):
                        if b + 1 < B:
                            pool_ff(g, d * B + b + 1, b + 1)
                        for part in range(0 if last else 2):
                            prepare(d + 1, beside_ff(b, part))

                prepare(layer0, range(NH))
                with g.Fori(layer0, layer1 - 1) as d:
                    layer(d, False)
                layer(layer1 - 1, True)

            @block.scalar
            def _(a):
                def prepare(turn, slots):
                    for slot in slots:
                        act_copy_chunks(a, turn, 0, slot)
                        act_prepare(a, turn, 0, slot)

                def layer(d, last):
                    turn = d * B
                    a.activation(c.cols[:, 30:31], c.neg_half[:, 0:1], ACT.Exp)
                    act_probs(a, turn, 0)
                    act_window(a, turn, 0, first=True)
                    with a.Fori(0, B // 2 - 1) as pair:
                        act_window(a, turn + pair * 2 + 1, 1)
                        act_window(a, turn + pair * 2 + 2, 0)
                    a.wait_ge(s.ff_weights, d * n_ff + n_ff)
                    act_window(a, turn + B - 1, 1, last=True)
                    a.activation(c.cols[:, 30:31], c.neg_half[:, 0:1], ACT.Gelu)
                    for b in range(B):
                        act_ff_step(a, turn + b, b, b == B - 1, lambda step, part: last or prepare(
                            turn + B, beside_ff(step, part)))

                prepare(layer0 * B, range(NH))
                with a.Fori(layer0, layer1 - 1) as d:
                    layer(d, False)
                layer(layer1 - 1, True)

            @block.vector
            def _(v):
                if number == 0:
                    v.sem_inc(s.attn_added, ATTN_FROM)
                    v.sem_inc(s.ff_added, FF_FROM)
                v.wait_ge(tables_loaded, 16 * (number + 1))
                v.memset(c.recip[:, 0, 31:32], 0.0)
                v.memset(V[1][:, :, :, :], 1.0)
                v.memset(hT[1][:, :, :], 1.0)

                def tables(d):
                    v.wait_ge(s.attn_weights, (d + 1) * n_attn)
                    v.tensor_tensor(c.ropes[:, :, :, :], c.rope[:, :, :, 0:DH],
                                    c.scl[:, :, :].unsqueeze(2).broadcast_to((P, 4, HALVES, DH)),
                                    ALU.mult).then_inc(s.tables_ready, 1)
                    v.wait_ge(s.tables_ready, d + 1)

                def prepare(d, step, slots):
                    for slot in slots:
                        if slot == PE_XT_SLOT:
                            tables(d)
                        dve_prepare(v, step, d * B, 0, slot)

                def layer(d, last):
                    turn = d * B
                    dve_negmax(v, turn, 0)
                    dve_window(v, turn, 0, 0, first=True)
                    with v.Fori(0, B // 2 - 1) as pair:
                        dve_window(v, turn + pair * 2 + 1, pair * 2 + 1, 1)
                        dve_window(v, turn + pair * 2 + 2, pair * 2 + 2, 0)
                    dve_window(v, turn + B - 1, B - 1, 1, last=True)
                    v.wait_ge(s.ff_weights, d * n_ff + n_ff)
                    step = None if last else dve_steps(v, turn + B)
                    for b in range(B):
                        dve_ff_step(v, turn + b, b, b % 2, b == 0, b == B - 1, lambda at, part: last or prepare(
                            d + 1, step, beside_ff(at, part)))
                    dve_ff_add(v, turn + B - 1, B - 1)
                    if not last:
                        step.end()

                step = dve_steps(v, layer0 * B)
                prepare(layer0, step, range(NH))
                step.end()
                with v.Fori(layer0, layer1 - 1) as d:
                    layer(d, False)
                layer(layer1 - 1, True)

    return run


def store(nc, sem, c, io):
    stored = sem("stored")
    with nc.Block() as block:

        @block.sync
        def _(sp):
            for b in range(B):
                sp.dma_start(io["out"][b].rearrange("(t p) d -> p t d", p=P),
                             c.X[:, b * ROW:(b + 1) * ROW].rearrange("p (t d) -> p t d", t=HALVES)).then_inc(stored, 16)
            sp.wait_ge(stored, 16 * B)


def program(nc, io):
    with ExitStack() as ctx:
        c = allocate(nc, ctx)

        def sem(name):
            return ctx.enter_context(nc.semaphore(name))

        c.shared = Shared(sem)
        setup(nc, sem, c, io)

        transformer = windowed_transformers(nc, sem, c, "wt", io)

        def layer_on_Y(body):
            norm_rows(nc, c)
            body()
            add_back(nc, c)

        def last_block():
            plain_attention(nc, sem, c, "a3", io, c.Y, False, True)
            experts(nc, sem, c, "e3", io, c.Y, False)

        parts = [
            lambda: plain_attention(nc, sem, c, "a0", io, c.X, True, False),
            lambda: experts(nc, sem, c, "e0", io, c.X, True),
            lambda: linear_attention(nc, sem, c, "l1", io, c.X),
            lambda: layer_on_Y(lambda: transformer(0)),
            lambda: rotary_attention(nc, sem, c, "r2", io, c.X),
            lambda: layer_on_Y(lambda: transformer(1)),
            lambda: latent_attention(nc, sem, c, "m3", io, c.X),
            lambda: layer_on_Y(last_block),
        ]
        for part in parts:
            part()
        store(nc, sem, c, io)




def kernel(**inputs):
    import numpy as np
    import concourse.bacc as bacc
    from concourse.bass_utils import run_bass_kernel_spmd

    a = {k: np.ascontiguousarray(v) for k, v in inputs.items()}
    nc = bacc.Bacc("TRN2", target_bir_lowering=False, num_devices=1)
    arrays = {}

    def give(name, array):
        array = np.ascontiguousarray(array)
        name = "in_" + name
        arrays[name] = array
        return nc.dram_tensor(name, array.shape, mybir.dt.from_np(array.dtype), kind="ExternalInput").ap()

    def plain(name, wq, wk, wv, wo, bq, bk, bv, bo, g=None, bln=None):
        cols = np.zeros((P, 4), np.float32)
        cols[:, 0], cols[:, 1] = bq, bk
        if g is not None:
            cols[:, 2], cols[:, 3] = g, bln
        return {"wq": give(name + "_wq", wq), "wk": give(name + "_wk", wk),
                "wv": give(name + "_wv", wv), "wo": give(name + "_wo", wo), "cols": give(name + "_cols", cols),
                "bv": give(name + "_bv", bv), "bo": give(name + "_bo", bo)}

    def chunks(w, n, m):
        return w.reshape(n, P, m).transpose(1, 0, 2).reshape(P, n * m)

    def halves(t):
        return t.reshape(HALVES, P, -1).transpose(1, 0, 2)

    f32 = np.float32
    hd = np.arange(0, DH, 2, dtype=f32)
    inv_freq = (f32(1.0) / np.power(f32(10000.0), hd / f32(DH))).astype(f32)
    tok = np.arange(S, dtype=f32)
    fr = tok[:, None] * inv_freq[None, :]
    cos, sin = np.cos(fr).astype(f32), np.sin(fr).astype(f32)
    base = ((hd + f32(0.4 * DH)) / f32(1.4 * DH)).astype(f32)
    power = ((tok - S // 2) / (WINDOW // 2)).astype(f32)
    sc = np.power(base[None, :], power[:, None]).astype(f32)
    inv = (f32(1.0) / sc).astype(f32)
    tabs = []
    for m in (sc * f32(8.0), inv):
        tabs.append(np.concatenate([cos * m, cos * m], 1))
        tabs.append(np.concatenate([-(sin * m), sin * m], 1))
    window_rope = np.stack([halves(t) for t in tabs], 1).astype(f32)
    i = np.arange(D // 2, dtype=f32)
    ang = tok[:, None] * np.power(f32(10000.0), (f32(-2.0) * (i - f32(1.0)) / f32(D))).astype(f32)[None, :]
    c2, s2 = np.cos(ang).astype(f32), np.sin(ang).astype(f32)
    wide_rope = np.stack([halves(np.concatenate([c2, c2], 1)), halves(np.concatenate([s2, -s2], 1))], 1).astype(f32)

    def windowed(p):
        def swap(x):
            return np.concatenate([x[:, DH // 2:], x[:, :DH // 2]], 1)

        qs, ks = a[p + "q_scale"], a[p + "k_scale"]
        w1, w2, b1 = a[p + "W1"], a[p + "W2"], a[p + "b1"]
        w2p = np.zeros((DEPTH, P, 3, D), f32)
        cols = np.zeros((DEPTH, P, 8), f32)
        cols[:, :, 0], cols[:, :, 1] = a[p + "ln_g"], a[p + "ln_b"]
        for k, (at, n) in enumerate(FF_CHUNKS):
            w2p[:, 0:n, k] = w2[:, at:at + n]
            cols[:, 0:n, 2 + k] = b1[:, at:at + n]
            cols[:, 0:n, 5 + k] = b1[:, FF + at:FF + at + n]
        w2p[:, FF_CHUNKS[2][1], 2] = a[p + "b2"]
        return (a[p + "Wqkv"], a[p + "Wo"].reshape(DEPTH, 8, P, D).transpose(0, 2, 1, 3).reshape(DEPTH, P, 8 * D),
                np.concatenate([qs, swap(qs), ks, swap(ks)], 1), w1, w2p.reshape(DEPTH, P, 3 * D), cols)

    stacks = [np.concatenate(both) for both in zip(windowed("L1_ffn_"), windowed("L2_ffn_"))]
    window_io = {k: give("wt_" + k, v) for k, v in zip(("wqkv", "wo", "scales", "w1", "w2", "cols"), stacks)}
    window_io["rope"] = give("window_rope", window_rope)
    evens_first = np.concatenate([np.arange(0, D, 2), np.arange(1, D, 2)])
    wqkv1 = a["L1_attn_Wqkv"]
    tiles = np.zeros((P, 10, D), f32)
    m3 = {k: a["L3_attn_" + k] for k in ("W_DQ", "W_UQ", "W_DKV", "W_UKV", "W_QR", "W_KR", "W_O")}
    for n, t in enumerate((m3["W_DQ"], m3["W_UQ"].T, m3["W_DKV"], m3["W_UKV"][0:HD].T, m3["W_KR"], m3["W_QR"],
                           m3["W_UKV"][HD:2 * HD].T)):
        tiles[0:t.shape[0], n] = np.tile(t, (1, NH))
    tiles[:, 7] = np.tile(m3["W_O"].T, (NH, NH))
    eye = np.arange(D) // HD
    io = {
        "x": give("x", a["L0_attn_x"]),
        "headmask": give("headmask", (eye[:, None] == eye[None, :]).astype(np.float32)),
        "headcol": give("headcol", (eye[:, None] == np.arange(NH)[None, :]).astype(np.float32)),
        "a0": plain("a0", *[a["L0_attn_" + k] for k in ("Wq", "Wk", "Wv", "Wo", "bq", "bk", "bv", "bo")]),
    }
    io["e0"] = {"up": give("e0_up", a["L0_ffn_w1"].T), "side": give("e0_side", a["L0_ffn_v1"].T),
                "down": give("e0_down", chunks(a["L0_ffn_w2"], EXPERTS * 2, D)),
                "router": give("e0_router", a["L0_ffn_router_w"].T)}
    io["l1"] = {"wq": give("l1_wq", wqkv1[0:D].T), "wkv": give("l1_wkv", wqkv1[D:3 * D].T),
                "wp": give("l1_wp", a["L1_attn_Wproj"].T), "bp": give("l1_bp", a["L1_attn_bproj"])}
    io["wt"] = window_io
    io["r2"] = {"wqkv": give("r2_wqkv", np.concatenate([a["L2_attn_wq"].T[:, evens_first],
                                                        a["L2_attn_wk"].T[:, evens_first], a["L2_attn_wv"].T], 1)),
                "rope": give("r2_rope", wide_rope)}
    io["m3"] = {"tiles": give("m3_tiles", tiles),
                "norms": give("m3_norms", np.concatenate([a["L3_attn_q_norm_w"], a["L3_attn_k_norm_w"]]))}
    f = "L3_ffn_"
    io["a3"] = plain("a3", *[a[f + k] for k in ("wq", "wk", "wv", "wo", "bq", "bk", "bv", "bo", "ln1_g", "ln1_b")])
    io["e3"] = {"up": give("e3_up", a[f + "w1"].transpose(1, 0, 2).reshape(D, EXPERTS * 512)),
                "down": give("e3_down", chunks(a[f + "w2"].reshape(EXPERTS * 512, D), EXPERTS * 4, D)),
                "router": give("e3_router", a[f + "gate_w"]), "gate_b": give("e3_gate_b", a[f + "gate_b"]),
                "b1": give("e3_b1", a[f + "b1"].reshape(EXPERTS * 4, P).T), "b2": give("e3_b2", a[f + "b2"]),
                "ln": give("e3_ln", np.stack([a[f + "ln2_g"], a[f + "ln2_b"]], 1))}
    io["out"] = nc.dram_tensor("out", (B, S, D), F32, kind="ExternalOutput").ap()
    program(nc, io)
    result = run_bass_kernel_spmd(nc, [arrays], core_ids=[0])
    return result.results[0]["out"].reshape(B, S, D)
```
